# Optimizing a Trainium2 kernel written in Bass

```python
import numpy as np
import jax
import jax.numpy as jnp

def _softmax(x, axis=-1):
    return jax.nn.softmax(x, axis=axis)

def _gelu(x):
    return jax.nn.gelu(x, approximate=True)

def _silu(x):
    return jax.nn.silu(x)

def _sigmoid(x):
    return jax.nn.sigmoid(x)

def _layernorm(x, axis=-1, eps=1e-05):
    m = jnp.mean(x, axis=axis, keepdims=True)
    v = jnp.var(x, axis=axis, keepdims=True)
    return (x - m) / jnp.sqrt(v + eps)

def _scatter_add(tgt, idx, src, axis=0):
    return tgt.at[idx].add(src)

def _segment_sum(src, seg, n):
    return jax.ops.segment_sum(src, seg, n)
kernel_name = 'mk_adj_resnorm_d2_adj_r2_885b19'

def setup_inputs(seed: int=0):
    np.random.seed(seed)
    _w = jnp.asarray

    def _rec_inputs():
        import jax
        import jax.numpy as jnp
        _gk = jax.random.key(seed)
        x = 7.22e-05 + 1 * jax.random.normal(jax.random.fold_in(_gk, 1), (16, 512, 128), jnp.float32)
        _a = jax.random.bernoulli(jax.random.fold_in(_gk, 2), 0.015625, (16, 512, 512))
        _a = jnp.logical_or(_a, jnp.swapaxes(_a, -1, -2))
        _a = jnp.logical_or(_a, jnp.eye(512, dtype=bool))
        _af = _a.astype(jnp.float32)
        adj = _af
        return (x, adj)
    x, adj = _rec_inputs()

    def _L0_gnn_setup():
        import jax, jax.numpy as jnp
        import numpy as np
        from jax import lax
        DIM = 128
        EPS = 1e-05

        def _bn(h, g, b, m, v):
            scale = g / jnp.sqrt(v + EPS)
            return h * scale[None, :, None] + (b - m * scale)[None, :, None]

        def _conv1d(h, w, pad):
            return lax.conv_general_dilated(h, w, window_strides=(1,), padding=[(pad, pad)], dimension_numbers=('NCH', 'OIH', 'NCH'))
        key = jax.random.key(seed)
        ks = jax.random.split(key, 16)
        bs, n, d = (16, 1024, DIM)
        s = 0.05
        return {'x': jax.random.normal(ks[0], (bs, n, d), jnp.float32), 'mask': jnp.ones((bs, n, n), jnp.float32), 'w_se': jax.random.normal(ks[1], (3, d), jnp.float32) * s, 'b_se': jnp.zeros((3,), jnp.float32), 'conv1_w': jax.random.normal(ks[2], (d, d, 1), jnp.float32) * s, 'bn1_g': jnp.ones((d,), jnp.float32), 'bn1_b': jnp.zeros((d,), jnp.float32), 'bn1_m': jnp.zeros((d,), jnp.float32), 'bn1_v': jnp.ones((d,), jnp.float32), 'conv2_w': jax.random.normal(ks[3], (d, d, 17), jnp.float32) * s, 'bn2_g': jnp.ones((d,), jnp.float32), 'bn2_b': jnp.zeros((d,), jnp.float32), 'bn2_m': jnp.zeros((d,), jnp.float32), 'bn2_v': jnp.ones((d,), jnp.float32), 'w_msg': jax.random.normal(ks[4], (d, d), jnp.float32) * s, 'b_msg': jnp.zeros((d,), jnp.float32), 'w_ih': jax.random.normal(ks[5], (3 * d, 2 * d), jnp.float32) * s, 'b_ih': jnp.zeros((3 * d,), jnp.float32), 'w_hh': jax.random.normal(ks[6], (3 * d, d), jnp.float32) * s, 'b_hh': jnp.zeros((3 * d,), jnp.float32)}
    _L0_gnn_all = _L0_gnn_setup()
    _L0_gnn_in = {k: v for k, v in _L0_gnn_all.items() if k in ('w_se', 'b_se', 'conv1_w', 'bn1_g', 'bn1_b', 'bn1_m', 'bn1_v', 'conv2_w', 'bn2_g', 'bn2_b', 'bn2_m', 'bn2_v', 'w_msg', 'b_msg', 'w_ih', 'b_ih', 'w_hh', 'b_hh')}
    del _L0_gnn_all

    def _L1_gnn_setup():
        import jax, jax.numpy as jnp
        import numpy as np
        GROUPS = [list(range(25)), [0, 1, 2, 3, 4, 5, 6, 7, 8], [0, 9, 10, 11, 12, 13, 14], [6, 7, 8, 12, 13, 14], [3, 4, 5, 9, 10, 11]]
        B, N, D_IN, D_HID = (4096, 25, 128, 256)

        def _graph_conv(x, adj, W, b):
            n = adj.shape[-1]
            A = adj + jnp.eye(n, dtype=adj.dtype)
            deg = jnp.sum(A, axis=-1)
            deg_safe = jnp.where(deg == 0, 1.0, deg)
            dinv = jnp.where(deg == 0, 0.0, deg_safe ** (-0.5))
            norm_adj = dinv[:, :, None] * A * dinv[:, None, :]
            support = jnp.einsum('bnd,de->bne', x, W)
            out = jnp.einsum('bnm,bme->bne', norm_adj, support) + b
            return jax.nn.relu(out)
        key = jax.random.key(seed)
        ks = jax.random.split(key, 7)
        s1 = float(np.sqrt(6.0 / (D_IN + D_HID)))
        s2 = float(np.sqrt(6.0 / (D_HID + D_IN)))
        return {'x': jax.random.normal(ks[0], (B, N, D_IN), dtype=jnp.float32), 'adj': jax.random.uniform(ks[1], (B, N, N), dtype=jnp.float32), 'W1': jax.random.uniform(ks[2], (5, D_IN, D_HID), jnp.float32, -s1, s1), 'b1': jnp.zeros((5, D_HID), dtype=jnp.float32), 'W2': jax.random.uniform(ks[3], (5, D_HID, D_IN), jnp.float32, -s2, s2), 'b2': jnp.zeros((5, D_IN), dtype=jnp.float32), 'fusion_w': jnp.ones((5,), dtype=jnp.float32)}
    _L1_gnn_all = _L1_gnn_setup()
    _L1_gnn_in = {k: v for k, v in _L1_gnn_all.items() if k in ('W1', 'b1', 'W2', 'b2', 'fusion_w')}
    del _L1_gnn_all
    return {'x': x, 'adj': adj, 'L0_gnn_w_se': _L0_gnn_in['w_se'], 'L0_gnn_b_se': _L0_gnn_in['b_se'], 'L0_gnn_conv1_w': _L0_gnn_in['conv1_w'], 'L0_gnn_bn1_g': _L0_gnn_in['bn1_g'], 'L0_gnn_bn1_b': _L0_gnn_in['bn1_b'], 'L0_gnn_bn1_m': _L0_gnn_in['bn1_m'], 'L0_gnn_bn1_v': _L0_gnn_in['bn1_v'], 'L0_gnn_conv2_w': _L0_gnn_in['conv2_w'], 'L0_gnn_bn2_g': _L0_gnn_in['bn2_g'], 'L0_gnn_bn2_b': _L0_gnn_in['bn2_b'], 'L0_gnn_bn2_m': _L0_gnn_in['bn2_m'], 'L0_gnn_bn2_v': _L0_gnn_in['bn2_v'], 'L0_gnn_w_msg': _L0_gnn_in['w_msg'], 'L0_gnn_b_msg': _L0_gnn_in['b_msg'], 'L0_gnn_w_ih': _L0_gnn_in['w_ih'], 'L0_gnn_b_ih': _L0_gnn_in['b_ih'], 'L0_gnn_w_hh': _L0_gnn_in['w_hh'], 'L0_gnn_b_hh': _L0_gnn_in['b_hh'], 'L1_gnn_W1': _L1_gnn_in['W1'], 'L1_gnn_b1': _L1_gnn_in['b1'], 'L1_gnn_W2': _L1_gnn_in['W2'], 'L1_gnn_b2': _L1_gnn_in['b2'], 'L1_gnn_fusion_w': _L1_gnn_in['fusion_w']}

def reference(x, adj, L0_gnn_w_se, L0_gnn_b_se, L0_gnn_conv1_w, L0_gnn_bn1_g, L0_gnn_bn1_b, L0_gnn_bn1_m, L0_gnn_bn1_v, L0_gnn_conv2_w, L0_gnn_bn2_g, L0_gnn_bn2_b, L0_gnn_bn2_m, L0_gnn_bn2_v, L0_gnn_w_msg, L0_gnn_b_msg, L0_gnn_w_ih, L0_gnn_b_ih, L0_gnn_w_hh, L0_gnn_b_hh, L1_gnn_W1, L1_gnn_b1, L1_gnn_W2, L1_gnn_b2, L1_gnn_fusion_w):
    import jax
    import jax.numpy as jnp

    def _L0_gnn_ref(x, mask, w_se, b_se, conv1_w, bn1_g, bn1_b, bn1_m, bn1_v, conv2_w, bn2_g, bn2_b, bn2_m, bn2_v, w_msg, b_msg, w_ih, b_ih, w_hh, b_hh):
        import jax, jax.numpy as jnp
        import numpy as np
        from jax import lax
        DIM = 128
        EPS = 1e-05

        def _bn(h, g, b, m, v):
            scale = g / jnp.sqrt(v + EPS)
            return h * scale[None, :, None] + (b - m * scale)[None, :, None]

        def _conv1d(h, w, pad):
            return lax.conv_general_dilated(h, w, window_strides=(1,), padding=[(pad, pad)], dimension_numbers=('NCH', 'OIH', 'NCH'))
        d = x.shape[-1]
        xc = jnp.transpose(x, (0, 2, 1))
        h = _bn(_conv1d(xc, conv1_w, 0), bn1_g, bn1_b, bn1_m, bn1_v)
        h = jax.nn.relu(h)
        h = _bn(_conv1d(h, conv2_w, 8), bn2_g, bn2_b, bn2_m, bn2_v)
        x_conv = jnp.transpose(jax.nn.relu(h + xc), (0, 2, 1))
        s = x @ w_se.T + b_se
        sq = jnp.sum(s * s, axis=-1)
        dist = sq[:, :, None] + sq[:, None, :] - 2.0 * jnp.einsum('bnd,bmd->bnm', s, s)
        A = jnp.exp(-dist) * mask
        msg = jax.nn.relu(x @ w_msg.T + b_msg)
        x_nmp = jnp.einsum('bnm,bmd->bnd', A, msg)
        x_in = jnp.concatenate([x_conv, x_nmp], axis=-1)
        gi = x_in @ w_ih.T + b_ih
        gh = x @ w_hh.T + b_hh
        gi_r, gi_z, gi_n = (gi[..., :d], gi[..., d:2 * d], gi[..., 2 * d:])
        gh_r, gh_z, gh_n = (gh[..., :d], gh[..., d:2 * d], gh[..., 2 * d:])
        r = jax.nn.sigmoid(gi_r + gh_r)
        z = jax.nn.sigmoid(gi_z + gh_z)
        nn_ = jnp.tanh(gi_n + r * gh_n)
        return (1.0 - z) * nn_ + z * x

    def _L1_gnn_ref(x, adj, W1, b1, W2, b2, fusion_w):
        import jax, jax.numpy as jnp
        import numpy as np
        GROUPS = [list(range(25)), [0, 1, 2, 3, 4, 5, 6, 7, 8], [0, 9, 10, 11, 12, 13, 14], [6, 7, 8, 12, 13, 14], [3, 4, 5, 9, 10, 11]]
        B, N, D_IN, D_HID = (4096, 25, 128, 256)

        def _graph_conv(x, adj, W, b):
            n = adj.shape[-1]
            A = adj + jnp.eye(n, dtype=adj.dtype)
            deg = jnp.sum(A, axis=-1)
            deg_safe = jnp.where(deg == 0, 1.0, deg)
            dinv = jnp.where(deg == 0, 0.0, deg_safe ** (-0.5))
            norm_adj = dinv[:, :, None] * A * dinv[:, None, :]
            support = jnp.einsum('bnd,de->bne', x, W)
            out = jnp.einsum('bnm,bme->bne', norm_adj, support) + b
            return jax.nn.relu(out)
        norm_w = jax.nn.softmax(fusion_w)
        fused = jnp.zeros_like(x)
        for g, idx_list in enumerate(GROUPS):
            idx = jnp.asarray(idx_list)
            x_g = x[:, idx, :]
            adj_g = adj[:, idx][:, :, idx]
            h = _graph_conv(x_g, adj_g, W1[g], b1[g])
            out_g = _graph_conv(h, adj_g, W2[g], b2[g])
            fused = fused.at[:, idx, :].add(norm_w[g] * out_g)
        return fused
    x = _layernorm(x + _L0_gnn_ref(x, adj, L0_gnn_w_se, L0_gnn_b_se, L0_gnn_conv1_w, L0_gnn_bn1_g, L0_gnn_bn1_b, L0_gnn_bn1_m, L0_gnn_bn1_v, L0_gnn_conv2_w, L0_gnn_bn2_g, L0_gnn_bn2_b, L0_gnn_bn2_m, L0_gnn_bn2_v, L0_gnn_w_msg, L0_gnn_b_msg, L0_gnn_w_ih, L0_gnn_b_ih, L0_gnn_w_hh, L0_gnn_b_hh), axis=-1)
    x = _layernorm(x + _L1_gnn_ref(x, adj, L1_gnn_W1, L1_gnn_b1, L1_gnn_W2, L1_gnn_b2, L1_gnn_fusion_w), axis=-1)
    return x

_drawn_inputs = setup_inputs


def setup_inputs(seed=0):
    import zlib

    import numpy as np

    out = dict(_drawn_inputs(seed))
    spreads = {'L0_gnn_b_se': (0.0, 2.0),
     'L0_gnn_bn1_g': (1.0, 0.6),
     'L0_gnn_bn1_b': (0.0, 0.492),
     'L0_gnn_bn1_m': (0.0, 0.442),
     'L0_gnn_bn1_v': (1.0, 0.6),
     'L0_gnn_bn2_g': (1.0, 0.6),
     'L0_gnn_bn2_b': (0.0, 0.761),
     'L0_gnn_bn2_m': (0.0, 0.692),
     'L0_gnn_bn2_v': (1.0, 0.6),
     'L0_gnn_b_msg': (0.0, 0.1),
     'L0_gnn_b_ih': (0.0, 0.277),
     'L0_gnn_b_hh': (0.0, 0.388),
     'L1_gnn_b1': (0.0, 2.0),
     'L1_gnn_b2': (0.0, 0.8),
     'L1_gnn_fusion_w': (1.0, 0.6)}
    factors = {'L1_gnn_W1': 2.916}
    for name, (base, spread) in spreads.items():
        noise = np.random.default_rng([zlib.crc32(name.encode()), seed]).standard_normal(out[name].shape)
        drawn = base * np.exp(spread * noise) if base else spread * noise
        out[name] = jnp.asarray(drawn.astype(out[name].dtype))
    for name, factor in factors.items():
        out[name] = (out[name] * factor).astype(out[name].dtype)
    return out
```

```python
import numpy as np
import concourse.bass as bass
from concourse import mybir
from contextlib import ExitStack

B, N, D = 16, 512, 128
TAPS = 17
PAD = (TAPS - 1) // 2
EPS = 1e-5
GROUPS = [list(range(25)), [0, 1, 2, 3, 4, 5, 6, 7, 8], [0, 9, 10, 11, 12, 13, 14],
          [6, 7, 8, 12, 13, 14], [3, 4, 5, 9, 10, 11]]
HID = 256
GN = 25
SLOT = 32
PAIRS = B // 2
GSIZE = [2 * len(g) for g in GROUPS]
GOFF = [sum(GSIZE[:g]) for g in range(len(GROUPS))]
CC = sum(GSIZE)
NG = len(GROUPS)
CH = N // D
HALF = N // 2
NE = (TAPS + 1) // 2
NO = TAPS // 2
PH = HALF + PAD

KD = 24


def dist_rows():
    left, right = [], []
    for hl in ((0, 0), (0, 1), (1, 0), (1, 1)):
        for k in range(3):
            left.append((k, 0.0, 1.0, hl[0]))
            right.append((k, 0.0, 2.0, hl[1]))
    for low in (0, 1):
        for k in range(3):
            left.append((k, 1.0, 0.0, low))
            right.append((None, 0.0, -1.0, 0))
    for low in (0, 1):
        for k in range(3):
            left.append((None, 0.0, 1.0, 0))
            right.append((k, -1.0, 0.0, low))
    return left, right


(V_G1, V_B1, V_M1, V_V1, V_G2, V_B2, V_M2, V_V2, V_IR, V_IZ, V_IN, V_HR, V_HZ, V_HN) = range(14)
NV = 14

C_SEL = 0
C_SELT = C_SEL + CC
C_SAME = C_SELT + 64
C_G5 = C_SAME + CC
C_G5T = C_G5 + NG
C_ID = C_G5T + CC
C_ROW = C_ID + D
C_ONE = C_ROW + 3
C_MH = C_ONE + 1
NCONST = C_MH + 8


def constants():
    c = np.zeros((128, NCONST), np.float32)
    for g, nodes in enumerate(GROUPS):
        for b in range(2):
            for i, n in enumerate(nodes):
                row = GOFF[g] + b * len(nodes) + i
                c[SLOT * b + n, C_SEL + row] = 1
                c[row, C_SELT + SLOT * b + n] = 1
                c[row, C_SAME + GOFF[g]:C_SAME + GOFF[g] + GSIZE[g]] = 1
                c[row, C_G5 + g] = 1
                c[g, C_G5T + row] = 1
    c[:, C_ID:C_ID + D] = np.eye(D)
    for side, rows in enumerate(dist_rows()):
        for r, (_, alpha, beta, low) in enumerate(rows):
            c[32 * side + r, C_ROW:C_ROW + 3] = alpha, beta, -low
    c[:, C_ONE] = 1
    c[:, C_MH:C_MH + 8] = -0.5
    return c


def gnn_kernel(nc, xT, adjT, consts, vecs, w_rows, b_rows, w_c1, w_c2, w_ih, w_hh, w_msg, b_msg,
               g_w1, g_b1, g_w2, g_b2, g_fw, out):
    fp32 = mybir.dt.float32
    fp32r = mybir.dt.float32r
    ALU = mybir.AluOpType
    ACT = mybir.ActivationFunctionType
    AX = mybir.AxisListType

    ctx = ExitStack()
    with ctx:
        def sb(name, shape, dt=fp32):
            return ctx.enter_context(nc.sbuf_tensor(name, shape, dt))

        def sem(name):
            return ctx.enter_context(nc.semaphore(name))

        def full(ap):
            return ap.bitcast(fp32)

        cst = sb("cst", [128, NCONST])
        vec = sb("vec", [128, NV])
        brow = sb("brow", [64, 1])
        wrow = sb("wrow", [128, 128]); wrow_h = sb("wrow_h", [128, 128], fp32r); wrow_l = sb("wrow_l", [128, 128], fp32r)
        wc1 = sb("wc1", [128, D]); wc1_h = sb("wc1_h", [128, D], fp32r); wc1_l = sb("wc1_l", [128, D], fp32r)
        wc2 = sb("wc2", [128, TAPS, D])
        yy = sb("yy", [128, 3 * N])
        ya, yb, y2 = yy[:, 0:N], yy[:, N:2 * N], yy[:, 2 * N:3 * N]
        wsum = yy[:, 0:NE * D].rearrange("p (t d) -> p t d", d=D)
        wo_h = sb("wo_h", [128, NO, D], fp32r); wo_l = sb("wo_l", [128, NO, D], fp32r)
        we_h = sb("we_h", [128, NE, D], fp32r); we_l = sb("we_l", [128, NE, D], fp32r)
        ws_h = sb("ws_h", [128, NE, D], fp32r); ws_l = sb("ws_l", [128, NE, D], fp32r)
        wg = sb("wg", [128, 3, 3 * D])
        wg_h = sb("wg_h", [128, 3, 3 * D], fp32r); wg_l = sb("wg_l", [128, 3, 3 * D], fp32r)
        wmsg = sb("wmsg", [128, D])
        bmsg = sb("bmsg", [128, D])
        prm = sb("prm", [128, 16])
        P_VE, P_RS, P_S1, P_S2, P_T1, P_T2, P_A1, P_A2, P_R, P_Z, P_RH, P_ZH = 0, 2, 4, 5, 6, 7, 8, 9, 10, 11, 12, 13

        xin = [sb(f"xin{p}", [128, N]) for p in range(2)]
        xkeep = [sb(f"xkeep{p}", [128, N]) for p in range(2)]
        x_h = [sb(f"x_h{p}", [128, N], fp32r) for p in range(2)]
        x_l = [sb(f"x_l{p}", [128, N], fp32r) for p in range(2)]
        adj = [sb(f"adj{p}", [128, CH, N]) for p in range(2)]
        u = sb("u", [64, N]); ab = sb("ab", [64, N]); val = sb("val", [64, N]); val_h = sb("val_h", [64, N], fp32r)
        left = sb("left", [KD, N], fp32r); right = sb("right", [KD, N], fp32r)
        h1 = sb("h1", [128, N + 2 * PAD])
        ph = sb("ph", [128, 3, PH])
        ph_h = [sb(f"ph_h{p}", [128, 3, PH], fp32r) for p in range(2)]
        ph_l = [sb(f"ph_l{p}", [128, 3, PH], fp32r) for p in range(2)]
        am = sb("am", [128, CH, N])
        am_h = sb("am_h", [128, CH, N], fp32r); am_l = sb("am_l", [128, CH, N], fp32r)
        mt = sb("mt", [128, N])
        m_h = [sb(f"m_h{p}", [128, N], fp32r) for p in range(2)]
        m_l = [sb(f"m_l{p}", [128, N], fp32r) for p in range(2)]
        n_h = sb("n_h", [128, N], fp32r); n_l = sb("n_l", [128, N], fp32r)
        ca = sb("ca", [128, HALF]); cu = sb("cu", [128, N]); cv = sb("cv", [128, N])
        c_h = sb("c_h", [128, N], fp32r); c_l = sb("c_l", [128, N], fp32r)
        rt = sb("rt", [128, N]); r1 = rt; zt = sb("zt", [128, N])
        gg = sb("gg", [128, N]); tt = sb("tt", [128, N]); nn = sb("nn", [128, N])
        yn = sb("yn", [128, CH, D]); st = sb("st", [128, CH, 6]); mv = sb("mv", [128, CH, 2]); base = sb("base", [128, CH + 1]); rs = sb("rs", [128, CH + 1])
        yo = [sb(f"yo{p}", [128, CH, D]) for p in range(2)]

        x1 = sb("x1", [64, PAIRS, D])
        bd = sb("bd", [64, PAIRS, 64])
        ac = sb("ac", [CC, PAIRS, CC])
        dg = sb("dg", [CC, 4, PAIRS])
        dinv = sb("dinv", [CC, PAIRS])
        fw = sb("fw", [CC, NG]); fs = sb("fs", [CC, 4]); fe = sb("fe", [CC, NG]); wcol = sb("wcol", [CC, 1])
        b2g = sb("b2g", [NG, D]); b2r = sb("b2r", [CC, D])
        gw1 = sb("gw1", [128, NG, HID]); gw2 = sb("gw2", [128, NG, 2, D]); gb1 = sb("gb1", [128, NG, 2])

        ring = [ctx.enter_context(nc.psum_tensor(f"ring{i}", [128, N], fp32)) for i in range(2)]
        p_bc = ctx.enter_context(nc.psum_tensor("p_bc", [128, N], fp32))
        p_a = ctx.enter_context(nc.psum_tensor("p_a", [128, N], fp32))
        p_r, p_z, p_gi, p_gh = [ctx.enter_context(nc.psum_tensor(n, [128, N], fp32)) for n in ("p_r", "p_z", "p_gi", "p_gh")]

        s_cst = sem("s_cst"); s_small = sem("s_small"); s_w1d = sem("s_w1d"); s_w2d = sem("s_w2d"); s_wgd = sem("s_wgd")
        s_gd = sem("s_gd"); s_bdd = sem("s_bdd"); s_zero = sem("s_zero")
        s_prm = sem("s_prm"); s_pow = sem("s_pow"); s_wsum = sem("s_wsum")
        s_w1s = sem("s_w1s"); s_wohi = sem("s_wohi"); s_wolo = sem("s_wolo"); s_wgs = sem("s_wgs")
        s_bdi = sem("s_bdi"); s_sel1m = sem("s_sel1m"); s_sel1 = sem("s_sel1"); s_acm = sem("s_acm"); s_ac = sem("s_ac")
        s_deg = sem("s_deg"); s_dg = sem("s_dg"); s_dpow = sem("s_dpow"); s_dinv = sem("s_dinv")
        s_fw = sem("s_fw"); s_fe = sem("s_fe"); s_wcol = sem("s_wcol"); s_b2m = sem("s_b2m"); s_b2r = sem("s_b2r")
        s_x = [sem(f"s_x{p}") for p in range(2)]
        s_adj = [sem(f"s_adj{p}") for p in range(2)]
        s_xh = sem("s_xh"); s_xl = sem("s_xl"); s_xk = sem("s_xk")
        s_rows = sem("s_rows"); s_u = sem("s_u"); s_ab = sem("s_ab"); s_val = sem("s_val"); s_valh = sem("s_valh")
        s_left = sem("s_left"); s_right = sem("s_right")
        s_c1 = sem("s_c1"); s_h1 = sem("s_h1"); s_pho = sem("s_pho"); s_phd = sem("s_phd"); s_phh = sem("s_phh"); s_phl = sem("s_phl")
        s_msg = sem("s_msg"); s_mt = sem("s_mt"); s_mh = sem("s_mh"); s_ml = sem("s_ml")
        s_d = [sem(f"s_d{c}") for c in range(CH)]; s_e = [sem(f"s_e{c}") for c in range(CH)]
        s_am = [sem(f"s_am{c}") for c in range(CH)]; s_amh = sem("s_amh"); s_aml = sem("s_aml")
        s_bc = sem("s_bc"); s_a = sem("s_a"); s_ca = sem("s_ca"); s_cu = sem("s_cu"); s_cv = sem("s_cv"); s_ch = sem("s_ch"); s_cl = sem("s_cl")
        s_nmp = sem("s_nmp"); s_nh = sem("s_nh"); s_nl = sem("s_nl")
        s_gx = sem("s_gx"); s_gn = sem("s_gn"); s_gr = sem("s_gr"); s_gi = sem("s_gi"); s_gz = sem("s_gz")
        s_rt = sem("s_rt"); s_zt = sem("s_zt"); s_r1 = sem("s_r1"); s_gg = sem("s_gg"); s_tt = sem("s_tt"); s_nn = sem("s_nn")
        s_ya = sem("s_ya"); s_yb = sem("s_yb"); s_y2 = sem("s_y2")
        s_t = sem("s_t"); s_yn = sem("s_yn"); s_st = sem("s_st"); s_mv = sem("s_mv"); s_base = sem("s_base"); s_rs = sem("s_rs"); s_yo = sem("s_yo")
        s_out = [sem(f"s_out{p}") for p in range(2)]
        s_q = [sem(f"s_q{i}") for i in range(18)]
        s_fin = sem("s_fin")

        HP = PAIRS // 2

        def part(t, a, rows, width):
            flat = t[:] if len(t.shape) == 2 else t[:].rearrange("p a b -> p (a b)")
            return flat[0:rows, a:a + PAIRS * width].rearrange("p (j w) -> p j w", w=width)

        sel1 = part(wc2, 0, 64, CC)
        xs, ag = part(adj[0], 0, CC, D), part(adj[0], PAIRS * D, CC, D)
        agT, hT0 = part(adj[1], 0, 128, CC), part(adj[1], PAIRS * CC, 128, CC)
        hT1, sT = part(wc2, 0, 128, CC), part(wc2, PAIRS * CC, 128, CC)
        ss, o1 = part(am, 0, CC, D), part(am, PAIRS * D, CC, D)
        o2, zz, yfin = xs, part(adj[0], PAIRS * D, 64, D), part(adj[1], 0, 64, D)
        hT = (hT0, hT1)
        gst = sb("gst", [64, PAIRS, 6]); gmv = sb("gmv", [64, PAIRS, 2]); gbase = sb("gbase", [64, PAIRS]); grs = sb("grs", [64, PAIRS])
        (Q_SEL, Q_XS, Q_AGG, Q_AG, Q_TR, Q_AGT, Q_W1, Q_H0, Q_H1, Q_W2, Q_S, Q_TS, Q_SS, Q_AGG2, Q_O1, Q_O2, Q_SC, Q_FIN) = range(18)
        W1_BANKS = (p_bc, p_a, p_r, p_z)
        W2_BANKS = (p_gi, p_gh, ring[0], ring[1])

        def pairs(h):
            return slice(HP * h, HP * h + HP)

        def group(g):
            return slice(GOFF[g], GOFF[g] + GSIZE[g])

        def banked(bank_, rows, width):
            return bank_[0:rows, 0:HP * width].rearrange("p (j w) -> p j w", w=width)

        def cols(bank_, g):
            return bank_[:, 0:PAIRS * GSIZE[g]].rearrange("p (j w) -> p j w", w=GSIZE[g])

        def dinv_of(h):
            return dinv[:, pairs(h)].unsqueeze(2).broadcast_to([CC, HP, D])

        def groups_pe(pe, mm):
            pe.wait_ge(s_yo, B)
            pe.wait_ge(s_nl, B)
            for h in range(2):
                for j in range(HP):
                    last = mm((p_bc, p_a)[h][0:CC, D * j:D * j + D], cst[0:64, C_SEL:C_SEL + CC], x1[:, HP * h + j, :])
                last.then_inc(s_q[Q_SEL], 1)
            for h in range(2):
                pe.wait_ge(s_q[Q_XS], h + 1)
                for j in range(HP):
                    last = mm((p_r, p_z)[h][0:CC, D * j:D * j + D], ac[:, HP * h + j, :], xs[:, HP * h + j, :])
                last.then_inc(s_q[Q_AGG], 1)
            for h in range(2):
                pe.wait_ge(s_q[Q_AG], h + 1)
                for j in range(HP):
                    last = nc.tensor.transpose((p_gi, p_gh)[h][:, CC * j:CC * j + CC], ag[:, HP * h + j, :],
                                               cst[0:CC, C_ID:C_ID + CC])
                last.then_inc(s_q[Q_TR], 1)
            pe.wait_ge(s_q[Q_AGT], 2)
            for g in range(NG):
                for k in range(2):
                    if g >= 2:
                        pe.wait_ge(s_q[(Q_H0, Q_H1)[k]], g - 1)
                    mm(cols(W1_BANKS[(2 * g + k) % 4], g), gw1[:, g, D * k:D * k + D], agT[:, :, group(g)]).then_inc(s_q[Q_W1], 1)
            for g in range(NG):
                pe.wait_ge(s_q[Q_H0], g + 1); pe.wait_ge(s_q[Q_H1], g + 1)
                if g >= 4:
                    pe.wait_ge(s_q[Q_S], g - 3)
                for k in range(2):
                    last = mm(cols(W2_BANKS[g % 4], g), gw2[:, g, k, :], hT[k][:, :, group(g)], k == 0, k == 1)
                last.then_inc(s_q[Q_W2], 1)
            pe.wait_ge(s_q[Q_S], NG)
            for h in range(2):
                for j in range(HP):
                    last = nc.tensor.transpose((p_bc, p_a)[h][0:CC, D * j:D * j + D], sT[:, HP * h + j, :], cst[:, C_ID:C_ID + D])
                last.then_inc(s_q[Q_TS], 1)
            for h in range(2):
                pe.wait_ge(s_q[Q_SS], h + 1)
                for j in range(HP):
                    last = mm((p_r, p_z)[h][0:CC, D * j:D * j + D], ac[:, HP * h + j, :], ss[:, HP * h + j, :])
                last.then_inc(s_q[Q_AGG2], 1)
            for h in range(2):
                pe.wait_ge(s_q[Q_O2], h + 1)
                for j in range(HP):
                    last = mm((p_gi, p_gh)[h][0:64, D * j:D * j + D], cst[0:CC, C_SELT:C_SELT + 64], o2[:, HP * h + j, :])
                last.then_inc(s_q[Q_SC], 1)

        def groups_act(act):
            A = nc.scalar.activation
            for h in range(2):
                act.wait_ge(s_q[Q_TR], h + 1)
                A(agT[:, pairs(h), :], banked((p_gi, p_gh)[h], 128, CC), ACT.Copy).then_inc(s_q[Q_AGT], 1)
            for g in range(NG):
                act.wait_ge(s_q[Q_W1], 2 * g + 1)
                A(hT0[:, :, group(g)], cols(W1_BANKS[(2 * g) % 4], g), ACT.Relu, bias=gb1[:, g, 0:1]).then_inc(s_q[Q_H0], 1)
            for g in range(NG):
                act.wait_ge(s_q[Q_W2], g + 1)
                A(sT[:, :, group(g)], cols(W2_BANKS[g % 4], g), ACT.Copy).then_inc(s_q[Q_S], 1)
            act.wait_ge(s_wcol, 3)
            for h in range(2):
                act.wait_ge(s_q[Q_O1], 2 * h + 2)
                A(o2[:, pairs(h), :], o1[:, pairs(h), :], ACT.Relu, scale=wcol[:, 0:1]).then_inc(s_q[Q_O2], 1)

        def groups_pool(pool):
            pool.wait_ge(s_gmv, 1)
            nc.gpsimd.tensor_scalar(gbase[:], gmv[:, :, 1], 1.0, EPS, ALU.mult, ALU.add).then_inc(s_gbase, 1)
            pool.wait_ge(s_gbase, 1)
            nc.gpsimd.tensor_tensor(grs[:], gbase[:], cst[0:64, C_MH:C_MH + PAIRS], ALU.pow).then_inc(s_grs, 1)

        def groups_dve(dve):
            TT, TS = nc.vector.tensor_tensor, nc.vector.tensor_scalar
            dve.wait_ge(s_fe, 1)
            nc.vector.tensor_tensor_reduce(out=fw[:], in0=fe[:], in1=cst[0:CC, C_G5:C_G5 + NG], scale=1.0, scalar=0.0,
                                           op0=ALU.mult, op1=ALU.add, accum_out=fs[:, 3:4]).then_inc(s_wcol, 1)
            nc.vector.reciprocal(fs[:, 0:1], fs[:, 2:3]).then_inc(s_wcol, 1)
            dve.wait_ge(s_wcol, 2)
            TT(wcol[:], fs[:, 3:4], fs[:, 0:1], ALU.mult).then_inc(s_wcol, 1)
            dve.wait_ge(s_dpow, 1)
            TS(dg[:, 0, :], dg[:, 1, :], -1.0, 1.0, ALU.mult, ALU.add).then_inc(s_dinv, 1)
            dve.wait_ge(s_dinv, 1)
            TT(dinv[:], dg[:, 3, :], dg[:, 0, :], ALU.mult).then_inc(s_dinv, 1)
            dve.wait_ge(s_dinv, 2)
            for h in range(2):
                dve.wait_ge(s_q[Q_SEL], h + 1)
                TT(xs[:, pairs(h), :], banked((p_bc, p_a)[h], CC, D), dinv_of(h), ALU.mult).then_inc(s_q[Q_XS], 1)
            for h in range(2):
                dve.wait_ge(s_q[Q_AGG], h + 1)
                TT(ag[:, pairs(h), :], banked((p_r, p_z)[h], CC, D), dinv_of(h), ALU.mult).then_inc(s_q[Q_AG], 1)
            for g in range(NG):
                dve.wait_ge(s_q[Q_W1], 2 * g + 2)
                TS(hT1[:, :, group(g)], cols(W1_BANKS[(2 * g + 1) % 4], g), gb1[:, g, 1:2], 0.0, ALU.add, ALU.max).then_inc(s_q[Q_H1], 1)
            for h in range(2):
                dve.wait_ge(s_q[Q_TS], h + 1)
                TT(ss[:, pairs(h), :], banked((p_bc, p_a)[h], CC, D), dinv_of(h), ALU.mult).then_inc(s_q[Q_SS], 1)
            for h in range(2):
                dve.wait_ge(s_q[Q_AGG2], h + 1)
                TT(o1[:, pairs(h), :], banked((p_r, p_z)[h], CC, D), dinv_of(h), ALU.mult).then_inc(s_q[Q_O1], 1)
                dve.wait_ge(s_q[Q_O1], 2 * h + 1)
                TT(o1[:, pairs(h), :], o1[:, pairs(h), :], b2r[:].unsqueeze(1).broadcast_to([CC, HP, D]), ALU.add).then_inc(s_q[Q_O1], 1)
            for h in range(2):
                dve.wait_ge(s_q[Q_SC], h + 1)
                TT(zz[:, pairs(h), :], banked((p_gi, p_gh)[h], 64, D), x1[:, pairs(h), :], ALU.add).then_inc(s_gz2, 1)
                dve.wait_ge(s_gz2, h + 1)
                for j in range(HP * h, HP * h + HP):
                    last = nc.vector.bn_stats(gst[:, j, :], zz[:, j, :])
                last.then_inc(s_gst, 1)
            dve.wait_ge(s_gst, 2)
            for j in range(PAIRS):
                last = nc.vector.bn_aggr(gmv[:, j, :], gst[:, j, :])
            last.then_inc(s_gmv, 1)
            dve.wait_ge(s_gmv, 1); dve.wait_ge(s_grs, 1)
            for j in range(PAIRS):
                TS(yfin[:, j, :], zz[:, j, :], gmv[:, j, 0:1], grs[:, j:j + 1], ALU.subtract, ALU.mult).then_inc(s_q[Q_FIN], 1)

        s_gmv = sem("s_gmv"); s_gbase = sem("s_gbase"); s_grs = sem("s_grs"); s_gz2 = sem("s_gz2"); s_gst = sem("s_gst")

        block = ctx.enter_context(nc.Block())

        def after(eng, semaphore, n):
            if not isinstance(n, int) or n > 0:
                eng.wait_ge(semaphore, n)

        def batches(eng, step):
            step(0, 0, lambda k: k)
            step(1, 1, lambda k: 1 + k)
            with eng.Fori(1, PAIRS - 1) as i:
                for p in range(2):
                    known = {}

                    def count(k, p=p, known=known):
                        if k not in known:
                            known[k] = eng.snap(i * 2 + (p + k))
                        return known[k]
                    step(count(0), p, count)
            step(B - 2, 0, lambda k: B - 2 + k)
            step(B - 1, 1, lambda k: B - 1 + k)

        def dma_count(n, p, k):
            v = n(k)
            if isinstance(v, int):
                return 16 * (v // 2 + 1)
            return (v - p) * 8 + 16

        def static(b, value):
            return isinstance(b, int) and b == value

        S_ROWS, S_C1, S_MSG, S_T, S_NMP, S_D0 = 0, 1, 2, 3, 4, 5

        def bank(p, k):
            return ring[(9 * p + k) % 2]

        GATE = {"r": 0, "z": 1, "n": 2}

        @block.sync
        def _(sp):
            sp.dma_start(cst[:], consts[:, :]).then_inc(s_cst, 16)
            sp.dma_start(xin[0][:], xT[0, :, :]).then_inc(s_x[0], 16)
            sp.dma_start(wrow[:], w_rows[:, :]).then_inc(s_w1d, 16)
            sp.dma_start(wc1[:], w_c1[:, :]).then_inc(s_w1d, 16)
            sp.dma_start(wmsg[:], w_msg[:, :]).then_inc(s_w1d, 16)
            sp.dma_start(vec[:], vecs[:, :]).then_inc(s_small, 16)
            sp.dma_start(brow[:], b_rows[:, :]).then_inc(s_small, 16)
            sp.dma_start(bmsg[:], b_msg[:, :].to_broadcast([128, D])).then_inc(s_small, 16)
            sp.dma_start(wc2[:], w_c2[:, :, :]).then_inc(s_w2d, 16)
            sp.dma_start(adj[0][:], adjT[0, :, :].rearrange("(c p) n -> p c n", p=128)).then_inc(s_adj[0], 16)
            sp.dma_start(wg[:, 0:2, :], w_ih[:, :, :]).then_inc(s_wgd, 16)
            sp.dma_start(wg[:, 2, :], w_hh[:, :]).then_inc(s_wgd, 16)
            sp.dma_start(xin[1][:], xT[1, :, :]).then_inc(s_x[1], 16)
            sp.wait_ge(s_zero, 4)
            for q in range(2):
                sp.dma_start(bd[SLOT * q:SLOT * q + GN, :, SLOT * q:SLOT * q + GN],
                             adjT[q::2, 0:GN, 0:GN].rearrange("j m n -> m j n")).then_inc(s_bdd, 16)
            sp.dma_start(fw[:], g_fw[:, :].to_broadcast([CC, NG])).then_inc(s_gd, 16)
            sp.dma_start(b2g[:], g_b2[:, :]).then_inc(s_gd, 16)
            sp.dma_start(gb1[:], g_b1[:, :, :]).then_inc(s_gd, 16)
            sp.dma_start(gw1[:], g_w1.rearrange("g p h -> p g h")).then_inc(s_gd, 16)
            sp.dma_start(gw2[:], g_w2.rearrange("g (h p) o -> p g h o", p=128)).then_inc(s_gd, 16)

            sp.dma_start(adj[1][:], adjT[1, :, :].rearrange("(c p) n -> p c n", p=128)).then_inc(s_adj[1], 16)

            def step(b, p, n):
                if not (static(b, B - 2) or static(b, B - 1)):
                    after(sp, s_xl, n(1)); after(sp, s_xh, n(1)); after(sp, s_xk, n(1)); after(sp, s_msg, n(1))
                    sp.dma_start(xin[p][:], xT[b + 2, :, :]).then_inc(s_x[p], 16)
                    after(sp, s_am[CH - 1], n(1))
                    sp.dma_start(adj[p][:], adjT[b + 2, :, :].rearrange("(c p) n -> p c n", p=128)).then_inc(s_adj[p], 16)
                if not static(b, 0):
                    store(b - 1, 1 - p, n(0))

            def store(b, p, count):
                after(sp, s_yo, count)
                sp.dma_start(out[b, :, :].rearrange("(c p) d -> p c d", p=128), yo[p][:]).then_inc(s_out[p], 16)

            batches(sp, step)
            store(B - 1, 1, B)
            for p in range(2):
                sp.wait_ge(s_out[p], 16 * (B // 2))
            sp.wait_ge(s_q[17], PAIRS)
            for q in range(2):
                sp.dma_start(out[q::2, 0:GN, :].rearrange("j n d -> n j d"),
                             yfin[SLOT * q:SLOT * q + GN, :, :]).then_inc(s_fin, 16)
            sp.wait_ge(s_fin, 32)

        @block.tensor
        def _(pe):
            def mm(out_, w, x, start=True, stop=True):
                return nc.tensor.matmul(out_, w, x, start=start, stop=stop, skip_group_check=True)

            def mm3(out_, w_h, w_l, v_h, v_l, start=True, stop=True):
                mm(out_, w_h, v_h, start, False)
                mm(out_, w_h, v_l, False, False)
                return mm(out_, w_l, v_h, False, stop)

            def rows(p, n, k):
                after(pe, s_xh, n(k + 1)); after(pe, s_xl, n(k + 1))
                mm3(bank(1 - p, S_ROWS)[:], wrow_h[:], wrow_l[:], x_h[p][:], x_l[p][:]).then_inc(s_rows, 1)

            def conv1(p, n, k):
                mm3(bank(1 - p, S_C1)[:], wc1_h[:], wc1_l[:], x_h[p][:], x_l[p][:]).then_inc(s_c1, 1)

            def msg(p, n, k):
                for c in range(CH):
                    last = mm(bank(1 - p, S_MSG)[:, D * c:D * c + D], xin[p][:, D * c:D * c + D], wmsg[:])
                last.then_inc(s_msg, 1)

            def dist(p, c):
                mm(bank(1 - p, S_D0 + c)[:], left[:, D * c:D * c + D], right[:]).then_inc(s_d[c], 1)

            pe.wait_ge(s_w1s, 4)
            rows(0, lambda k: k, 0)
            conv1(0, None, 0)
            pe.wait_ge(s_u, 1); pe.wait_ge(s_w1d, 48)
            msg(0, None, 0)
            pe.wait_ge(s_left, 1); pe.wait_ge(s_right, 1)
            pe.wait_ge(s_h1, 1)
            dist(0, 0)
            pe.wait_ge(s_mt, 1)
            dist(0, 1)
            pe.wait_ge(s_e[0], 1)
            dist(0, 2)
            pe.wait_ge(s_e[1], 1)
            dist(0, 3)

            def conv_part(out_, w_h, w_l, phase, taps, p):
                for a in range(taps):
                    last = mm3(out_, w_h[:, a, :], w_l[:, a, :], ph_h[p][:, phase, a:a + HALF],
                               ph_l[p][:, phase, a:a + HALF], a == 0, a == taps - 1)
                return last

            def gate(out_, name, source, v_h, v_l, start, stop):
                cols = slice(D * GATE[name], D * GATE[name] + D)
                return mm3(out_[:], wg_h[:, source, cols], wg_l[:, source, cols], v_h[:], v_l[:], start, stop)

            def transposes(p, q):
                for c in range(CH):
                    last = nc.tensor.transpose(bank(p, S_T)[:, D * c:D * c + D], y2[:, D * c:D * c + D], cst[:, C_ID:C_ID + D])
                last.then_inc(s_t, 1)

            def adjacency(stage):
                sel = cst[0:64, C_SEL:C_SEL + CC]
                if stage == 0:
                    pe.wait_ge(s_bdi, 1)
                    for h in range(2):
                        for j in range(HP):
                            last = mm((p_r, p_z)[h][0:64, CC * j:CC * j + CC], bd[:, HP * h + j, :], sel)
                        last.then_inc(s_sel1m, 1)
                elif stage == 1:
                    for h in range(2):
                        pe.wait_ge(s_sel1, h + 1)
                        for j in range(HP):
                            last = mm((p_gi, p_gh)[h][0:CC, CC * j:CC * j + CC], sel1[:, HP * h + j, :], sel)
                        last.then_inc(s_acm, 1)
                else:
                    pe.wait_ge(s_ac, 2); pe.wait_ge(s_gd, 80)
                    for j in range(PAIRS):
                        last = mm(p_r[0:CC, j:j + 1], ac[:, j, :], cst[0:CC, C_ONE:C_ONE + 1])
                    last.then_inc(s_deg, 1)
                    mm(p_z[0:CC, 0:D], cst[0:NG, C_G5T:C_G5T + CC], b2g[:]).then_inc(s_b2m, 1)

            def step(b, p, n):
                q = 1 - p
                more = not static(b, B - 1)
                after(pe, s_phh, n(1)); after(pe, s_phl, n(1))
                after(pe, s_cu, n(0))
                if static(b, 0):
                    pe.wait_ge(s_wohi, 1); pe.wait_ge(s_wolo, 1)
                conv_part(p_bc[:, HALF:N], wo_h, wo_l, 2, NO, p)
                if static(b, 0):
                    adjacency(0)
                if more:
                    after(pe, s_e[2], n(1))
                    rows(q, n, 1)
                if static(b, 0):
                    pe.wait_ge(s_wohi, 2); pe.wait_ge(s_wolo, 2)
                conv_part(p_bc[:, 0:HALF], we_h, we_l, 1, NE, p).then_inc(s_bc, 1)
                if static(b, 0):
                    adjacency(1)
                if more:
                    after(pe, s_e[3], n(1))
                    conv1(q, n, 1)
                    after(pe, s_u, n(2))
                    msg(q, n, 1)
                if not static(b, 0):
                    after(pe, s_y2, n(0))
                    if more:
                        after(pe, s_h1, n(2))
                    else:
                        after(pe, s_e[3], n(1))
                    transposes(p, q)
                after(pe, s_ca, n(0))
                if static(b, 0):
                    pe.wait_ge(s_wohi, 3); pe.wait_ge(s_wolo, 3)
                conv_part(p_a[:, 0:HALF], ws_h, ws_l, 0, NE, p).then_inc(s_a, 1)
                if static(b, 0):
                    adjacency(2)
                after(pe, s_amh, n(1)); after(pe, s_aml, n(1)); after(pe, s_mh, n(1)); after(pe, s_ml, n(1))
                if more:
                    after(pe, s_mt, n(2))
                else:
                    after(pe, s_e[2], n(1))
                for c in range(CH):
                    cols = slice(D * c, D * c + D)
                    last = mm3(bank(p, S_NMP)[:], m_h[p][:, cols], m_l[p][:, cols], am_h[:, c, :], am_l[:, c, :],
                               c == 0, c == CH - 1)
                last.then_inc(s_nmp, 1)
                if more:
                    after(pe, s_left, n(2)); after(pe, s_right, n(2))
                    if static(b, 0):
                        after(pe, s_h1, n(2))
                    after(pe, s_yn, n(0))
                    dist(q, 0)
                if static(b, 0):
                    pe.wait_ge(s_wgs, 2)
                    pe.wait_ge(s_dg, 1); pe.wait_ge(s_b2r, 1)
                after(pe, s_rt, n(0)); gate(p_r, "r", 2, x_h[p], x_l[p], True, False)
                after(pe, s_zt, n(0)); gate(p_z, "z", 2, x_h[p], x_l[p], True, False)
                after(pe, s_gg, n(0)); gate(p_gh, "n", 2, x_h[p], x_l[p], True, True).then_inc(s_gx, 1)
                after(pe, s_nh, n(1)); after(pe, s_nl, n(1))
                if more:
                    dist(q, 1)
                gate(p_r, "r", 1, n_h, n_l, False, False)
                if more:
                    after(pe, s_e[0], n(2))
                    dist(q, 2)
                gate(p_z, "z", 1, n_h, n_l, False, False)
                after(pe, s_tt, n(0)); gate(p_gi, "n", 1, n_h, n_l, True, False).then_inc(s_gn, 1)
                if more:
                    after(pe, s_e[1], n(2))
                    dist(q, 3)
                after(pe, s_ch, n(1)); after(pe, s_cl, n(1))
                gate(p_r, "r", 0, c_h, c_l, False, True).then_inc(s_gr, 1)
                gate(p_gi, "n", 0, c_h, c_l, False, True).then_inc(s_gi, 1)
                gate(p_z, "z", 0, c_h, c_l, False, True).then_inc(s_gz, 1)

            batches(pe, step)
            pe.wait_ge(s_y2, B)
            pe.wait_ge(s_yn, B - 1)
            transposes(1, 0)
            groups_pe(pe, mm)

        @block.scalar
        def _(act):
            A = nc.scalar.activation

            def rows_u(p, n, k):
                after(act, s_rows, n(k + 1)); after(act, s_val, n(k))
                A(u[:], bank(1 - p, S_ROWS)[0:64, :], ACT.Identity, bias=brow[:, 0:1]).then_inc(s_u, 1)
                after(act, s_u, n(k + 1))
                A(ab[:], u[:], ACT.Identity, bias=cst[0:64, C_ROW + 1:C_ROW + 2], scale=cst[0:64, C_ROW:C_ROW + 1]).then_inc(s_ab, 1)

            def first_conv(p, n, k):
                after(act, s_c1, n(k + 1)); after(act, s_phd, n(k)); after(act, s_pho, n(k))
                A(h1[:, PAD:PAD + N], bank(1 - p, S_C1)[:], ACT.Relu, bias=prm[:, P_A1:P_A1 + 1],
                  scale=prm[:, P_S1:P_S1 + 1]).then_inc(s_h1, 1)
                after(act, s_h1, n(k + 1)); after(act, s_phl, n(k)); after(act, s_phh, n(k))
                A(ph[:, 0, :], h1[:, 1::2], ACT.Copy).then_inc(s_pho, 1)

            def keep_x(p, n, k):
                after(act, s_ya, n(k - 1)); after(act, s_cu, n(k - 1))
                A(xkeep[p][:], xin[p][:], ACT.Copy).then_inc(s_xk, 1)

            def msg_high(p, n, k):
                after(act, s_mt, n(k + 1)); after(act, s_nmp, n(k - 1))
                A(m_h[p][:], mt[:], ACT.Relu).then_inc(s_mh, 1)

            def exps(p, n, k, c):
                after(act, s_d[c], n(k + 1)); after(act, s_amh, n(k)); after(act, s_aml, n(k))
                A(am[:, c, :], bank(1 - p, S_D0 + c)[:], ACT.Exp).then_inc(s_e[c], 1)

            act.wait_ge(s_w2d, 16)
            A(wo_h[:], wc2[:, 1::2, :], ACT.Copy).then_inc(s_wohi, 1)
            act.wait_ge(s_cst, 16); act.wait_ge(s_small, 48); act.wait_ge(s_prm, 5)
            z = lambda k: k
            rows_u(0, z, 0)
            first_conv(0, z, 0)
            act.wait_ge(s_x[0], 16)
            keep_x(0, z, 0)
            A(we_h[:], wc2[:, 0::2, :], ACT.Copy).then_inc(s_wohi, 1)
            act.wait_ge(s_wsum, 2)
            A(ws_h[:], wsum, ACT.Copy).then_inc(s_wohi, 1)
            msg_high(0, z, 0)
            for c in range(CH):
                exps(0, z, 0, c)
            act.wait_ge(s_wgd, 32)
            A(wg_h[:], wg[:], ACT.Copy).then_inc(s_wgs, 1)
            act.wait_ge(s_fw, 2)
            A(fe[:], fw[:], ACT.Exp, bias=fs[:, 1:2], accum_out=fs[:, 2:3]).then_inc(s_fe, 1)

            def node_rows(p, n, k):
                after(act, s_t, n(k + 1)); after(act, s_yo, n(k))
                A(yn[:].rearrange("p c d -> p (c d)"), bank(p, S_T)[:], ACT.Copy).then_inc(s_yn, 1)

            def candidate(n, k):
                after(act, s_tt, n(k + 1)); after(act, s_yb, n(k))
                A(nn[:], tt[:], ACT.Tanh, bias=vec[:, V_IN:V_IN + 1]).then_inc(s_nn, 1)

            def step(b, p, n):
                q = 1 - p
                more = not static(b, B - 1)
                if static(b, 0):
                    act.wait_ge(s_wolo, 2)
                    for h in range(2):
                        act.wait_ge(s_sel1m, h + 1)
                        A(sel1[:, pairs(h), :], banked((p_r, p_z)[h], 64, CC), ACT.Copy).then_inc(s_sel1, 1)
                if not static(b, 0):
                    candidate(n, -1)
                for c in range(CH):
                    after(act, s_am[c], n(1))
                after(act, s_nmp, n(0))
                A(am_h[:], am[:], ACT.Copy).then_inc(s_amh, 1)
                if more:
                    rows_u(q, n, 1)
                    first_conv(q, n, 1)
                    after(act, s_x[q], dma_count(n, q, 1))
                    keep_x(q, n, 1)
                if not static(b, 0):
                    node_rows(p, n, -1)
                if more:
                    msg_high(q, n, 1)
                after(act, s_a, n(1)); after(act, s_cv, n(0))
                A(ca[:], p_a[:, 0:HALF], ACT.Identity, bias=prm[:, P_A2:P_A2 + 1], scale=prm[:, P_S2:P_S2 + 1]).then_inc(s_ca, 1)
                after(act, s_cv, n(1)); after(act, s_gz, n(0))
                A(c_h[:], cv[:], ACT.Relu).then_inc(s_ch, 1)
                after(act, s_nmp, n(1)); after(act, s_gn, n(0))
                A(n_h[:], bank(p, S_NMP)[:], ACT.Copy).then_inc(s_nh, 1)
                if more:
                    for c in range(CH):
                        exps(q, n, 1, c)
                after(act, s_gr, n(1)); after(act, s_gg, n(0))
                A(rt[:], p_r[:], ACT.Tanh, bias=prm[:, P_RH:P_RH + 1], scale=0.5).then_inc(s_rt, 1)
                after(act, s_gz, n(1)); after(act, s_yb, n(0)); after(act, s_ya, n(0))
                A(zt[:], p_z[:], ACT.Tanh, bias=prm[:, P_ZH:P_ZH + 1], scale=0.5).then_inc(s_zt, 1)

            batches(act, step)
            candidate(lambda k: B + k, -1)
            node_rows(1, lambda k: B + k, -1)
            groups_act(act)

        @block.gpsimd
        def _(pool):
            TT, TS = nc.gpsimd.tensor_tensor, nc.gpsimd.tensor_scalar
            nc.gpsimd.memset(bd[:], 0.0).then_inc(s_zero, 1)
            nc.gpsimd.memset(x1[:], 0.0).then_inc(s_zero, 1)
            nc.gpsimd.memset(h1[:, 0:PAD], 0.0).then_inc(s_zero, 1)
            nc.gpsimd.memset(h1[:, PAD + N:], 0.0).then_inc(s_zero, 1)
            pool.wait_ge(s_prm, 2)
            pool.wait_ge(s_cst, 16)
            TT(prm[:, P_RS:P_RS + 2], prm[:, P_VE:P_VE + 2], cst[:, C_MH:C_MH + 2], ALU.pow).then_inc(s_pow, 1)

            def rows_val(n, k):
                after(pool, s_u, n(k + 1)); after(pool, s_ab, n(k + 1)); after(pool, s_valh, n(k))
                after(pool, s_left, n(k)); after(pool, s_right, n(k))
                TT(val[:], u[:], ab[:], ALU.mult).then_inc(s_val, 1)

            def mask(p, n, k, c):
                if c == 0:
                    after(pool, s_adj[p], dma_count(n, p, k))
                after(pool, s_e[c], n(k + 1))
                TT(am[:, c, :], am[:, c, :], adj[p][:, c, :], ALU.mult).then_inc(s_am[c], 1)

            def powers(n, k):
                after(pool, s_base, n(k + 1))
                after(pool, s_yo, n(k))
                TT(rs[:], base[:], cst[:, C_MH:C_MH + CH + 1], ALU.pow).then_inc(s_rs, 1)

            rows_val(lambda k: k, 0)
            pool.wait_ge(s_w2d, 16)
            TT(wsum[:, 0:NO, :], wc2[:, 0:2 * NO:2, :], wc2[:, 1:2 * NO:2, :], ALU.add).then_inc(s_wsum, 1)
            nc.gpsimd.tensor_copy(wsum[:, NO:NE, :], wc2[:, TAPS - 1:TAPS, :]).then_inc(s_wsum, 1)
            for c in range(CH):
                mask(0, lambda k: k, 0, c)

            def step(b, p, n):
                q = 1 - p
                more = not static(b, B - 1)
                if more:
                    rows_val(n, 1)
                if not static(b, 0):
                    powers(n, -1)
                if static(b, 1):
                    pool.wait_ge(s_dg, 3)
                    TT(dg[:, 3, :], dg[:, 2, :], cst[0:CC, C_MH:C_MH + PAIRS], ALU.pow).then_inc(s_dpow, 1)
                if more:
                    for c in range(CH):
                        mask(q, n, 1, c)

            batches(pool, step)
            powers(lambda k: B + k, -1)
            groups_pool(pool)

        @block.vector
        def _(dve):
            TT, TS, STT, CP = nc.vector.tensor_tensor, nc.vector.tensor_scalar, nc.vector.scalar_tensor_tensor, nc.vector.tensor_copy

            dve.wait_ge(s_small, 48)
            TS(prm[:, P_VE:P_VE + 1], vec[:, V_V1:V_V1 + 1], EPS, None, ALU.add).then_inc(s_prm, 1)
            TS(prm[:, P_VE + 1:P_VE + 2], vec[:, V_V2:V_V2 + 1], EPS, None, ALU.add).then_inc(s_prm, 1)

            def split_x(p, n, k):
                after(dve, s_x[p], dma_count(n, p, k)); after(dve, s_gx, n(k - 1))
                CP(x_h[p][:], xin[p][:]).then_inc(s_xh, 1)
                after(dve, s_xh, n(k + 1))
                TT(x_l[p][:], xin[p][:], full(x_h[p][:]), ALU.subtract).then_inc(s_xl, 1)

            split_x(0, lambda k: k, 0)
            dve.wait_ge(s_w1d, 48)
            CP(wrow_h[:], wrow[:]).then_inc(s_w1s, 1)
            CP(wc1_h[:], wc1[:]).then_inc(s_w1s, 1)
            dve.wait_ge(s_w1s, 2)
            TT(wrow_l[:], wrow[:], full(wrow_h[:]), ALU.subtract).then_inc(s_w1s, 1)
            TT(wc1_l[:], wc1[:], full(wc1_h[:]), ALU.subtract).then_inc(s_w1s, 1)
            dve.wait_ge(s_pow, 1)
            TT(prm[:, P_S1:P_S1 + 1], vec[:, V_G1:V_G1 + 1], prm[:, P_RS:P_RS + 1], ALU.mult)
            TT(prm[:, P_S2:P_S2 + 1], vec[:, V_G2:V_G2 + 1], prm[:, P_RS + 1:P_RS + 2], ALU.mult)
            TT(prm[:, P_R:P_R + 2], vec[:, V_IR:V_IR + 2], vec[:, V_HR:V_HR + 2], ALU.add).then_inc(s_prm, 1)
            dve.wait_ge(s_prm, 3)
            TS(prm[:, P_RH:P_RH + 2], prm[:, P_R:P_R + 2], 0.5, None, ALU.mult)
            TT(prm[:, P_T1:P_T1 + 1], vec[:, V_M1:V_M1 + 1], prm[:, P_S1:P_S1 + 1], ALU.mult)
            TT(prm[:, P_T2:P_T2 + 1], vec[:, V_M2:V_M2 + 1], prm[:, P_S2:P_S2 + 1], ALU.mult).then_inc(s_prm, 1)
            dve.wait_ge(s_prm, 4)
            TT(prm[:, P_A1:P_A1 + 1], vec[:, V_B1:V_B1 + 1], prm[:, P_T1:P_T1 + 1], ALU.subtract)
            TT(prm[:, P_A2:P_A2 + 1], vec[:, V_B2:V_B2 + 1], prm[:, P_T2:P_T2 + 1], ALU.subtract).then_inc(s_prm, 1)

            def left_right(n, k):
                after(dve, s_val, n(k + 1))
                CP(val_h[:], val[:]).then_inc(s_valh, 1)
                after(dve, s_valh, n(k + 1)); after(dve, s_d[CH - 1], n(k))
                STT(left[:], full(val_h[0:KD, :]), cst[0:KD, C_ROW + 2:C_ROW + 3], val[0:KD, :], ALU.mult, ALU.add).then_inc(s_left, 1)
                STT(right[:], full(val_h[32:32 + KD, :]), cst[32:32 + KD, C_ROW + 2:C_ROW + 3], val[32:32 + KD, :],
                    ALU.mult, ALU.add).then_inc(s_right, 1)

            def phases(p, n, k):
                after(dve, s_h1, n(k + 1)); after(dve, s_phl, n(k))
                TT(ph[:, 1, :], h1[:, 0::2], h1[:, 1::2], ALU.subtract)
                TT(ph[:, 2, 0:PH - 1], h1[:, 2::2], h1[:, 1:N + 2 * PAD - 2:2], ALU.subtract).then_inc(s_phd, 1)
                after(dve, s_pho, n(k + 1)); after(dve, s_phd, n(k + 1)); after(dve, s_a, n(k - 1))
                CP(ph_h[p][:], ph[:]).then_inc(s_phh, 1)
                after(dve, s_phh, n(k + 1))
                TT(ph_l[p][:], ph[:], full(ph_h[p][:]), ALU.subtract).then_inc(s_phl, 1)

            def msg_sum(p, n, k):
                after(dve, s_msg, n(k + 1)); after(dve, s_mh, n(k)); after(dve, s_ml, n(k))
                TT(mt[:].rearrange("p (c d) -> p c d", c=CH), bank(1 - p, S_MSG)[:].rearrange("p (c d) -> p c d", c=CH),
                   bmsg[:].unsqueeze(1).broadcast_to([128, CH, D]), ALU.add).then_inc(s_mt, 1)

            def msg_low(p, n, k):
                after(dve, s_mh, n(k + 1)); after(dve, s_mt, n(k + 1))
                STT(m_l[p][:], mt[:], 0.0, full(m_h[p][:]), ALU.max, ALU.subtract).then_inc(s_ml, 1)

            zero = lambda k: k
            nc.vector.memset(ph[:, 2, PH - 1:PH], 0.0)
            left_right(zero, 0)
            dve.wait_ge(s_zero, 4)
            dve.wait_ge(s_wohi, 1)
            TT(wo_l[:], wc2[:, 1::2, :], full(wo_h[:]), ALU.subtract).then_inc(s_wolo, 1)
            phases(0, zero, 0)
            msg_sum(0, zero, 0)
            msg_low(0, zero, 0)
            dve.wait_ge(s_wohi, 2)
            TT(we_l[:], wc2[:, 0::2, :], full(we_h[:]), ALU.subtract).then_inc(s_wolo, 1)
            dve.wait_ge(s_wohi, 3)
            TT(ws_l[:], wsum, full(ws_h[:]), ALU.subtract).then_inc(s_wolo, 1)
            dve.wait_ge(s_wgs, 1)
            TT(wg_l[:], wg[:], full(wg_h[:]), ALU.subtract).then_inc(s_wgs, 1)
            dve.wait_ge(s_gd, 80)
            nc.vector.reduce_max(fs[:, 0:1], fw[:], AX.X).then_inc(s_fw, 1)
            dve.wait_ge(s_fw, 1)
            TS(fs[:, 1:2], fs[:, 0:1], -1.0, None, ALU.mult).then_inc(s_fw, 1)
            dve.wait_ge(s_bdd, 32); dve.wait_ge(s_cst, 16)
            TT(bd[:], bd[:], cst[0:64, C_ID:C_ID + 64].unsqueeze(1).broadcast_to([64, PAIRS, 64]), ALU.add).then_inc(s_bdi, 1)

            def adjacency(stage):
                if stage == 0:
                    for h in range(2):
                        dve.wait_ge(s_acm, h + 1)
                        TT(ac[:, pairs(h), :], banked((p_gi, p_gh)[h], CC, CC),
                           cst[0:CC, C_SAME:C_SAME + CC].unsqueeze(1).broadcast_to([CC, HP, CC]), ALU.mult).then_inc(s_ac, 1)
                else:
                    dve.wait_ge(s_deg, 1)
                    CP(dg[:, 0, :], p_r[0:CC, 0:PAIRS]).then_inc(s_dg, 1)
                    dve.wait_ge(s_b2m, 1)
                    CP(b2r[:], p_z[0:CC, 0:D]).then_inc(s_b2r, 1)
                    dve.wait_ge(s_dg, 1)
                    TS(dg[:, 1, :], dg[:, 0, :], 0.0, None, ALU.is_equal).then_inc(s_dg, 1)
                    dve.wait_ge(s_dg, 2)
                    TT(dg[:, 2, :], dg[:, 0, :], dg[:, 1, :], ALU.add).then_inc(s_dg, 1)

            def gate_mid(n, k):
                after(dve, s_rt, n(k + 1)); after(dve, s_gg, n(k))
                TS(r1[:], rt[:], 0.5, 0.5, ALU.mult, ALU.add).then_inc(s_r1, 1)
                after(dve, s_r1, n(k + 1)); after(dve, s_gx, n(k + 1)); after(dve, s_tt, n(k))
                STT(gg[:], p_gh[:], vec[:, V_HN:V_HN + 1], r1[:], ALU.add, ALU.mult).then_inc(s_gg, 1)
                after(dve, s_gg, n(k + 1)); after(dve, s_gi, n(k + 1)); after(dve, s_nn, n(k))
                TT(tt[:], p_gi[:], gg[:], ALU.add).then_inc(s_tt, 1)

            def result(p, n, k):
                after(dve, s_zt, n(k + 1)); after(dve, s_xk, n(k + 1)); after(dve, s_y2, n(k))
                STT(ya, zt[:], 3.0, xkeep[p][:], ALU.add, ALU.mult).then_inc(s_ya, 1)
                after(dve, s_nn, n(k + 1))
                STT(yb, zt[:], -1.0, nn[:], ALU.add, ALU.mult).then_inc(s_yb, 1)
                after(dve, s_ya, n(k + 1)); after(dve, s_yb, n(k + 1)); after(dve, s_t, n(k))
                TT(y2, ya, yb, ALU.subtract).then_inc(s_y2, 1)

            def stats(n, k):
                after(dve, s_yn, n(k + 1)); after(dve, s_mv, n(k))
                for c in range(CH):
                    last = nc.vector.bn_stats(st[:, c, :], yn[:, c, :])
                last.then_inc(s_st, 1)
                after(dve, s_st, n(k + 1)); after(dve, s_base, n(k)); after(dve, s_yo, n(k))

            def moments(n, k):
                for c in range(CH):
                    last = nc.vector.bn_aggr(mv[:, c, :], st[:, c, :])
                last.then_inc(s_mv, 1)
                after(dve, s_mv, n(k + 1)); after(dve, s_rs, n(k))
                TS(base[:, 0:CH], mv[:, :, 1], 1.0 + EPS, 4 * EPS * EPS, ALU.mult, ALU.add)
                TS(base[:, CH:CH + 1], mv[:, 0, 1:2], 1.0, 4 * EPS, ALU.mult, ALU.add).then_inc(s_base, 1)

            def normalise(q, n, k, pair):
                after(dve, s_rs, n(k + 1)); after(dve, s_mv, n(k + 1))
                if isinstance(n(k), int):
                    after(dve, s_out[q], 16 * (n(k) // 2))
                else:
                    dve.wait_ge(s_out[q], (n(k) - q) * 8)
                for c in range(CH):
                    TS(yo[q][:, c, :], yn[:, c, :], mv[:, c, 0:1], rs[:, c:c + 1], ALU.subtract, ALU.mult)
                TS(x1[SLOT * q:SLOT * q + GN, pair, :], yn[0:GN, 0, :], mv[0:GN, 0, 0:1], rs[0:GN, CH:CH + 1],
                   ALU.subtract, ALU.mult).then_inc(s_yo, 1)

            def step(b, p, n):
                q = 1 - p
                more = not static(b, B - 1)
                if more:
                    split_x(q, n, 1)
                if not static(b, 0):
                    gate_mid(n, -1)
                    result(q, n, -1)
                after(dve, s_amh, n(1)); after(dve, s_nmp, n(0))
                TT(am_l[:], am[:], full(am_h[:]), ALU.subtract).then_inc(s_aml, 1)
                if more:
                    left_right(n, 1)
                if static(b, 0):
                    adjacency(0)
                after(dve, s_bc, n(1)); after(dve, s_cv, n(0)); after(dve, s_xk, n(1))
                STT(cu[:].rearrange("p (k two) -> p two k", two=2), p_bc[:].rearrange("p (two k) -> p two k", two=2),
                    prm[:, P_S2:P_S2 + 1], xkeep[p][:].rearrange("p (k two) -> p two k", two=2),
                    ALU.mult, ALU.add).then_inc(s_cu, 1)
                if more:
                    msg_sum(q, n, 1)
                if not static(b, 0):
                    stats(n, -1)
                if more:
                    phases(q, n, 1)
                    msg_low(q, n, 1)
                if not static(b, 0):
                    moments(n, -1)
                if static(b, 0):
                    adjacency(1)
                after(dve, s_ca, n(1)); after(dve, s_cu, n(1)); after(dve, s_ch, n(0)); after(dve, s_cl, n(0))
                TT(cv[:].rearrange("p (k two) -> p k two", two=2), cu[:].rearrange("p (k two) -> p k two", two=2),
                   ca[:].unsqueeze(2).broadcast_to([128, HALF, 2]), ALU.add).then_inc(s_cv, 1)
                after(dve, s_ch, n(1)); after(dve, s_cv, n(1)); after(dve, s_gz, n(0))
                STT(c_l[:], cv[:], 0.0, full(c_h[:]), ALU.max, ALU.subtract).then_inc(s_cl, 1)
                after(dve, s_nh, n(1)); after(dve, s_gn, n(0))
                TT(n_l[:], bank(p, S_NMP)[:], full(n_h[:]), ALU.subtract).then_inc(s_nl, 1)
                if not static(b, 0):
                    normalise(q, n, -1, pair_of(b, p, n))

            def pair_of(b, p, n):
                if isinstance(b, int):
                    return (b - 1) // 2
                return loop_pair[0] - (1 - p)

            loop_pair = [None]
            step(0, 0, lambda k: k)
            step(1, 1, lambda k: 1 + k)
            with dve.Fori(1, PAIRS - 1) as i:
                loop_pair[0] = i
                for p in range(2):
                    known = {}

                    def count(k, p=p, known=known):
                        if k not in known:
                            known[k] = dve.snap(i * 2 + (p + k))
                        return known[k]
                    step(count(0), p, count)
            step(B - 2, 0, lambda k: B - 2 + k)
            step(B - 1, 1, lambda k: B - 1 + k)
            last = lambda k: B + k
            gate_mid(last, -1)
            result(1, last, -1)
            stats(last, -1)
            moments(last, -1)
            normalise(1, last, -1, PAIRS - 1)
            groups_dve(dve)



def kernel(x, adj, L0_gnn_w_se, L0_gnn_b_se, L0_gnn_conv1_w, L0_gnn_bn1_g, L0_gnn_bn1_b, L0_gnn_bn1_m, L0_gnn_bn1_v,
           L0_gnn_conv2_w, L0_gnn_bn2_g, L0_gnn_bn2_b, L0_gnn_bn2_m, L0_gnn_bn2_v, L0_gnn_w_msg, L0_gnn_b_msg,
           L0_gnn_w_ih, L0_gnn_b_ih, L0_gnn_w_hh, L0_gnn_b_hh, L1_gnn_W1, L1_gnn_b1, L1_gnn_W2, L1_gnn_b2, L1_gnn_fusion_w):
    import concourse.bacc as bacc
    from concourse.bass_utils import run_bass_kernel_spmd

    a = lambda t: np.asarray(t)
    c = np.ascontiguousarray
    b_ih, b_hh = a(L0_gnn_b_ih).reshape(3, D), a(L0_gnn_b_hh).reshape(3, D)
    vecs = c(np.stack([a(L0_gnn_bn1_g), a(L0_gnn_bn1_b), a(L0_gnn_bn1_m), a(L0_gnn_bn1_v),
                       a(L0_gnn_bn2_g), a(L0_gnn_bn2_b), a(L0_gnn_bn2_m), a(L0_gnn_bn2_v),
                       b_ih[0], b_ih[1], b_ih[2], b_hh[0], b_hh[1], b_hh[2]], axis=1))
    w_se, b_se = a(L0_gnn_w_se), a(L0_gnn_b_se)
    w_rows, b_rows = np.zeros((D, 128), w_se.dtype), np.zeros((64, 1), b_se.dtype)
    for side, rows in enumerate(dist_rows()):
        for r, (k, _, _, _) in enumerate(rows):
            if k is None:
                b_rows[32 * side + r, 0] = 1
            else:
                w_rows[:, 32 * side + r] = w_se[k]
                b_rows[32 * side + r, 0] = b_se[k]
    arrays = {
        "xT": c(a(x).transpose(0, 2, 1)), "adjT": c(a(adj).transpose(0, 2, 1)), "consts": constants(),
        "vecs": vecs, "w_rows": w_rows, "b_rows": b_rows,
        "w_c1": c(a(L0_gnn_conv1_w)[:, :, 0].T), "w_c2": c(a(L0_gnn_conv2_w).transpose(1, 2, 0)),
        "w_ih": c(a(L0_gnn_w_ih).reshape(3 * D, 2, D).transpose(2, 1, 0)), "w_hh": c(a(L0_gnn_w_hh).T),
        "w_msg": c(a(L0_gnn_w_msg).T), "b_msg": a(L0_gnn_b_msg).reshape(1, D),
        "g_w1": a(L1_gnn_W1), "g_b1": c(a(L1_gnn_b1).reshape(NG, 2, D).transpose(2, 0, 1)),
        "g_w2": a(L1_gnn_W2), "g_b2": a(L1_gnn_b2), "g_fw": a(L1_gnn_fusion_w).reshape(1, NG),
    }
    nc = bacc.Bacc("TRN2", target_bir_lowering=False, num_devices=1)
    args = [nc.dram_tensor(name, v.shape, mybir.dt.from_np(v.dtype), kind="ExternalInput").ap() for name, v in arrays.items()]
    args.append(nc.dram_tensor("out", (B, N, D), mybir.dt.float32, kind="ExternalOutput").ap())
    gnn_kernel(nc, *args)
    result = run_bass_kernel_spmd(nc, [arrays], core_ids=[0])
    return result.results[0]["out"]
```

```python
import numpy as np
import concourse.bass as bass
from concourse import mybir
from contextlib import ExitStack

B, N, D = 16, 512, 128
TAPS = 17
PAD = (TAPS - 1) // 2
EPS = 1e-5
GROUPS = [list(range(25)), [0, 1, 2, 3, 4, 5, 6, 7, 8], [0, 9, 10, 11, 12, 13, 14],
          [6, 7, 8, 12, 13, 14], [3, 4, 5, 9, 10, 11]]
HID = 256
GN = 25
SLOT = 32
PAIRS = B // 2
GSIZE = [2 * len(g) for g in GROUPS]
GOFF = [sum(GSIZE[:g]) for g in range(len(GROUPS))]
CC = sum(GSIZE)
NG = len(GROUPS)
CH = N // D
HALF = N // 2
NE = (TAPS + 1) // 2
NO = TAPS // 2
PH = HALF + PAD

KD = 24


def dist_rows():
    left, right = [], []
    for hl in ((0, 0), (0, 1), (1, 0), (1, 1)):
        for k in range(3):
            left.append((k, 0.0, 1.0, hl[0]))
            right.append((k, 0.0, 2.0, hl[1]))
    for low in (0, 1):
        for k in range(3):
            left.append((k, 1.0, 0.0, low))
            right.append((None, 0.0, -1.0, 0))
    for low in (0, 1):
        for k in range(3):
            left.append((None, 0.0, 1.0, 0))
            right.append((k, -1.0, 0.0, low))
    return left, right


(V_G1, V_B1, V_M1, V_V1, V_G2, V_B2, V_M2, V_V2, V_IR, V_IZ, V_IN, V_HR, V_HZ, V_HN) = range(14)
NV = 14

C_SEL = 0
C_SELT = C_SEL + CC
C_SAME = C_SELT + 64
C_G5 = C_SAME + CC
C_G5T = C_G5 + NG
C_ID = C_G5T + CC
C_ROW = C_ID + D
C_ONE = C_ROW + 3
C_MH = C_ONE + 1
NCONST = C_MH + 8


def constants():
    c = np.zeros((128, NCONST), np.float32)
    for g, nodes in enumerate(GROUPS):
        for b in range(2):
            for i, n in enumerate(nodes):
                row = GOFF[g] + b * len(nodes) + i
                c[SLOT * b + n, C_SEL + row] = 1
                c[row, C_SELT + SLOT * b + n] = 1
                c[row, C_SAME + GOFF[g]:C_SAME + GOFF[g] + GSIZE[g]] = 1
                c[row, C_G5 + g] = 1
                c[g, C_G5T + row] = 1
    c[:, C_ID:C_ID + D] = np.eye(D)
    for side, rows in enumerate(dist_rows()):
        for r, (_, alpha, beta, low) in enumerate(rows):
            c[32 * side + r, C_ROW:C_ROW + 3] = alpha, beta, -low
    c[:, C_ONE] = 1
    c[:, C_MH:C_MH + 8] = -0.5
    return c


def gnn_kernel(nc, xT, adjT, consts, vecs, w_rows, b_rows, w_c1, w_c2, w_ih, w_hh, w_msg, b_msg,
               g_w1, g_b1, g_w2, g_b2, g_fw, out):
    fp32 = mybir.dt.float32
    fp32r = mybir.dt.float32r
    ALU = mybir.AluOpType
    ACT = mybir.ActivationFunctionType
    AX = mybir.AxisListType

    ctx = ExitStack()
    with ctx:
        def sb(name, shape, dt=fp32):
            return ctx.enter_context(nc.sbuf_tensor(name, shape, dt))

        def sem(name):
            return ctx.enter_context(nc.semaphore(name))

        def full(ap):
            return ap.bitcast(fp32)

        cst = sb("cst", [128, NCONST])
        vec = sb("vec", [128, NV])
        brow = sb("brow", [64, 1])
        wrow = sb("wrow", [128, 128]); wrow_h = sb("wrow_h", [128, 128], fp32r); wrow_l = sb("wrow_l", [128, 128], fp32r)
        wc1 = sb("wc1", [128, D]); wc1_h = sb("wc1_h", [128, D], fp32r); wc1_l = sb("wc1_l", [128, D], fp32r)
        wc2 = sb("wc2", [128, TAPS, D])
        yy = sb("yy", [128, 3 * N])
        ya, yb, y2 = yy[:, 0:N], yy[:, N:2 * N], yy[:, 2 * N:3 * N]
        wsum = yy[:, 0:NE * D].rearrange("p (t d) -> p t d", d=D)
        wo_h = sb("wo_h", [128, NO, D], fp32r); wo_l = sb("wo_l", [128, NO, D], fp32r)
        we_h = sb("we_h", [128, NE, D], fp32r); we_l = sb("we_l", [128, NE, D], fp32r)
        ws_h = sb("ws_h", [128, NE, D], fp32r); ws_l = sb("ws_l", [128, NE, D], fp32r)
        wg = sb("wg", [128, 3, 3 * D])
        wg_h = sb("wg_h", [128, 3, 3 * D], fp32r); wg_l = sb("wg_l", [128, 3, 3 * D], fp32r)
        wmsg = sb("wmsg", [128, D])
        bmsg = sb("bmsg", [128, D])
        prm = sb("prm", [128, 16])
        P_VE, P_RS, P_S1, P_S2, P_T1, P_T2, P_A1, P_A2, P_R, P_Z, P_RH, P_ZH = 0, 2, 4, 5, 6, 7, 8, 9, 10, 11, 12, 13

        xin = [sb(f"xin{p}", [128, N]) for p in range(2)]
        xkeep = [sb(f"xkeep{p}", [128, N]) for p in range(2)]
        x_h = [sb(f"x_h{p}", [128, N], fp32r) for p in range(2)]
        x_l = [sb(f"x_l{p}", [128, N], fp32r) for p in range(2)]
        adj = [sb(f"adj{p}", [128, CH, N]) for p in range(2)]
        uab = sb("uab", [64, 2 * N]); u = uab[:, 0:N]; ab = uab[:, N:2 * N]; val = sb("val", [64, N]); val_h = sb("val_h", [64, N], fp32r)
        left = sb("left", [KD, N], fp32r); right = sb("right", [KD, N], fp32r)
        h1 = sb("h1", [128, N + 2 * PAD])
        ph = sb("ph", [128, 3, PH])
        ph_h = [sb(f"ph_h{p}", [128, 3, PH], fp32r) for p in range(2)]
        ph_l = [sb(f"ph_l{p}", [128, 3, PH], fp32r) for p in range(2)]
        am = sb("am", [128, CH, N])
        am_h = sb("am_h", [128, CH, N], fp32r); am_l = sb("am_l", [128, CH, N], fp32r)
        mt = sb("mt", [128, N])
        m_h = [sb(f"m_h{p}", [128, N], fp32r) for p in range(2)]
        m_l = [sb(f"m_l{p}", [128, N], fp32r) for p in range(2)]
        n_h = sb("n_h", [128, N], fp32r); n_l = sb("n_l", [128, N], fp32r)
        ca = sb("ca", [128, HALF]); cu = sb("cu", [128, N]); cv = sb("cv", [128, N])
        c_h = sb("c_h", [128, N], fp32r); c_l = sb("c_l", [128, N], fp32r)
        rt = sb("rt", [128, N]); r1 = rt; zt = sb("zt", [128, N])
        gg = sb("gg", [128, N]); tt = sb("tt", [128, N]); nn = sb("nn", [128, N])
        yn = sb("yn", [128, CH, D]); st = sb("st", [128, CH, 6]); mv = sb("mv", [128, CH, 2]); base = sb("base", [128, CH + 1]); rs = sb("rs", [128, CH + 1])
        yo = [sb(f"yo{p}", [128, CH, D]) for p in range(2)]

        x1 = sb("x1", [64, PAIRS, D])
        bd = sb("bd", [64, PAIRS, 64])
        ac = sb("ac", [CC + NG, PAIRS, CC])
        dg = sb("dg", [CC, 4, PAIRS])
        dinv = sb("dinv", [CC, PAIRS])
        fw = sb("fw", [CC, NG]); fs = sb("fs", [CC, 4]); fe = sb("fe", [CC, NG]); wcol = sb("wcol", [CC, 1])
        
        gw1 = sb("gw1", [128, NG, HID]); gw2 = sb("gw2", [128, NG, 2, D]); gb1 = sb("gb1", [128, NG, 2])

        ring = [ctx.enter_context(nc.psum_tensor(f"ring{i}", [128, N], fp32)) for i in range(2)]
        p_bc = ctx.enter_context(nc.psum_tensor("p_bc", [128, N], fp32))
        p_a = ctx.enter_context(nc.psum_tensor("p_a", [128, N], fp32))
        p_r, p_z, p_gi, p_gh = [ctx.enter_context(nc.psum_tensor(n, [128, N], fp32)) for n in ("p_r", "p_z", "p_gi", "p_gh")]

        s_cst = sem("s_cst"); s_vec = sem("s_vec"); s_wc1d = sem("s_wc1d"); s_wrowd = sem("s_wrowd")
        s_brow = sem("s_brow"); s_wmsgd = sem("s_wmsgd"); s_bmsg = sem("s_bmsg"); s_w2od = sem("s_w2od"); s_w2ed = sem("s_w2ed"); s_wgd = sem("s_wgd")
        s_gd = sem("s_gd"); s_bdd = sem("s_bdd"); s_zero = sem("s_zero")
        s_prm = sem("s_prm"); s_pow = sem("s_pow"); s_wsum = sem("s_wsum")
        s_w1s = sem("s_w1s"); s_wohi = sem("s_wohi"); s_wolo = sem("s_wolo"); s_wgs = sem("s_wgs")
        s_bdi = sem("s_bdi"); s_sel1m = sem("s_sel1m"); s_sel1 = sem("s_sel1"); s_acm = sem("s_acm"); s_ac = sem("s_ac")
        s_deg = sem("s_deg"); s_dg = sem("s_dg"); s_dpow = sem("s_dpow"); s_dinv = sem("s_dinv")
        s_fw = sem("s_fw"); s_fe = sem("s_fe"); s_wcol = sem("s_wcol")
        s_x = [sem(f"s_x{p}") for p in range(2)]
        s_adj = [sem(f"s_adj{p}") for p in range(2)]
        s_xh = sem("s_xh"); s_xl = sem("s_xl"); s_xk = sem("s_xk")
        s_rows = sem("s_rows"); s_u = sem("s_u"); s_ab = sem("s_ab"); s_val = sem("s_val"); s_valh = sem("s_valh")
        s_left = sem("s_left"); s_right = sem("s_right")
        s_c1 = sem("s_c1"); s_h1 = sem("s_h1"); s_pho = sem("s_pho"); s_phd = sem("s_phd"); s_phh = sem("s_phh"); s_phl = sem("s_phl")
        s_msg = sem("s_msg"); s_mt = sem("s_mt"); s_mh = sem("s_mh"); s_ml = sem("s_ml")
        s_d = [sem(f"s_d{c}") for c in range(CH)]; s_e = [sem(f"s_e{c}") for c in range(CH)]
        s_am = [sem(f"s_am{c}") for c in range(CH)]; s_amh = sem("s_amh"); s_aml = sem("s_aml")
        s_bc = sem("s_bc"); s_a = sem("s_a"); s_ca = sem("s_ca"); s_cu = sem("s_cu"); s_cv = sem("s_cv"); s_ch = sem("s_ch"); s_cl = sem("s_cl")
        s_nmp = sem("s_nmp"); s_nh = sem("s_nh"); s_nl = sem("s_nl")
        s_gx = sem("s_gx"); s_gn = sem("s_gn"); s_gr = sem("s_gr"); s_gi = sem("s_gi"); s_gz = sem("s_gz")
        s_rt = sem("s_rt"); s_zt = sem("s_zt"); s_r1 = sem("s_r1"); s_gg = sem("s_gg"); s_tt = sem("s_tt"); s_nn = sem("s_nn")
        s_ya = sem("s_ya"); s_yb = sem("s_yb"); s_y2 = sem("s_y2")
        s_t = sem("s_t"); s_yn = sem("s_yn"); s_st = sem("s_st"); s_mv = sem("s_mv"); s_base = sem("s_base"); s_rs = sem("s_rs"); s_grow = sem("s_grow"); s_yo = sem("s_yo")
        s_out = [sem(f"s_out{p}") for p in range(2)]
        s_q = [sem(f"s_q{i}") for i in range(18)]
        s_fin = sem("s_fin")

        HP = 4
        LOTS = [(0, 4), (4, PAIRS - 1), (PAIRS - 1, PAIRS)]
        EARLY, LATE = (0, 1), (2,)
        SPAN = {0: (0, PAIRS - 1), 1: (PAIRS - 1, PAIRS)}

        def part(t, a, rows, width):
            flat = t[:] if len(t.shape) == 2 else t[:].rearrange("p a b -> p (a b)")
            return flat[0:rows, a:a + PAIRS * width].rearrange("p (j w) -> p j w", w=width)

        sel1 = part(wc2, 0, 64, CC)
        diag = part(wc2, 0, CC, CC)
        msel = part(wc2, PAIRS * CC, 64, CC)
        agT, hT0, hT1 = part(adj[1], 0, 128, CC), part(adj[1], PAIRS * CC, 128, CC), part(wc2, 0, 128, CC)
        hT = (hT0, hT1)
        hz = adj[0][:].rearrange("p a b -> p (a b)")[:, 0:2 * NG * CC].rearrange("p (k g c) -> p k g c", k=2, g=NG)
        sT = part(adj[0], 2 * NG * CC, 128, CC)
        ss, o2 = part(am, 0, CC + NG, D), part(am, PAIRS * D, CC, D)
        yfin = uab[:, 0:PAIRS * D].rearrange("p (j d) -> p j d", d=D)
        gst = sb("gst", [64, PAIRS, 6]); gmv = sb("gmv", [64, PAIRS, 2]); gbase = sb("gbase", [64, PAIRS]); grs = sb("grs", [64, PAIRS])
        (Q_BC, Q_AC, Q_MSEL, Q_MS, Q_TR, Q_AGT, Q_W1, Q_H0, Q_H1, Q_W2, Q_S, Q_TS, Q_SS, Q_AGG2, Q_O2, Q_SC, Q_FIN) = range(17)
        s_bias = sem("s_bias"); s_zz = sem("s_zz"); s_diag = sem("s_diag"); s_hz = sem("s_hz")
        s_gmv = sem("s_gmv"); s_gbase = sem("s_gbase"); s_grs = sem("s_grs"); s_gst = sem("s_gst")

        BC_BANKS, MSEL_BANKS = (p_r, p_z), (p_gi, p_gh)
        TR_BANKS = (p_r, p_z, p_z)
        W1_BANKS = (p_bc, p_a, ring[1], p_gh)
        W2_BANKS = (p_r, p_z, p_gi)
        W1_LATE = (ring[0], p_z)
        W2_LATE = p_gi
        TS_BANKS = (p_bc, p_a)
        AGG2_BANKS = (ring[1], p_gh, p_r)
        SC_BANKS = (p_bc, p_a, ring[0])

        def lot(i):
            return slice(*LOTS[i])

        def lot_size(i):
            return LOTS[i][1] - LOTS[i][0]

        def pairs(h):
            return slice(HP * h, HP * h + HP)

        def group(g):
            return slice(GOFF[g], GOFF[g] + GSIZE[g])

        def banked(bank_, rows, width, count=HP):
            return bank_[0:rows, 0:count * width].rearrange("p (j w) -> p j w", w=width)

        def cols(bank_, g):
            return bank_[:, 0:(PAIRS - 1) * GSIZE[g]].rearrange("p (j w) -> p j w", w=GSIZE[g])

        ERL = slice(0, PAIRS - 1)

        class GroupsPE:

            def spread(self, pe, mm):
                pe.wait_ge(s_diag, 2)
                for h in range(2):
                    mm(BC_BANKS[h][0:CC, 0:HP * CC], cst[0:CC, C_SAME:C_SAME + CC], diag[:, pairs(h), :]).then_inc(s_q[Q_BC], 1)

            def combine(self, pe, mm):
                for h in range(2):
                    pe.wait_ge(s_q[Q_AC], h + 1)
                    mm(MSEL_BANKS[h][0:64, 0:HP * CC], cst[0:CC, C_SELT:C_SELT + 64], ac[0:CC, pairs(h), :]).then_inc(s_q[Q_MSEL], 1)

            def aggregate(self, pe, mm, i):
                for n, j in enumerate(range(*LOTS[i])):
                    last = mm(TR_BANKS[i][:, CC * n:CC * n + CC], x1[:, j, :], msel[:, j, :])
                last.then_inc(s_q[Q_TR], 1)

            def first_early(self, pe, mm):
                pe.wait_ge(s_q[Q_AGT], 2)
                for g in range(NG):
                    for k in range(2):
                        if g >= 2:
                            pe.wait_ge(s_q[(Q_H0, Q_H1)[k]], g - 1)
                        mm(cols(W1_BANKS[(2 * g + k) % 4], g), gw1[:, g, D * k:D * k + D],
                           agT[:, ERL, group(g)]).then_inc(s_q[Q_W1], 1)

            def second_early(self, pe, mm):
                for g in range(NG):
                    pe.wait_ge(s_q[Q_H0], g + 1); pe.wait_ge(s_q[Q_H1], g + 1)
                    if g >= 3:
                        pe.wait_ge(s_q[Q_S], g - 2)
                    for k in range(2):
                        last = mm(cols(W2_BANKS[g % 3], g), gw2[:, g, k, :], hT[k][:, ERL, group(g)], k == 0, k == 1)
                    last.then_inc(s_q[Q_W2], 1)

            def first_late(self, pe, mm):
                pe.wait_ge(s_q[Q_AGT], 3)
                for k in range(2):
                    for g in range(NG):
                        last = mm(W1_LATE[k][:, group(g)], gw1[:, g, D * k:D * k + D], agT[:, PAIRS - 1, group(g)])
                    last.then_inc(s_q[Q_W1], 1)

            def second_late(self, pe, mm):
                for k in range(2):
                    pe.wait_ge(s_q[(Q_H0, Q_H1)[k]], NG + 1)
                    for g in range(NG):
                        last = mm(W2_LATE[0:CC, 0:D], hz[:, k, g, :], gw2[:, g, k, :], g == 0 and k == 0, g == NG - 1 and k == 1)
                last.then_inc(s_q[Q_W2], 1)

            def back(self, pe, mm, i):
                for n, j in enumerate(range(*LOTS[i])):
                    last = nc.tensor.transpose(TS_BANKS[i][0:CC, D * n:D * n + D], sT[:, j, :], cst[:, C_ID:C_ID + D])
                last.then_inc(s_q[Q_TS], 1)

            def aggregate2(self, pe, mm, i):
                pe.wait_ge(s_bias, 32)
                pe.wait_ge(s_q[Q_SS], i + 1)
                for n, j in enumerate(range(*LOTS[i])):
                    last = mm(AGG2_BANKS[i][0:CC, D * n:D * n + D], ac[:, j, :], ss[:, j, :])
                last.then_inc(s_q[Q_AGG2], 1)

            def residual(self, pe, mm, i):
                mm(SC_BANKS[i][0:64, 0:D * lot_size(i)], cst[0:64, C_ID:C_ID + 64], x1[:, lot(i), :], True, False)

            def scatter(self, pe, mm, i):
                pe.wait_ge(s_q[Q_O2], i + 1)
                first = i in EARLY
                mm(SC_BANKS[i][0:64, 0:D * lot_size(i)], cst[0:CC, C_SELT:C_SELT + 64], o2[:, lot(i), :], first, True).then_inc(s_q[Q_SC], 1)

        class GroupsAct:
            def combined(self, act):
                for h in range(2):
                    act.wait_ge(s_q[Q_MSEL], h + 1)
                    nc.scalar.activation(msel[:, pairs(h), :], banked(MSEL_BANKS[h], 64, CC), ACT.Copy).then_inc(s_q[Q_MS], 1)

            def channels(self, act, i):
                act.wait_ge(s_q[Q_TR], i + 1)
                nc.scalar.activation(agT[:, lot(i), :], banked(TR_BANKS[i], 128, CC, lot_size(i)), ACT.Copy).then_inc(s_q[Q_AGT], 1)

            def hidden(self, act, g):
                act.wait_ge(s_q[Q_W1], 2 * g + 1)
                nc.scalar.activation(hT0[:, ERL, group(g)], cols(W1_BANKS[(2 * g) % 4], g), ACT.Relu,
                                     bias=gb1[:, g, 0:1]).then_inc(s_q[Q_H0], 1)

            def hidden_late(self, act):
                act.wait_ge(s_hz, 1)
                act.wait_ge(s_q[Q_W1], 2 * NG + 1)
                for g in range(NG):
                    last = nc.scalar.activation(hz[:, 0, g, group(g)], W1_LATE[0][:, group(g)], ACT.Relu, bias=gb1[:, g, 0:1])
                last.then_inc(s_q[Q_H0], 1)

            def support(self, act, g):
                act.wait_ge(s_q[Q_W2], g + 1)
                nc.scalar.activation(sT[:, ERL, group(g)], cols(W2_BANKS[g % 3], g), ACT.Copy).then_inc(s_q[Q_S], 1)

            def rows_early(self, act, i):
                act.wait_ge(s_q[Q_TS], i + 1)
                nc.scalar.activation(ss[0:CC, lot(i), :], banked(TS_BANKS[i], CC, D, lot_size(i)), ACT.Copy).then_inc(s_q[Q_SS], 1)

            def rows_late(self, act):
                act.wait_ge(s_q[Q_W2], NG + 1)
                nc.scalar.activation(ss[0:CC, PAIRS - 1, :], W2_LATE[0:CC, 0:D], ACT.Copy).then_inc(s_q[Q_SS], 1)

            def weigh(self, act, i):
                act.wait_ge(s_wcol, 3)
                act.wait_ge(s_q[Q_AGG2], i + 1)
                nc.scalar.activation(o2[:, lot(i), :], banked(AGG2_BANKS[i], CC, D, lot_size(i)), ACT.Relu,
                                     scale=wcol[:, 0:1]).then_inc(s_q[Q_O2], 1)

        def residual_sum(j):
            return SC_BANKS[2][0:64, 0:D] if j == PAIRS - 1 else yfin[:, j, :]

        def groups_power(pool, e):
            js = slice(*SPAN[e])
            pool.wait_ge(s_gmv, e + 1)
            nc.gpsimd.tensor_scalar(gbase[:, js], gmv[:, js, 1], 1.0, EPS, ALU.mult, ALU.add).then_inc(s_gbase, 1)
            pool.wait_ge(s_gbase, e + 1)
            nc.gpsimd.tensor_tensor(grs[:, js], gbase[:, js], cst[0:64, C_MH:C_MH + js.stop - js.start], ALU.pow).then_inc(s_grs, 1)

        class GroupsDVE:
            def prepare(self, dve):
                TT, TS = nc.vector.tensor_tensor, nc.vector.tensor_scalar
                dve.wait_ge(s_fe, 1)
                nc.vector.tensor_tensor_reduce(out=fw[:], in0=fe[:], in1=cst[0:CC, C_G5:C_G5 + NG], scale=1.0, scalar=0.0,
                                               op0=ALU.mult, op1=ALU.add, accum_out=fs[:, 3:4]).then_inc(s_wcol, 1)
                nc.vector.reciprocal(fs[:, 0:1], fs[:, 2:3]).then_inc(s_wcol, 1)
                dve.wait_ge(s_wcol, 2)
                TT(wcol[:], fs[:, 3:4], fs[:, 0:1], ALU.mult).then_inc(s_wcol, 1)

            def columns(self, dve):
                for h in range(2):
                    dve.wait_ge(s_q[Q_BC], h + 1)
                    nc.vector.tensor_tensor(ac[0:CC, pairs(h), :], ac[0:CC, pairs(h), :], banked(BC_BANKS[h], CC, CC), ALU.mult).then_inc(s_q[Q_AC], 1)

            def hidden(self, dve, g):
                dve.wait_ge(s_q[Q_W1], 2 * g + 2)
                nc.vector.tensor_scalar(hT1[:, ERL, group(g)], cols(W1_BANKS[(2 * g + 1) % 4], g), gb1[:, g, 1:2], 0.0,
                                        ALU.add, ALU.max).then_inc(s_q[Q_H1], 1)

            def hidden_late(self, dve):
                dve.wait_ge(s_hz, 1)
                dve.wait_ge(s_q[Q_W1], 2 * NG + 2)
                for g in range(NG):
                    last = nc.vector.tensor_scalar(hz[:, 1, g, group(g)], W1_LATE[1][:, group(g)], gb1[:, g, 1:2], 0.0,
                                                   ALU.add, ALU.max)
                last.then_inc(s_q[Q_H1], 1)

            def sums(self, dve, i):
                dve.wait_ge(s_q[Q_SC], i + 1)
                if i in EARLY:
                    nc.vector.tensor_tensor(yfin[:, lot(i), :], banked(SC_BANKS[i], 64, D, lot_size(i)), x1[:, lot(i), :], ALU.add).then_inc(s_zz, 1)
                    dve.wait_ge(s_zz, i + 1)
                for j in range(*LOTS[i]):
                    last = nc.vector.bn_stats(gst[:, j, :], residual_sum(j))
                last.then_inc(s_gst, 1)

            def moments(self, dve, e):
                dve.wait_ge(s_gst, (2, 3)[e])
                for j in range(*SPAN[e]):
                    last = nc.vector.bn_aggr(gmv[:, j, :], gst[:, j, :])
                last.then_inc(s_gmv, 1)

            def normalise(self, dve, i):
                e = int(i in LATE)
                dve.wait_ge(s_gmv, e + 1); dve.wait_ge(s_grs, e + 1)
                for j in range(*LOTS[i]):
                    last = nc.vector.tensor_scalar(yfin[:, j, :], residual_sum(j), gmv[:, j, 0:1], grs[:, j:j + 1], ALU.subtract, ALU.mult)
                last.then_inc(s_q[Q_FIN], 1)

        g_pe, g_act, g_dve = GroupsPE(), GroupsAct(), GroupsDVE()

        block = ctx.enter_context(nc.Block())

        def after(eng, semaphore, n):
            if not isinstance(n, int) or n > 0:
                eng.wait_ge(semaphore, n)

        def batches(eng, step):
            step(0, 0, lambda k: k)
            step(1, 1, lambda k: 1 + k)
            with eng.Fori(1, PAIRS - 1) as i:
                for p in range(2):
                    known = {}

                    def count(k, p=p, known=known):
                        if k not in known:
                            known[k] = eng.snap(i * 2 + (p + k))
                        return known[k]
                    step(count(0), p, count)
            step(B - 2, 0, lambda k: B - 2 + k)
            step(B - 1, 1, lambda k: B - 1 + k)

        def dma_count(n, p, k):
            v = n(k)
            if isinstance(v, int):
                return 16 * (v // 2 + 1)
            return (v - p) * 8 + 16

        def static(b, value):
            return isinstance(b, int) and b == value

        S_ROWS, S_C1, S_MSG, S_T, S_NMP, S_D0 = 0, 1, 2, 3, 4, 5

        def bank(p, k):
            return ring[(9 * p + k) % 2]

        GATE = {"r": 0, "z": 1, "n": 2}

        @block.sync
        def _(sp):
            sp.dma_start(xin[0][:], xT[0, :, :]).then_inc(s_x[0], 16)
            sp.dma_start(wc1[:], w_c1[:, :]).then_inc(s_wc1d, 16)
            sp.dma_start(vec[:], vecs[:, :]).then_inc(s_vec, 16)
            sp.dma_start(cst[:], consts[:, :]).then_inc(s_cst, 16)
            sp.dma_start(wrow[:], w_rows[:, :]).then_inc(s_wrowd, 16)
            sp.dma_start(wc2[:, 1::2, :], w_c2[:, 1::2, :]).then_inc(s_w2od, 16)
            sp.dma_start(brow[:], b_rows[:, :]).then_inc(s_brow, 16)
            sp.dma_start(wmsg[:], w_msg[:, :]).then_inc(s_wmsgd, 16)
            sp.dma_start(wc2[:, 0::2, :], w_c2[:, 0::2, :]).then_inc(s_w2ed, 16)
            sp.dma_start(bmsg[:], b_msg[:, :].to_broadcast([128, D])).then_inc(s_bmsg, 16)
            sp.dma_start(adj[0][:], adjT[0, :, :].rearrange("(c p) n -> p c n", p=128)).then_inc(s_adj[0], 16)
            sp.dma_start(wg[:, 0:2, :], w_ih[:, :, :]).then_inc(s_wgd, 16)
            sp.dma_start(wg[:, 2, :], w_hh[:, :]).then_inc(s_wgd, 16)
            sp.dma_start(xin[1][:], xT[1, :, :]).then_inc(s_x[1], 16)
            sp.wait_ge(s_zero, 4)
            for q in range(2):
                sp.dma_start(bd[SLOT * q:SLOT * q + GN, :, SLOT * q:SLOT * q + GN],
                             adjT[q::2, 0:GN, 0:GN].rearrange("j m n -> m j n")).then_inc(s_bdd, 16)
            sp.dma_start(fw[:], g_fw[:, :].to_broadcast([CC, NG])).then_inc(s_gd, 16)
            sp.dma_start(gb1[:], g_b1[:, :, :]).then_inc(s_gd, 16)
            sp.dma_start(gw1[:], g_w1.rearrange("g p h -> p g h")).then_inc(s_gd, 16)
            sp.dma_start(gw2[:], g_w2.rearrange("g (h p) o -> p g h o", p=128)).then_inc(s_gd, 16)

            sp.dma_start(adj[1][:], adjT[1, :, :].rearrange("(c p) n -> p c n", p=128)).then_inc(s_adj[1], 16)

            def step(b, p, n):
                if not (static(b, B - 2) or static(b, B - 1)):
                    after(sp, s_xl, n(1)); after(sp, s_xh, n(1)); after(sp, s_xk, n(1)); after(sp, s_msg, n(1))
                    sp.dma_start(xin[p][:], xT[b + 2, :, :]).then_inc(s_x[p], 16)
                    if static(b, 0):
                        sp.wait_ge(s_am[0], 1); sp.wait_ge(s_am[1], 1); sp.wait_ge(s_am[2], 1)
                    after(sp, s_am[CH - 1], n(1))
                    sp.dma_start(adj[p][:], adjT[b + 2, :, :].rearrange("(c p) n -> p c n", p=128)).then_inc(s_adj[p], 16)
                if not static(b, 0):
                    store(b - 1, 1 - p, n(0))

            def store(b, p, count):
                after(sp, s_yo, count)
                sp.dma_start(out[b, :, :].rearrange("(c p) d -> p c d", p=128), yo[p][:]).then_inc(s_out[p], 16)

            batches(sp, step)
            sp.wait_ge(s_q[Q_MSEL], 2); sp.wait_ge(s_aml, B)
            sp.dma_start(ac[CC:CC + NG, :, :], consts[0:NG, C_G5T:C_G5T + CC].unsqueeze(1).broadcast_to([NG, PAIRS, CC])).then_inc(s_bias, 16)
            sp.dma_start(ss[CC:CC + NG, :, :], g_b2.unsqueeze(1).broadcast_to([NG, PAIRS, D])).then_inc(s_bias, 16)
            store(B - 1, 1, B)
            for e in range(2):
                for p in range(2):
                    sp.wait_ge(s_out[p], 16 * SPAN[e][1])
                sp.wait_ge(s_q[Q_FIN], e + 2)
                j0, j1 = SPAN[e]
                for q in range(2):
                    sp.dma_start(out[2 * j0 + q:2 * j1:2, 0:GN, :].rearrange("j n d -> n j d"),
                                 yfin[SLOT * q:SLOT * q + GN, j0:j1, :]).then_inc(s_fin, 16)
            sp.wait_ge(s_fin, 64)

        @block.tensor
        def _(pe):
            def mm(out_, w, x, start=True, stop=True):
                return nc.tensor.matmul(out_, w, x, start=start, stop=stop, skip_group_check=True)

            def mm3(out_, w_h, w_l, v_h, v_l, start=True, stop=True):
                mm(out_, w_h, v_h, start, False)
                mm(out_, w_h, v_l, False, False)
                return mm(out_, w_l, v_h, False, stop)

            def rows(p, n, k):
                after(pe, s_xh, n(k + 1)); after(pe, s_xl, n(k + 1))
                mm3(bank(1 - p, S_ROWS)[:], wrow_h[:], wrow_l[:], x_h[p][:], x_l[p][:]).then_inc(s_rows, 1)

            def conv1(p, n, k):
                mm3(bank(1 - p, S_C1)[:], wc1_h[:], wc1_l[:], x_h[p][:], x_l[p][:]).then_inc(s_c1, 1)

            def msg(p, n, k):
                for c in range(CH):
                    last = mm(bank(1 - p, S_MSG)[:, D * c:D * c + D], xin[p][:, D * c:D * c + D], wmsg[:])
                last.then_inc(s_msg, 1)

            def dist(p, c):
                mm(bank(1 - p, S_D0 + c)[:], left[:, D * c:D * c + D], right[:]).then_inc(s_d[c], 1)

            pe.wait_ge(s_xh, 1); pe.wait_ge(s_xl, 1); pe.wait_ge(s_w1s, 2)
            conv1(0, None, 0)
            pe.wait_ge(s_w1s, 4)
            rows(0, lambda k: k, 0)
            pe.wait_ge(s_u, 1); pe.wait_ge(s_wmsgd, 16)
            msg(0, None, 0)

            def conv_part(out_, w_h, w_l, phase, taps, p):
                for a in range(taps):
                    last = mm3(out_, w_h[:, a, :], w_l[:, a, :], ph_h[p][:, phase, a:a + HALF],
                               ph_l[p][:, phase, a:a + HALF], a == 0, a == taps - 1)
                return last

            def gate(out_, name, source, v_h, v_l, start, stop):
                cols = slice(D * GATE[name], D * GATE[name] + D)
                return mm3(out_[:], wg_h[:, source, cols], wg_l[:, source, cols], v_h[:], v_l[:], start, stop)

            def transposes(p, q):
                for c in range(CH):
                    last = nc.tensor.transpose(bank(p, S_T)[:, D * c:D * c + D], y2[:, D * c:D * c + D], cst[:, C_ID:C_ID + D])
                last.then_inc(s_t, 1)

            def adjacency(stage):
                sel = cst[0:64, C_SEL:C_SEL + CC]
                if stage == 0:
                    pe.wait_ge(s_bdi, 1)
                    for h in range(2):
                        for j in range(HP):
                            last = mm((p_r, p_z)[h][0:64, CC * j:CC * j + CC], bd[:, HP * h + j, :], sel)
                        last.then_inc(s_sel1m, 1)
                elif stage == 1:
                    for h in range(2):
                        pe.wait_ge(s_sel1, h + 1)
                        for j in range(HP):
                            last = mm((p_gi, p_gh)[h][0:CC, CC * j:CC * j + CC], sel1[:, HP * h + j, :], sel)
                        last.then_inc(s_acm, 1)
                else:
                    pe.wait_ge(s_ac, 2)
                    for j in range(PAIRS):
                        last = mm(p_a[0:CC, j:j + 1], ac[0:CC, j, :], cst[0:CC, C_ONE:C_ONE + 1])
                    last.then_inc(s_deg, 1)

            def step(b, p, n):
                q = 1 - p
                more = not static(b, B - 1)

                def all_taps():
                    after(pe, s_ca, n(0))
                    if static(b, 1):
                        pe.wait_ge(s_dg, 1)
                    if static(b, 0):
                        pe.wait_ge(s_wohi, 3); pe.wait_ge(s_wolo, 3)
                    conv_part(p_a[:, 0:HALF], ws_h, ws_l, 0, NE, p).then_inc(s_a, 1)

                after(pe, s_phh, n(1)); after(pe, s_phl, n(1))
                after(pe, s_cu, n(0))
                if static(b, 0):
                    pe.wait_ge(s_wohi, 1); pe.wait_ge(s_wolo, 1)
                conv_part(p_bc[:, HALF:N], wo_h, wo_l, 2, NO, p)
                if static(b, 0):
                    pe.wait_ge(s_left, 1); pe.wait_ge(s_right, 1); pe.wait_ge(s_h1, 1)
                    dist(0, 0)
                    pe.wait_ge(s_mt, 1)
                    dist(0, 1)
                    pe.wait_ge(s_e[0], 1)
                    dist(0, 2)
                    pe.wait_ge(s_e[1], 1)
                    dist(0, 3)
                if static(b, B - 1):
                    pe.wait_ge(s_rt, B - 1); pe.wait_ge(s_zt, B - 1)
                    g_pe.spread(pe, mm)
                if more and not static(b, 0):
                    after(pe, s_e[2], n(1))
                    rows(q, n, 1)
                if static(b, 0):
                    pe.wait_ge(s_wohi, 2); pe.wait_ge(s_wolo, 2)
                conv_part(p_bc[:, 0:HALF], we_h, we_l, 1, NE, p).then_inc(s_bc, 1)
                if static(b, 0):
                    all_taps()
                    pe.wait_ge(s_e[2], 1)
                    rows(q, n, 1)
                    adjacency(0)
                if static(b, B - 1):
                    pe.wait_ge(s_gg, B - 1); pe.wait_ge(s_tt, B - 1)
                    g_pe.combine(pe, mm)
                if more:
                    after(pe, s_e[3], n(1))
                    conv1(q, n, 1)
                    after(pe, s_u, n(2))
                    msg(q, n, 1)
                if not static(b, 0):
                    after(pe, s_y2, n(0))
                    if more:
                        after(pe, s_h1, n(2))
                    else:
                        after(pe, s_e[3], n(1))
                    transposes(p, q)
                if static(b, 0):
                    adjacency(1)
                else:
                    all_taps()
                if static(b, B - 1):
                    pe.wait_ge(s_q[Q_MS], 2)
                    pe.wait_ge(s_grow, B - 2)
                    for i in EARLY:
                        g_pe.aggregate(pe, mm, i)
                after(pe, s_amh, n(1)); after(pe, s_aml, n(1)); after(pe, s_mh, n(1)); after(pe, s_ml, n(1))
                if more:
                    after(pe, s_mt, n(2))
                else:
                    after(pe, s_e[2], n(1))
                for c in range(CH):
                    cols = slice(D * c, D * c + D)
                    last = mm3(bank(p, S_NMP)[:], m_h[p][:, cols], m_l[p][:, cols], am_h[:, c, :], am_l[:, c, :],
                               c == 0, c == CH - 1)
                last.then_inc(s_nmp, 1)
                if more:
                    after(pe, s_left, n(2)); after(pe, s_right, n(2))
                    if static(b, 0):
                        after(pe, s_h1, n(2))
                    after(pe, s_yn, n(0))
                    dist(q, 0)
                if static(b, 0):
                    pe.wait_ge(s_wgs, 2)
                if static(b, B - 1):
                    pe.wait_ge(s_q[Q_AGT], 2)
                after(pe, s_rt, n(0)); gate(p_r, "r", 2, x_h[p], x_l[p], True, False)
                after(pe, s_zt, n(0)); gate(p_z, "z", 2, x_h[p], x_l[p], True, False)
                if static(b, 0):
                    pe.wait_ge(s_ac, 2)
                after(pe, s_gg, n(0)); gate(p_gh, "n", 2, x_h[p], x_l[p], True, True).then_inc(s_gx, 1)
                after(pe, s_nh, n(1)); after(pe, s_nl, n(1))
                if more:
                    dist(q, 1)
                gate(p_r, "r", 1, n_h, n_l, False, False)
                if static(b, 0):
                    pe.wait_ge(s_ca, 1)
                    adjacency(2)
                if more:
                    after(pe, s_e[0], n(2))
                    dist(q, 2)
                gate(p_z, "z", 1, n_h, n_l, False, False)
                after(pe, s_tt, n(0)); gate(p_gi, "n", 1, n_h, n_l, True, False).then_inc(s_gn, 1)
                if more:
                    after(pe, s_e[1], n(2))
                    dist(q, 3)
                after(pe, s_ch, n(1)); after(pe, s_cl, n(1))
                gate(p_r, "r", 0, c_h, c_l, False, True).then_inc(s_gr, 1)
                gate(p_gi, "n", 0, c_h, c_l, False, True).then_inc(s_gi, 1)
                gate(p_z, "z", 0, c_h, c_l, False, True).then_inc(s_gz, 1)

            batches(pe, step)
            pe.wait_ge(s_cu, B); pe.wait_ge(s_ca, B); pe.wait_ge(s_nl, B); pe.wait_ge(s_gg, B)
            g_pe.first_early(pe, mm)
            pe.wait_ge(s_y2, B)
            transposes(1, 0)
            pe.wait_ge(s_rt, B); pe.wait_ge(s_zt, B); pe.wait_ge(s_tt, B)
            g_pe.second_early(pe, mm)
            pe.wait_ge(s_q[Q_S], NG)
            for i in EARLY:
                g_pe.back(pe, mm, i)
            g_pe.aggregate2(pe, mm, 0)
            pe.wait_ge(s_grow, B)
            g_pe.aggregate(pe, mm, 2)
            g_pe.aggregate2(pe, mm, 1)
            pe.wait_ge(s_yn, B)
            g_pe.scatter(pe, mm, 0)
            g_pe.first_late(pe, mm)
            g_pe.scatter(pe, mm, 1)
            g_pe.second_late(pe, mm)
            g_pe.residual(pe, mm, 2)
            g_pe.aggregate2(pe, mm, 2)
            g_pe.scatter(pe, mm, 2)

        @block.scalar
        def _(act):
            A = nc.scalar.activation

            def rows_u(p, n, k):
                after(act, s_rows, n(k + 1)); after(act, s_val, n(k))
                A(u, bank(1 - p, S_ROWS)[0:64, :], ACT.Identity, bias=brow[:, 0:1]).then_inc(s_u, 1)
                after(act, s_u, n(k + 1))
                A(ab, u, ACT.Identity, bias=cst[0:64, C_ROW + 1:C_ROW + 2], scale=cst[0:64, C_ROW:C_ROW + 1]).then_inc(s_ab, 1)

            def first_conv(p, n, k):
                after(act, s_c1, n(k + 1)); after(act, s_phd, n(k)); after(act, s_pho, n(k))
                A(h1[:, PAD:PAD + N], bank(1 - p, S_C1)[:], ACT.Relu, bias=prm[:, P_A1:P_A1 + 1],
                  scale=prm[:, P_S1:P_S1 + 1]).then_inc(s_h1, 1)
                after(act, s_h1, n(k + 1)); after(act, s_phl, n(k)); after(act, s_phh, n(k))
                A(ph[:, 0, :], h1[:, 1::2], ACT.Copy).then_inc(s_pho, 1)

            def keep_x(p, n, k):
                after(act, s_ya, n(k - 1)); after(act, s_cu, n(k - 1))
                A(xkeep[p][:], xin[p][:], ACT.Copy).then_inc(s_xk, 1)

            def msg_high(p, n, k):
                after(act, s_mt, n(k + 1)); after(act, s_nmp, n(k - 1))
                A(m_h[p][:], mt[:], ACT.Relu).then_inc(s_mh, 1)

            def exps(p, n, k, c):
                after(act, s_d[c], n(k + 1)); after(act, s_amh, n(k)); after(act, s_aml, n(k))
                A(am[:, c, :], bank(1 - p, S_D0 + c)[:], ACT.Exp).then_inc(s_e[c], 1)

            act.wait_ge(s_w2od, 16)
            A(wo_h[:], wc2[:, 1::2, :], ACT.Copy).then_inc(s_wohi, 1)
            z = lambda k: k
            act.wait_ge(s_zero, 4); act.wait_ge(s_prm, 5)
            first_conv(0, z, 0)
            act.wait_ge(s_brow, 16); act.wait_ge(s_cst, 16)
            rows_u(0, z, 0)
            act.wait_ge(s_w2ed, 16)
            A(we_h[:], wc2[:, 0::2, :], ACT.Copy).then_inc(s_wohi, 1)
            msg_high(0, z, 0)
            act.wait_ge(s_x[0], 16)
            keep_x(0, z, 0)
            for c in range(CH):
                exps(0, z, 0, c)
            act.wait_ge(s_wsum, 2)
            A(ws_h[:], wsum, ACT.Copy).then_inc(s_wohi, 1)

            def node_rows(p, n, k):
                after(act, s_t, n(k + 1)); after(act, s_yo, n(k))
                A(yn[:].rearrange("p c d -> p (c d)"), bank(p, S_T)[:], ACT.Copy).then_inc(s_yn, 1)

            def candidate(n, k):
                after(act, s_tt, n(k + 1)); after(act, s_yb, n(k))
                A(nn[:], tt[:], ACT.Tanh, bias=vec[:, V_IN:V_IN + 1]).then_inc(s_nn, 1)

            def step(b, p, n):
                q = 1 - p
                more = not static(b, B - 1)
                if not static(b, 0):
                    candidate(n, -1)
                for c in range(CH):
                    after(act, s_am[c], n(1))
                after(act, s_nmp, n(0))
                A(am_h[:], am[:], ACT.Copy).then_inc(s_amh, 1)
                if static(b, 0):
                    act.wait_ge(s_wgd, 32)
                    A(wg_h[:], wg[:], ACT.Copy).then_inc(s_wgs, 1)
                    rows_u(q, n, 1)
                    act.wait_ge(s_wolo, 2); act.wait_ge(s_wsum, 2)
                    for h in range(2):
                        act.wait_ge(s_sel1m, h + 1)
                        A(sel1[:, pairs(h), :], banked((p_r, p_z)[h], 64, CC), ACT.Copy).then_inc(s_sel1, 1)
                if more and not static(b, 0):
                    rows_u(q, n, 1)
                if more:
                    first_conv(q, n, 1)
                    after(act, s_x[q], dma_count(n, q, 1))
                    keep_x(q, n, 1)
                if static(b, B - 1):
                    g_act.combined(act)
                if not static(b, 0):
                    node_rows(p, n, -1)
                if more:
                    msg_high(q, n, 1)
                after(act, s_a, n(1)); after(act, s_cv, n(0))
                A(ca[:], p_a[:, 0:HALF], ACT.Identity, bias=prm[:, P_A2:P_A2 + 1], scale=prm[:, P_S2:P_S2 + 1]).then_inc(s_ca, 1)
                if static(b, B - 1):
                    for i in EARLY:
                        g_act.channels(act, i)
                after(act, s_nmp, n(1)); after(act, s_gn, n(0))
                A(n_h[:], bank(p, S_NMP)[:], ACT.Copy).then_inc(s_nh, 1)
                if more:
                    exps(q, n, 1, 0)
                after(act, s_cv, n(1)); after(act, s_gz, n(0))
                A(c_h[:], cv[:], ACT.Relu).then_inc(s_ch, 1)
                if more:
                    for c in range(1, CH):
                        exps(q, n, 1, c)
                if static(b, 0):
                    act.wait_ge(s_fw, 2)
                    A(fe[:], fw[:], ACT.Exp, bias=fs[:, 1:2], accum_out=fs[:, 2:3]).then_inc(s_fe, 1)
                after(act, s_gr, n(1)); after(act, s_gg, n(0))
                A(rt[:], p_r[:], ACT.Tanh, bias=prm[:, P_RH:P_RH + 1], scale=0.5).then_inc(s_rt, 1)
                after(act, s_gz, n(1)); after(act, s_yb, n(0)); after(act, s_ya, n(0))
                A(zt[:], p_z[:], ACT.Tanh, bias=prm[:, P_ZH:P_ZH + 1], scale=0.5).then_inc(s_zt, 1)

            batches(act, step)
            candidate(lambda k: B + k, -1)
            for g in range(NG):
                g_act.hidden(act, g)
            node_rows(1, lambda k: B + k, -1)
            for g in range(NG):
                g_act.support(act, g)
            for i in EARLY:
                g_act.rows_early(act, i)
            g_act.weigh(act, 0)
            g_act.channels(act, 2)
            g_act.weigh(act, 1)
            g_act.hidden_late(act)
            g_act.rows_late(act)
            g_act.weigh(act, 2)

        @block.gpsimd
        def _(pool):
            TT, TS = nc.gpsimd.tensor_tensor, nc.gpsimd.tensor_scalar
            nc.gpsimd.memset(bd[:], 0.0).then_inc(s_zero, 1)
            nc.gpsimd.memset(x1[:], 0.0).then_inc(s_zero, 1)
            nc.gpsimd.memset(h1[:, 0:PAD], 0.0).then_inc(s_zero, 1)
            nc.gpsimd.memset(h1[:, PAD + N:], 0.0).then_inc(s_zero, 1)
            pool.wait_ge(s_prm, 2)
            pool.wait_ge(s_cst, 16)
            TT(prm[:, P_RS:P_RS + 2], prm[:, P_VE:P_VE + 2], cst[:, C_MH:C_MH + 2], ALU.pow).then_inc(s_pow, 1)

            def rows_val(n, k):
                after(pool, s_u, n(k + 1)); after(pool, s_ab, n(k + 1)); after(pool, s_valh, n(k))
                after(pool, s_left, n(k)); after(pool, s_right, n(k))
                TT(val[:], u, ab, ALU.mult).then_inc(s_val, 1)

            def mask(p, n, k, c):
                if c == 0:
                    after(pool, s_adj[p], dma_count(n, p, k))
                after(pool, s_e[c], n(k + 1))
                TT(am[:, c, :], am[:, c, :], adj[p][:, c, :], ALU.mult).then_inc(s_am[c], 1)

            def powers(n, k):
                after(pool, s_base, n(k + 1))
                after(pool, s_yo, n(k))
                TT(rs[:], base[:], cst[:, C_MH:C_MH + CH + 1], ALU.pow).then_inc(s_rs, 1)

            rows_val(lambda k: k, 0)
            pool.wait_ge(s_w2od, 16); pool.wait_ge(s_w2ed, 16)
            TT(wsum[:, 0:NO, :], wc2[:, 0:2 * NO:2, :], wc2[:, 1:2 * NO:2, :], ALU.add).then_inc(s_wsum, 1)
            nc.gpsimd.tensor_copy(wsum[:, NO:NE, :], wc2[:, TAPS - 1:TAPS, :]).then_inc(s_wsum, 1)
            pool.wait_ge(s_adj[0], 16)
            for c in range(CH // 2, CH):
                mask(0, lambda k: k, 0, c)

            def step(b, p, n):
                q = 1 - p
                more = not static(b, B - 1)
                if more:
                    rows_val(n, 1)
                if static(b, B - 2):
                    TS(dg[:, 0, :], dg[:, 1, :], -1.0, 1.0, ALU.mult, ALU.add).then_inc(s_dinv, 1)
                    pool.wait_ge(s_dinv, 1); pool.wait_ge(s_dpow, 1)
                    TT(dinv[:], dg[:, 3, :], dg[:, 0, :], ALU.mult).then_inc(s_dinv, 1)
                    pool.wait_ge(s_dinv, 2)
                    TT(diag[:], cst[0:CC, C_ID:C_ID + CC].unsqueeze(1).broadcast_to([CC, PAIRS, CC]),
                       dinv[:].unsqueeze(2).broadcast_to([CC, PAIRS, CC]), ALU.mult).then_inc(s_diag, 1)
                    TT(ac[0:CC, :, :], ac[0:CC, :, :], dinv[:].unsqueeze(2).broadcast_to([CC, PAIRS, CC]), ALU.mult).then_inc(s_diag, 1)
                if static(b, B - 1):
                    nc.gpsimd.memset(hz[:], 0.0).then_inc(s_hz, 1)
                if not static(b, 0):
                    powers(n, -1)
                if static(b, 1):
                    pool.wait_ge(s_dg, 3)
                    TT(dg[:, 3, :], dg[:, 2, :], cst[0:CC, C_MH:C_MH + PAIRS], ALU.pow).then_inc(s_dpow, 1)
                if more:
                    for c in range(CH):
                        mask(q, n, 1, c)

            batches(pool, step)
            powers(lambda k: B + k, -1)
            for e in range(2):
                groups_power(pool, e)

        @block.vector
        def _(dve):
            TT, TS, STT, CP = nc.vector.tensor_tensor, nc.vector.tensor_scalar, nc.vector.scalar_tensor_tensor, nc.vector.tensor_copy

            dve.wait_ge(s_vec, 16)
            TS(prm[:, P_VE:P_VE + 1], vec[:, V_V1:V_V1 + 1], EPS, None, ALU.add).then_inc(s_prm, 1)
            TS(prm[:, P_VE + 1:P_VE + 2], vec[:, V_V2:V_V2 + 1], EPS, None, ALU.add).then_inc(s_prm, 1)

            def split_x(p, n, k):
                after(dve, s_x[p], dma_count(n, p, k)); after(dve, s_gx, n(k - 1))
                CP(x_h[p][:], xin[p][:]).then_inc(s_xh, 1)
                after(dve, s_xh, n(k + 1))
                TT(x_l[p][:], xin[p][:], full(x_h[p][:]), ALU.subtract).then_inc(s_xl, 1)

            split_x(0, lambda k: k, 0)
            dve.wait_ge(s_wc1d, 16)
            CP(wc1_h[:], wc1[:]).then_inc(s_w1s, 1)
            dve.wait_ge(s_w1s, 1)
            TT(wc1_l[:], wc1[:], full(wc1_h[:]), ALU.subtract).then_inc(s_w1s, 1)
            dve.wait_ge(s_wrowd, 16)
            CP(wrow_h[:], wrow[:]).then_inc(s_w1s, 1)
            dve.wait_ge(s_w1s, 3)
            TT(wrow_l[:], wrow[:], full(wrow_h[:]), ALU.subtract).then_inc(s_w1s, 1)
            dve.wait_ge(s_pow, 1)
            TT(prm[:, P_S1:P_S1 + 1], vec[:, V_G1:V_G1 + 1], prm[:, P_RS:P_RS + 1], ALU.mult)
            TT(prm[:, P_S2:P_S2 + 1], vec[:, V_G2:V_G2 + 1], prm[:, P_RS + 1:P_RS + 2], ALU.mult)
            TT(prm[:, P_R:P_R + 2], vec[:, V_IR:V_IR + 2], vec[:, V_HR:V_HR + 2], ALU.add).then_inc(s_prm, 1)
            dve.wait_ge(s_prm, 3)
            TS(prm[:, P_RH:P_RH + 2], prm[:, P_R:P_R + 2], 0.5, None, ALU.mult)
            TT(prm[:, P_T1:P_T1 + 1], vec[:, V_M1:V_M1 + 1], prm[:, P_S1:P_S1 + 1], ALU.mult)
            TT(prm[:, P_T2:P_T2 + 1], vec[:, V_M2:V_M2 + 1], prm[:, P_S2:P_S2 + 1], ALU.mult).then_inc(s_prm, 1)
            dve.wait_ge(s_prm, 4)
            TT(prm[:, P_A1:P_A1 + 1], vec[:, V_B1:V_B1 + 1], prm[:, P_T1:P_T1 + 1], ALU.subtract)
            TT(prm[:, P_A2:P_A2 + 1], vec[:, V_B2:V_B2 + 1], prm[:, P_T2:P_T2 + 1], ALU.subtract).then_inc(s_prm, 1)

            def left_right(n, k):
                after(dve, s_val, n(k + 1))
                CP(val_h[:], val[:]).then_inc(s_valh, 1)
                after(dve, s_valh, n(k + 1)); after(dve, s_d[CH - 1], n(k))
                STT(left[:], full(val_h[0:KD, :]), cst[0:KD, C_ROW + 2:C_ROW + 3], val[0:KD, :], ALU.mult, ALU.add).then_inc(s_left, 1)
                STT(right[:], full(val_h[32:32 + KD, :]), cst[32:32 + KD, C_ROW + 2:C_ROW + 3], val[32:32 + KD, :],
                    ALU.mult, ALU.add).then_inc(s_right, 1)

            def phases(p, n, k):
                after(dve, s_h1, n(k + 1)); after(dve, s_phl, n(k))
                TT(ph[:, 1, :], h1[:, 0::2], h1[:, 1::2], ALU.subtract)
                TT(ph[:, 2, 0:PH - 1], h1[:, 2::2], h1[:, 1:N + 2 * PAD - 2:2], ALU.subtract).then_inc(s_phd, 1)
                after(dve, s_pho, n(k + 1)); after(dve, s_phd, n(k + 1)); after(dve, s_a, n(k - 1))
                CP(ph_h[p][:], ph[:]).then_inc(s_phh, 1)
                after(dve, s_phh, n(k + 1))
                TT(ph_l[p][:], ph[:], full(ph_h[p][:]), ALU.subtract).then_inc(s_phl, 1)

            def msg_sum(p, n, k):
                after(dve, s_msg, n(k + 1)); after(dve, s_mh, n(k)); after(dve, s_ml, n(k))
                TT(mt[:].rearrange("p (c d) -> p c d", c=CH), bank(1 - p, S_MSG)[:].rearrange("p (c d) -> p c d", c=CH),
                   bmsg[:].unsqueeze(1).broadcast_to([128, CH, D]), ALU.add).then_inc(s_mt, 1)

            def msg_low(p, n, k):
                after(dve, s_mh, n(k + 1)); after(dve, s_mt, n(k + 1))
                STT(m_l[p][:], mt[:], 0.0, full(m_h[p][:]), ALU.max, ALU.subtract).then_inc(s_ml, 1)

            zero = lambda k: k
            nc.vector.memset(ph[:, 2, PH - 1:PH], 0.0)
            dve.wait_ge(s_wohi, 1)
            TT(wo_l[:], wc2[:, 1::2, :], full(wo_h[:]), ALU.subtract).then_inc(s_wolo, 1)
            dve.wait_ge(s_zero, 4)
            phases(0, zero, 0)
            dve.wait_ge(s_bmsg, 16)
            msg_sum(0, zero, 0)
            left_right(zero, 0)
            dve.wait_ge(s_wohi, 2)
            TT(we_l[:], wc2[:, 0::2, :], full(we_h[:]), ALU.subtract).then_inc(s_wolo, 1)
            dve.wait_ge(s_adj[0], 16)
            for c in range(CH // 2):
                dve.wait_ge(s_e[c], 1)
                TT(am[:, c, :], am[:, c, :], adj[0][:, c, :], ALU.mult).then_inc(s_am[c], 1)
            msg_low(0, zero, 0)
            dve.wait_ge(s_wohi, 3)
            TT(ws_l[:], wsum, full(ws_h[:]), ALU.subtract).then_inc(s_wolo, 1)
            dve.wait_ge(s_bdd, 32); dve.wait_ge(s_cst, 16)
            TT(bd[:], bd[:], cst[0:64, C_ID:C_ID + 64].unsqueeze(1).broadcast_to([64, PAIRS, 64]), ALU.add).then_inc(s_bdi, 1)

            def adjacency(stage):
                if stage == 0:
                    for h in range(2):
                        dve.wait_ge(s_acm, h + 1)
                        TT(ac[0:CC, pairs(h), :], banked((p_gi, p_gh)[h], CC, CC),
                           cst[0:CC, C_SAME:C_SAME + CC].unsqueeze(1).broadcast_to([CC, HP, CC]), ALU.mult).then_inc(s_ac, 1)
                else:
                    dve.wait_ge(s_deg, 1)
                    CP(dg[:, 0, :], p_a[0:CC, 0:PAIRS]).then_inc(s_dg, 1)
                    dve.wait_ge(s_dg, 1)
                    TS(dg[:, 1, :], dg[:, 0, :], 0.0, None, ALU.is_equal).then_inc(s_dg, 1)
                    dve.wait_ge(s_dg, 2)
                    TT(dg[:, 2, :], dg[:, 0, :], dg[:, 1, :], ALU.add).then_inc(s_dg, 1)

            def gate_mid(n, k):
                after(dve, s_rt, n(k + 1)); after(dve, s_gg, n(k))
                TS(r1[:], rt[:], 0.5, 0.5, ALU.mult, ALU.add).then_inc(s_r1, 1)
                after(dve, s_r1, n(k + 1)); after(dve, s_gx, n(k + 1)); after(dve, s_tt, n(k))
                STT(gg[:], p_gh[:], vec[:, V_HN:V_HN + 1], r1[:], ALU.add, ALU.mult).then_inc(s_gg, 1)
                after(dve, s_gg, n(k + 1)); after(dve, s_gi, n(k + 1)); after(dve, s_nn, n(k))
                TT(tt[:], p_gi[:], gg[:], ALU.add).then_inc(s_tt, 1)

            def result(p, n, k, between=lambda: None):
                after(dve, s_zt, n(k + 1)); after(dve, s_xk, n(k + 1)); after(dve, s_y2, n(k))
                STT(ya, zt[:], 3.0, xkeep[p][:], ALU.add, ALU.mult).then_inc(s_ya, 1)
                between()
                after(dve, s_nn, n(k + 1))
                STT(yb, zt[:], -1.0, nn[:], ALU.add, ALU.mult).then_inc(s_yb, 1)
                after(dve, s_ya, n(k + 1)); after(dve, s_yb, n(k + 1)); after(dve, s_t, n(k))
                TT(y2, ya, yb, ALU.subtract).then_inc(s_y2, 1)

            def stats(n, k):
                after(dve, s_yn, n(k + 1)); after(dve, s_mv, n(k))
                for c in range(CH):
                    last = nc.vector.bn_stats(st[:, c, :], yn[:, c, :])
                last.then_inc(s_st, 1)
                after(dve, s_st, n(k + 1)); after(dve, s_base, n(k)); after(dve, s_yo, n(k))

            def moments(n, k):
                for c in range(CH):
                    last = nc.vector.bn_aggr(mv[:, c, :], st[:, c, :])
                last.then_inc(s_mv, 1)
                after(dve, s_mv, n(k + 1)); after(dve, s_rs, n(k))
                TS(base[:, 0:CH], mv[:, :, 1], 1.0 + EPS, 4 * EPS * EPS, ALU.mult, ALU.add)
                TS(base[:, CH:CH + 1], mv[:, 0, 1:2], 1.0, 4 * EPS, ALU.mult, ALU.add).then_inc(s_base, 1)

            def normalise(q, n, k, pair):
                after(dve, s_mv, n(k + 1)); after(dve, s_rs, n(k + 1))
                TS(x1[SLOT * q:SLOT * q + GN, pair, :], yn[0:GN, 0, :], mv[0:GN, 0, 0:1], rs[0:GN, CH:CH + 1],
                   ALU.subtract, ALU.mult).then_inc(s_grow, 1)
                if isinstance(n(k), int):
                    after(dve, s_out[q], 16 * (n(k) // 2))
                else:
                    dve.wait_ge(s_out[q], (n(k) - q) * 8)
                for c in range(CH):
                    last = TS(yo[q][:, c, :], yn[:, c, :], mv[:, c, 0:1], rs[:, c:c + 1], ALU.subtract, ALU.mult)
                last.then_inc(s_yo, 1)
            def step(b, p, n):
                q = 1 - p
                more = not static(b, B - 1)
                if more:
                    split_x(q, n, 1)
                if not static(b, 0):
                    gate_mid(n, -1)
                    result(q, n, -1)
                if static(b, B - 1):
                    g_dve.columns(dve)
                after(dve, s_amh, n(1)); after(dve, s_nmp, n(0))
                TT(am_l[:], am[:], full(am_h[:]), ALU.subtract).then_inc(s_aml, 1)
                if static(b, 0):
                    dve.wait_ge(s_wgs, 1)
                    TT(wg_l[:], wg[:], full(wg_h[:]), ALU.subtract).then_inc(s_wgs, 1)
                if more and not static(b, 0):
                    left_right(n, 1)
                if static(b, B - 1):
                    g_dve.prepare(dve)
                after(dve, s_bc, n(1)); after(dve, s_cv, n(0)); after(dve, s_xk, n(1))
                STT(cu[:].rearrange("p (k two) -> p two k", two=2), p_bc[:].rearrange("p (two k) -> p two k", two=2),
                    prm[:, P_S2:P_S2 + 1], xkeep[p][:].rearrange("p (k two) -> p two k", two=2),
                    ALU.mult, ALU.add).then_inc(s_cu, 1)
                if more:
                    msg_sum(q, n, 1)
                if static(b, 0):
                    left_right(n, 1)
                if not static(b, 0):
                    stats(n, -1)
                if more:
                    phases(q, n, 1)
                if static(b, 0):
                    adjacency(0)
                after(dve, s_nh, n(1)); after(dve, s_gn, n(0))
                TT(n_l[:], bank(p, S_NMP)[:], full(n_h[:]), ALU.subtract).then_inc(s_nl, 1)
                if not static(b, 0):
                    moments(n, -1)
                after(dve, s_ca, n(1)); after(dve, s_cu, n(1)); after(dve, s_ch, n(0)); after(dve, s_cl, n(0))
                TT(cv[:].rearrange("p (k two) -> p k two", two=2), cu[:].rearrange("p (k two) -> p k two", two=2),
                   ca[:].unsqueeze(2).broadcast_to([128, HALF, 2]), ALU.add).then_inc(s_cv, 1)
                after(dve, s_ch, n(1)); after(dve, s_cv, n(1)); after(dve, s_gz, n(0))
                STT(c_l[:], cv[:], 0.0, full(c_h[:]), ALU.max, ALU.subtract).then_inc(s_cl, 1)
                if static(b, 0):
                    adjacency(1)
                    dve.wait_ge(s_gd, 64)
                    nc.vector.reduce_max(fs[:, 0:1], fw[:], AX.X).then_inc(s_fw, 1)
                    dve.wait_ge(s_fw, 1)
                    TS(fs[:, 1:2], fs[:, 0:1], -1.0, None, ALU.mult).then_inc(s_fw, 1)
                if more:
                    msg_low(q, n, 1)
                if not static(b, 0):
                    normalise(q, n, -1, pair_of(b, p, n))

            def pair_of(b, p, n):
                if isinstance(b, int):
                    return (b - 1) // 2
                return loop_pair[0] - (1 - p)

            loop_pair = [None]
            step(0, 0, lambda k: k)
            step(1, 1, lambda k: 1 + k)
            with dve.Fori(1, PAIRS - 1) as i:
                loop_pair[0] = i
                for p in range(2):
                    known = {}

                    def count(k, p=p, known=known):
                        if k not in known:
                            known[k] = dve.snap(i * 2 + (p + k))
                        return known[k]
                    step(count(0), p, count)
            step(B - 2, 0, lambda k: B - 2 + k)
            step(B - 1, 1, lambda k: B - 1 + k)
            last = lambda k: B + k
            gate_mid(last, -1)
            result(1, last, -1, lambda: g_dve.hidden(dve, 0))
            for g in range(1, NG):
                g_dve.hidden(dve, g)
            stats(last, -1)
            moments(last, -1)
            normalise(1, last, -1, PAIRS - 1)
            g_dve.sums(dve, 0)
            g_dve.hidden_late(dve)
            g_dve.sums(dve, 1)
            g_dve.moments(dve, 0)
            g_dve.normalise(dve, 0)
            g_dve.sums(dve, 2)
            g_dve.moments(dve, 1)
            g_dve.normalise(dve, 1)
            g_dve.normalise(dve, 2)


def kernel(x, adj, L0_gnn_w_se, L0_gnn_b_se, L0_gnn_conv1_w, L0_gnn_bn1_g, L0_gnn_bn1_b, L0_gnn_bn1_m, L0_gnn_bn1_v,
           L0_gnn_conv2_w, L0_gnn_bn2_g, L0_gnn_bn2_b, L0_gnn_bn2_m, L0_gnn_bn2_v, L0_gnn_w_msg, L0_gnn_b_msg,
           L0_gnn_w_ih, L0_gnn_b_ih, L0_gnn_w_hh, L0_gnn_b_hh, L1_gnn_W1, L1_gnn_b1, L1_gnn_W2, L1_gnn_b2, L1_gnn_fusion_w):
    import concourse.bacc as bacc
    from concourse.bass_utils import run_bass_kernel_spmd

    a = lambda t: np.asarray(t)
    c = np.ascontiguousarray
    b_ih, b_hh = a(L0_gnn_b_ih).reshape(3, D), a(L0_gnn_b_hh).reshape(3, D)
    vecs = c(np.stack([a(L0_gnn_bn1_g), a(L0_gnn_bn1_b), a(L0_gnn_bn1_m), a(L0_gnn_bn1_v),
                       a(L0_gnn_bn2_g), a(L0_gnn_bn2_b), a(L0_gnn_bn2_m), a(L0_gnn_bn2_v),
                       b_ih[0], b_ih[1], b_ih[2], b_hh[0], b_hh[1], b_hh[2]], axis=1))
    w_se, b_se = a(L0_gnn_w_se), a(L0_gnn_b_se)
    w_rows, b_rows = np.zeros((D, 128), w_se.dtype), np.zeros((64, 1), b_se.dtype)
    for side, rows in enumerate(dist_rows()):
        for r, (k, _, _, _) in enumerate(rows):
            if k is None:
                b_rows[32 * side + r, 0] = 1
            else:
                w_rows[:, 32 * side + r] = w_se[k]
                b_rows[32 * side + r, 0] = b_se[k]
    arrays = {
        "xT": c(a(x).transpose(0, 2, 1)), "adjT": c(a(adj).transpose(0, 2, 1)), "consts": constants(),
        "vecs": vecs, "w_rows": w_rows, "b_rows": b_rows,
        "w_c1": c(a(L0_gnn_conv1_w)[:, :, 0].T), "w_c2": c(a(L0_gnn_conv2_w).transpose(1, 2, 0)),
        "w_ih": c(a(L0_gnn_w_ih).reshape(3 * D, 2, D).transpose(2, 1, 0)), "w_hh": c(a(L0_gnn_w_hh).T),
        "w_msg": c(a(L0_gnn_w_msg).T), "b_msg": a(L0_gnn_b_msg).reshape(1, D),
        "g_w1": a(L1_gnn_W1), "g_b1": c(a(L1_gnn_b1).reshape(NG, 2, D).transpose(2, 0, 1)),
        "g_w2": a(L1_gnn_W2), "g_b2": a(L1_gnn_b2), "g_fw": a(L1_gnn_fusion_w).reshape(1, NG),
    }
    nc = bacc.Bacc("TRN2", target_bir_lowering=False, num_devices=1)
    args = [nc.dram_tensor(name, v.shape, mybir.dt.from_np(v.dtype), kind="ExternalInput").ap() for name, v in arrays.items()]
    args.append(nc.dram_tensor("out", (B, N, D), mybir.dt.float32, kind="ExternalOutput").ap())
    gnn_kernel(nc, *args)
    result = run_bass_kernel_spmd(nc, [arrays], core_ids=[0])
    return result.results[0]["out"]
```

```python
import numpy as np
import concourse.bass as bass
from concourse import mybir
from contextlib import ExitStack

B, N, D = 16, 512, 128
TAPS = 17
PAD = (TAPS - 1) // 2
EPS = 1e-5
GROUPS = [list(range(25)), [0, 1, 2, 3, 4, 5, 6, 7, 8], [0, 9, 10, 11, 12, 13, 14],
          [6, 7, 8, 12, 13, 14], [3, 4, 5, 9, 10, 11]]
HID = 256
GN = 25
SLOT = 32
PAIRS = B // 2
GSIZE = [2 * len(g) for g in GROUPS]
GOFF = [sum(GSIZE[:g]) for g in range(len(GROUPS))]
CC = sum(GSIZE)
NG = len(GROUPS)
CH = N // D
HALF = N // 2
G3 = (TAPS + 1) // 3
PH = HALF + PAD

KD = 24


def dist_rows():
    left, right = [], []
    for hl in ((0, 0), (0, 1), (1, 0), (1, 1)):
        for k in range(3):
            left.append((k, 0.0, 1.0, hl[0]))
            right.append((k, 0.0, 2.0, hl[1]))
    for low in (0, 1):
        for k in range(3):
            left.append((k, 1.0, 0.0, low))
            right.append((None, 0.0, -1.0, 0))
    for low in (0, 1):
        for k in range(3):
            left.append((None, 0.0, 1.0, 0))
            right.append((k, -1.0, 0.0, low))
    return left, right


(V_G1, V_B1, V_M1, V_V1, V_G2, V_B2, V_M2, V_V2, V_IR, V_IZ, V_IN, V_HR, V_HZ, V_HN) = range(14)
NV = 14

C_SEL = 0
C_SELT = C_SEL + CC
C_SAME = C_SELT + 64
C_G5 = C_SAME + CC
C_G5T = C_G5 + NG
C_ID = C_G5T + CC
C_ROW = C_ID + D
C_ONE = C_ROW + 3
C_MH = C_ONE + 1
NCONST = C_MH + 8


def constants():
    c = np.zeros((128, NCONST), np.float32)
    for g, nodes in enumerate(GROUPS):
        for b in range(2):
            for i, n in enumerate(nodes):
                row = GOFF[g] + b * len(nodes) + i
                c[SLOT * b + n, C_SEL + row] = 1
                c[row, C_SELT + SLOT * b + n] = 1
                c[row, C_SAME + GOFF[g]:C_SAME + GOFF[g] + GSIZE[g]] = 1
                c[row, C_G5 + g] = 1
                c[g, C_G5T + row] = 1
    c[:, C_ID:C_ID + D] = np.eye(D)
    for side, rows in enumerate(dist_rows()):
        for r, (_, alpha, beta, low) in enumerate(rows):
            c[32 * side + r, C_ROW:C_ROW + 3] = alpha, beta, -low
    c[:, C_ONE] = 1
    c[:, C_MH:C_MH + 8] = -0.5
    return c


def gnn_kernel(nc, xT, adjT, consts, vecs, w_rows, b_rows, w_c1, w_c2, w_ih, w_hh, w_msg, b_msg,
               g_w1, g_b1, g_w2, g_b2, g_fw, out):
    fp32 = mybir.dt.float32
    fp32r = mybir.dt.float32r
    ALU = mybir.AluOpType
    ACT = mybir.ActivationFunctionType
    AX = mybir.AxisListType

    ctx = ExitStack()
    with ctx:
        def sb(name, shape, dt=fp32):
            return ctx.enter_context(nc.sbuf_tensor(name, shape, dt))

        def sem(name):
            return ctx.enter_context(nc.semaphore(name))

        def full(ap):
            return ap.bitcast(fp32)

        cst = sb("cst", [128, NCONST])
        vec = sb("vec", [128, NV])
        brow = sb("brow", [64, 1])
        wrow = sb("wrow", [128, 64]); wrow_hl = sb("wrow_hl", [128, 128], fp32r)
        wc1 = sb("wc1", [128, D]); wc1_h = sb("wc1_h", [128, D], fp32r); wc1_l = sb("wc1_l", [128, D], fp32r)
        wc2 = sb("wc2", [128, TAPS, D])
        yy = sb("yy", [128, 3 * N])
        ya, yb, y2 = yy[:, 0:N], yy[:, N:2 * N], yy[:, 2 * N:3 * N]
        wsum = yy[:, 0:2 * G3 * D].rearrange("p (k g d) -> p k g d", k=2, g=G3)
        w1_h = sb("w1_h", [128, G3, D], fp32r); w1_l = sb("w1_l", [128, G3, D], fp32r)
        w2_h = sb("w2_h", [128, G3, D], fp32r); w2_l = sb("w2_l", [128, G3, D], fp32r)
        w3_h = sb("w3_h", [128, G3, D], fp32r); w3_l = sb("w3_l", [128, G3, D], fp32r)
        w4_h = sb("w4_h", [128, G3 - 1, D], fp32r); w4_l = sb("w4_l", [128, G3 - 1, D], fp32r)
        wg = sb("wg", [128, 3, 3 * D])
        wg_h = sb("wg_h", [128, 3, 3 * D], fp32r); wg_l = sb("wg_l", [128, 3, 3 * D], fp32r)
        wmsg = sb("wmsg", [128, D])
        bmsg = sb("bmsg", [128, D])
        prm = sb("prm", [128, 16])
        P_VE, P_RS, P_S1, P_S2, P_T1, P_T2, P_A1, P_A2, P_R, P_Z, P_RH, P_ZH, P_H2, P_N2 = 0, 2, 4, 5, 6, 7, 8, 9, 10, 11, 12, 13, 14, 15

        xin = [sb(f"xin{p}", [128, N]) for p in range(2)]
        xkeep = [sb(f"xkeep{p}", [128, N]) for p in range(2)]
        x_h = [sb(f"x_h{p}", [128, N], fp32r) for p in range(2)]
        x_l = [sb(f"x_l{p}", [128, N], fp32r) for p in range(2)]
        adj = [sb(f"adj{p}", [128, CH, N]) for p in range(2)]
        uab = sb("uab", [64, 2 * N]); u = uab[:, 0:N]; ab = uab[:, N:2 * N]; val = sb("val", [64, N]); val_h = sb("val_h", [64, N], fp32r)
        left = sb("left", [KD, N], fp32r); right = sb("right", [KD, N], fp32r)
        h1 = sb("h1", [128, 2 * PH + 2])
        dd = sb("dd", [128, 2, PH]); dd_h = sb("dd_h", [128, 2, PH], fp32r); dd_l = sb("dd_l", [128, 2, PH], fp32r)
        sd = sb("sd", [128, 2, 2, PH]); sd_h = sb("sd_h", [128, 2, 2, PH], fp32r); sd_l = sb("sd_l", [128, 2, 2, PH], fp32r)
        am = sb("am", [128, CH, N])
        am_h = sb("am_h", [128, CH, N], fp32r); am_l = sb("am_l", [128, CH, N], fp32r)
        mt = sb("mt", [128, N])
        m_h = [sb(f"m_h{p}", [128, N], fp32r) for p in range(2)]
        m_l = [sb(f"m_l{p}", [128, N], fp32r) for p in range(2)]
        n_h = sb("n_h", [128, N], fp32r); n_l = sb("n_l", [128, N], fp32r)
        mid = sb("mid", [128, 2, HALF]); cu = sb("cu", [128, N]); cv = sb("cv", [128, N])
        c_h = sb("c_h", [128, N], fp32r); c_l = sb("c_l", [128, N], fp32r)
        rt = sb("rt", [128, N]); r1 = rt; zt = sb("zt", [128, N])
        gg = sb("gg", [128, N]); tt = sb("tt", [128, N]); nn = sb("nn", [128, N])
        yn = sb("yn", [128, CH, D]); st = sb("st", [128, CH, 6]); mv = sb("mv", [128, CH, 2]); base = sb("base", [128, CH + 1]); rs = sb("rs", [128, CH + 1])
        yo = [sb(f"yo{p}", [128, CH, D]) for p in range(2)]

        x1 = sb("x1", [64, PAIRS, D])
        bd = sb("bd", [64, PAIRS, 64])
        ac = sb("ac", [CC + NG, PAIRS, CC])
        dg = sb("dg", [CC, 4, PAIRS])
        dinv = sb("dinv", [CC, PAIRS])
        fw = sb("fw", [CC, NG]); fs = sb("fs", [CC, 4]); fe = sb("fe", [CC, NG]); wcol = sb("wcol", [CC, 1])
        gw1 = sb("gw1", [128, NG, HID]); gw2 = sb("gw2", [128, NG, 2, D]); gb1 = sb("gb1", [128, NG, 2])

        ring = [ctx.enter_context(nc.psum_tensor(f"ring{i}", [128, N], fp32)) for i in range(2)]
        p_outer = ctx.enter_context(nc.psum_tensor("p_outer", [128, N], fp32))
        p_middle = ctx.enter_context(nc.psum_tensor("p_middle", [128, N], fp32))
        p_r, p_z, p_gi, p_gh = [ctx.enter_context(nc.psum_tensor(n, [128, N], fp32)) for n in ("p_r", "p_z", "p_gi", "p_gh")]

        s_cst = sem("s_cst"); s_vec = sem("s_vec"); s_wc1d = sem("s_wc1d"); s_wrowd = sem("s_wrowd")
        s_brow = sem("s_brow"); s_wmsgd = sem("s_wmsgd"); s_bmsg = sem("s_bmsg"); s_w2d = [sem(f"s_w2d{i}") for i in range(3)]; s_wgd = sem("s_wgd")
        s_gd = sem("s_gd"); s_bdd = sem("s_bdd"); s_zero = sem("s_zero")
        s_prm = sem("s_prm"); s_pow = sem("s_pow"); s_wsum = sem("s_wsum")
        s_w1s = sem("s_w1s"); s_whi = sem("s_whi"); s_wlo = sem("s_wlo"); s_w4l = sem("s_w4l"); s_wgs = sem("s_wgs")
        s_bdi = sem("s_bdi"); s_sel1m = sem("s_sel1m"); s_sel1 = sem("s_sel1"); s_acm = sem("s_acm"); s_ac = sem("s_ac")
        s_deg = sem("s_deg"); s_dg = sem("s_dg"); s_dpow = sem("s_dpow"); s_dinv = sem("s_dinv")
        s_fw = sem("s_fw"); s_fe = sem("s_fe"); s_wcol = sem("s_wcol")
        s_x = [sem(f"s_x{p}") for p in range(2)]
        s_adj = [sem(f"s_adj{p}") for p in range(2)]
        s_xh = sem("s_xh"); s_xl = sem("s_xl"); s_xk = sem("s_xk")
        s_rows = sem("s_rows"); s_u0 = sem("s_u0"); s_u = sem("s_u"); s_ab = sem("s_ab"); s_val = sem("s_val"); s_valh = sem("s_valh")
        s_left = sem("s_left"); s_right = sem("s_right")
        s_c1 = sem("s_c1"); s_h1 = sem("s_h1"); s_dd = sem("s_dd"); s_ddh = sem("s_ddh"); s_ddl = sem("s_ddl")
        s_sd = sem("s_sd"); s_sdh = sem("s_sdh"); s_sdl = sem("s_sdl")
        s_msg = sem("s_msg"); s_mt = sem("s_mt"); s_mh = sem("s_mh"); s_ml = sem("s_ml")
        s_d = [sem(f"s_d{c}") for c in range(CH)]; s_e = [sem(f"s_e{c}") for c in range(CH)]
        s_am = [sem(f"s_am{c}") for c in range(CH)]; s_amh = sem("s_amh"); s_aml = sem("s_aml")
        s_outer = sem("s_outer"); s_middle = sem("s_middle"); s_mid = sem("s_mid"); s_mids = sem("s_mids"); s_cu = sem("s_cu"); s_cv = sem("s_cv"); s_ch = sem("s_ch"); s_cl = sem("s_cl")
        s_nmp = sem("s_nmp"); s_nh = sem("s_nh"); s_nl = sem("s_nl")
        s_gx = sem("s_gx"); s_gn = sem("s_gn"); s_gr = sem("s_gr"); s_gi = sem("s_gi"); s_gz = sem("s_gz")
        s_rt = sem("s_rt"); s_zt = sem("s_zt"); s_r1 = sem("s_r1"); s_gg = sem("s_gg"); s_tt = sem("s_tt"); s_nn = sem("s_nn")
        s_ya = sem("s_ya"); s_yb = sem("s_yb"); s_y2 = sem("s_y2")
        s_t = sem("s_t"); s_yn = sem("s_yn"); s_st = sem("s_st"); s_mv = sem("s_mv"); s_base = sem("s_base"); s_rs = sem("s_rs"); s_grow = sem("s_grow"); s_yo = sem("s_yo")
        s_out = [sem(f"s_out{p}") for p in range(2)]
        s_spread = sem("s_spread"); s_columns = sem("s_columns"); s_combined = sem("s_combined"); s_msel = sem("s_msel")
        s_gathered = sem("s_gathered"); s_agT = sem("s_agT"); s_first = sem("s_first"); s_hid0 = sem("s_hid0"); s_hid1 = sem("s_hid1")
        s_second = sem("s_second"); s_sT = sem("s_sT"); s_back = sem("s_back"); s_ss = sem("s_ss"); s_agg2 = sem("s_agg2")
        s_o2 = sem("s_o2"); s_scattered = sem("s_scattered"); s_yfin = sem("s_yfin")
        s_fin = sem("s_fin")

        HP = 4
        LOTS = [(0, 4), (4, PAIRS - 1), (PAIRS - 1, PAIRS)]
        EARLY, LATE = (0, 1), (2,)

        def part(t, a, rows, width):
            flat = t[:] if len(t.shape) == 2 else t[:].rearrange("p a b -> p (a b)")
            return flat[0:rows, a:a + PAIRS * width].rearrange("p (j w) -> p j w", w=width)

        sel1 = part(wc2, 0, 64, CC)
        diag = part(wc2, 0, CC, CC)
        msel = part(wc2, PAIRS * CC, 64, CC)
        agT, hT0, hT1 = part(adj[1], 0, 128, CC), part(adj[1], PAIRS * CC, 128, CC), part(wc2, 0, 128, CC)
        hT = (hT0, hT1)
        hz = adj[0][:].rearrange("p a b -> p (a b)")[:, 0:2 * NG * CC].rearrange("p (k g c) -> p k g c", k=2, g=NG)
        sT = part(adj[0], 2 * NG * CC, 128, CC)
        ss, o2 = part(am, 0, CC + NG, D), part(am, PAIRS * D, CC, D)
        yfin = uab[:, 0:PAIRS * D].rearrange("p (j d) -> p j d", d=D)
        gst = sb("gst", [64, PAIRS, 6]); gmv = sb("gmv", [64, PAIRS, 2]); gbase = sb("gbase", [64, PAIRS]); grs = sb("grs", [64, PAIRS])
        s_bias = sem("s_bias"); s_zz = sem("s_zz"); s_diag = sem("s_diag"); s_hz = sem("s_hz")
        s_gmv = sem("s_gmv"); s_gbase = sem("s_gbase"); s_grs = sem("s_grs"); s_gst = sem("s_gst")

        BC_BANKS, MSEL_BANKS = (p_r, p_z), (p_gi, p_gh)
        TR_BANKS = (p_r, p_z, p_z)
        W1_BANKS = (p_outer, p_middle, ring[1], p_gh, p_r, p_z)
        W2_BANKS = (p_gi, p_r, p_z)
        W1_LATE = (ring[0], p_z)
        W2_LATE = p_gi
        TS_BANKS = (p_outer, p_middle)
        AGG2_BANKS = (ring[1], p_gh, p_r)
        SC_BANKS = (p_outer, p_middle, ring[0])

        def lot(i):
            return slice(*LOTS[i])

        def lot_size(i):
            return LOTS[i][1] - LOTS[i][0]

        def pairs(h):
            return slice(HP * h, HP * h + HP)

        def group(g):
            return slice(GOFF[g], GOFF[g] + GSIZE[g])

        def banked(bank_, rows, width, count=HP):
            return bank_[0:rows, 0:count * width].rearrange("p (j w) -> p j w", w=width)

        def cols(bank_, g):
            return bank_[:, 0:(PAIRS - 1) * GSIZE[g]].rearrange("p (j w) -> p j w", w=GSIZE[g])

        ERL = slice(0, PAIRS - 1)

        class GroupsPE:

            def spread(self, pe, mm):
                pe.wait_ge(s_diag, 2)
                for h in range(2):
                    mm(BC_BANKS[h][0:CC, 0:HP * CC], cst[0:CC, C_SAME:C_SAME + CC], diag[:, pairs(h), :]).then_inc(s_spread, 1)

            def combine(self, pe, mm):
                for h in range(2):
                    pe.wait_ge(s_columns, h + 1)
                    mm(MSEL_BANKS[h][0:64, 0:HP * CC], cst[0:CC, C_SELT:C_SELT + 64], ac[0:CC, pairs(h), :]).then_inc(s_combined, 1)

            def aggregate(self, pe, mm, i):
                for n, j in enumerate(range(*LOTS[i])):
                    last = mm(TR_BANKS[i][:, CC * n:CC * n + CC], x1[:, j, :], msel[:, j, :])
                last.then_inc(s_gathered, 1)

            def first_early(self, pe, mm, groups):
                for g in groups:
                    for k in range(2):
                        if g == 2:
                            pe.wait_ge((s_rt, s_zt)[k], B)
                        if g >= 3:
                            pe.wait_ge((s_hid0, s_hid1)[k], g - 2)
                        if (g, k) == (1, 1):
                            pe.wait_ge(s_gg, B)
                        mm(cols(W1_BANKS[(2 * g + k) % 6], g), gw1[:, g, D * k:D * k + D],
                           agT[:, ERL, group(g)]).then_inc(s_first, 1)

            def second_early(self, pe, mm, groups):
                for g in groups:
                    pe.wait_ge(s_hid0, g + 1); pe.wait_ge(s_hid1, g + 1)
                    if g in (1, 2):
                        pe.wait_ge((s_hid0, s_hid1)[g - 1], 3)
                    if g >= 3:
                        pe.wait_ge(s_sT, g - 2)
                    for k in range(2):
                        last = mm(cols(W2_BANKS[g % 3], g), gw2[:, g, k, :], hT[k][:, ERL, group(g)], k == 0, k == 1)
                    last.then_inc(s_second, 1)

            def first_late(self, pe, mm):
                pe.wait_ge(s_agT, 3)
                for k in range(2):
                    for g in range(NG):
                        last = mm(W1_LATE[k][:, group(g)], gw1[:, g, D * k:D * k + D], agT[:, PAIRS - 1, group(g)])
                    last.then_inc(s_first, 1)

            def second_late(self, pe, mm):
                for k in range(2):
                    pe.wait_ge((s_hid0, s_hid1)[k], NG + 1)
                    for g in range(NG):
                        last = mm(W2_LATE[0:CC, 0:D], hz[:, k, g, :], gw2[:, g, k, :], g == 0 and k == 0, g == NG - 1 and k == 1)
                last.then_inc(s_second, 1)

            def back(self, pe, mm, i):
                for n, j in enumerate(range(*LOTS[i])):
                    last = nc.tensor.transpose(TS_BANKS[i][0:CC, D * n:D * n + D], sT[:, j, :], cst[:, C_ID:C_ID + D])
                last.then_inc(s_back, 1)

            def aggregate2(self, pe, mm, i):
                pe.wait_ge(s_bias, 32)
                pe.wait_ge(s_ss, i + 1)
                for n, j in enumerate(range(*LOTS[i])):
                    last = mm(AGG2_BANKS[i][0:CC, D * n:D * n + D], ac[:, j, :], ss[:, j, :])
                last.then_inc(s_agg2, 1)

            def residual(self, pe, mm, i):
                mm(SC_BANKS[i][0:64, 0:D * lot_size(i)], cst[0:64, C_ID:C_ID + 64], x1[:, lot(i), :], True, False)

            def scatter(self, pe, mm, i):
                pe.wait_ge(s_o2, i + 1)
                first = i in EARLY
                mm(SC_BANKS[i][0:64, 0:D * lot_size(i)], cst[0:CC, C_SELT:C_SELT + 64], o2[:, lot(i), :], first, True).then_inc(s_scattered, 1)

        class GroupsAct:
            def combined(self, act):
                for h in range(2):
                    act.wait_ge(s_combined, h + 1)
                    nc.scalar.activation(msel[:, pairs(h), :], banked(MSEL_BANKS[h], 64, CC), ACT.Copy).then_inc(s_msel, 1)

            def channels(self, act, i):
                act.wait_ge(s_gathered, i + 1)
                nc.scalar.activation(agT[:, lot(i), :], banked(TR_BANKS[i], 128, CC, lot_size(i)), ACT.Copy).then_inc(s_agT, 1)

            def hidden(self, act, g):
                act.wait_ge(s_first, 2 * g + 1)
                nc.scalar.activation(hT0[:, ERL, group(g)], cols(W1_BANKS[(2 * g) % 6], g), ACT.Relu,
                                     bias=gb1[:, g, 0:1]).then_inc(s_hid0, 1)

            def hidden_late(self, act):
                act.wait_ge(s_hz, 1)
                act.wait_ge(s_first, 2 * NG + 1)
                for g in range(NG):
                    last = nc.scalar.activation(hz[:, 0, g, group(g)], W1_LATE[0][:, group(g)], ACT.Relu, bias=gb1[:, g, 0:1])
                last.then_inc(s_hid0, 1)

            def support(self, act, g):
                act.wait_ge(s_second, g + 1)
                nc.scalar.activation(sT[:, ERL, group(g)], cols(W2_BANKS[g % 3], g), ACT.Copy).then_inc(s_sT, 1)

            def rows_early(self, act, i):
                act.wait_ge(s_back, i + 1)
                nc.scalar.activation(ss[0:CC, lot(i), :], banked(TS_BANKS[i], CC, D, lot_size(i)), ACT.Copy).then_inc(s_ss, 1)

            def rows_late(self, act):
                act.wait_ge(s_second, NG + 1)
                nc.scalar.activation(ss[0:CC, PAIRS - 1, :], W2_LATE[0:CC, 0:D], ACT.Copy).then_inc(s_ss, 1)

            def weigh(self, act, i):
                act.wait_ge(s_wcol, 3)
                act.wait_ge(s_agg2, i + 1)
                nc.scalar.activation(o2[:, lot(i), :], banked(AGG2_BANKS[i], CC, D, lot_size(i)), ACT.Relu,
                                     scale=wcol[:, 0:1]).then_inc(s_o2, 1)

        def residual_sum(j):
            return SC_BANKS[2][0:64, 0:D] if j == PAIRS - 1 else yfin[:, j, :]

        def groups_power(pool, e):
            js = lot(e)
            pool.wait_ge(s_gmv, e + 1)
            nc.gpsimd.tensor_scalar(gbase[:, js], gmv[:, js, 1], 1.0, EPS, ALU.mult, ALU.add).then_inc(s_gbase, 1)
            pool.wait_ge(s_gbase, e + 1)
            nc.gpsimd.tensor_tensor(grs[:, js], gbase[:, js], cst[0:64, C_MH:C_MH + js.stop - js.start], ALU.pow).then_inc(s_grs, 1)

        class GroupsDVE:
            def prepare(self, dve):
                TT, TS = nc.vector.tensor_tensor, nc.vector.tensor_scalar
                dve.wait_ge(s_fe, 1)
                nc.vector.tensor_tensor_reduce(out=fw[:], in0=fe[:], in1=cst[0:CC, C_G5:C_G5 + NG], scale=1.0, scalar=0.0,
                                               op0=ALU.mult, op1=ALU.add, accum_out=fs[:, 3:4]).then_inc(s_wcol, 1)
                nc.vector.reciprocal(fs[:, 0:1], fs[:, 2:3]).then_inc(s_wcol, 1)
                dve.wait_ge(s_wcol, 2)
                TT(wcol[:], fs[:, 3:4], fs[:, 0:1], ALU.mult).then_inc(s_wcol, 1)

            def columns(self, dve):
                for h in range(2):
                    dve.wait_ge(s_spread, h + 1)
                    nc.vector.tensor_tensor(ac[0:CC, pairs(h), :], ac[0:CC, pairs(h), :], banked(BC_BANKS[h], CC, CC), ALU.mult).then_inc(s_columns, 1)

            def hidden(self, dve, g):
                dve.wait_ge(s_first, 2 * g + 2)
                nc.vector.tensor_scalar(hT1[:, ERL, group(g)], cols(W1_BANKS[(2 * g + 1) % 6], g), gb1[:, g, 1:2], 0.0,
                                        ALU.add, ALU.max).then_inc(s_hid1, 1)

            def hidden_late(self, dve):
                dve.wait_ge(s_hz, 1)
                dve.wait_ge(s_first, 2 * NG + 2)
                for g in range(NG):
                    last = nc.vector.tensor_scalar(hz[:, 1, g, group(g)], W1_LATE[1][:, group(g)], gb1[:, g, 1:2], 0.0,
                                                   ALU.add, ALU.max)
                last.then_inc(s_hid1, 1)

            def sums(self, dve, i):
                dve.wait_ge(s_scattered, i + 1)
                if i in EARLY:
                    nc.vector.tensor_tensor(yfin[:, lot(i), :], banked(SC_BANKS[i], 64, D, lot_size(i)), x1[:, lot(i), :], ALU.add).then_inc(s_zz, 1)
                    dve.wait_ge(s_zz, i + 1)
                for j in range(*LOTS[i]):
                    last = nc.vector.bn_stats(gst[:, j, :], residual_sum(j))
                last.then_inc(s_gst, 1)

            def moments(self, dve, e):
                dve.wait_ge(s_gst, e + 1)
                for j in range(*LOTS[e]):
                    last = nc.vector.bn_aggr(gmv[:, j, :], gst[:, j, :])
                last.then_inc(s_gmv, 1)

            def normalise(self, dve, i):
                dve.wait_ge(s_gmv, i + 1); dve.wait_ge(s_grs, i + 1)
                for j in range(*LOTS[i]):
                    last = nc.vector.tensor_scalar(yfin[:, j, :], residual_sum(j), gmv[:, j, 0:1], grs[:, j:j + 1], ALU.subtract, ALU.mult)
                last.then_inc(s_yfin, 1)

        g_pe, g_act, g_dve = GroupsPE(), GroupsAct(), GroupsDVE()

        block = ctx.enter_context(nc.Block())

        def after(eng, semaphore, n):
            if not isinstance(n, int) or n > 0:
                eng.wait_ge(semaphore, n)

        def batches(eng, step):
            step(0, 0, lambda k: k)
            step(1, 1, lambda k: 1 + k)
            with eng.Fori(1, PAIRS - 1) as i:
                for p in range(2):
                    known = {}

                    def count(k, p=p, known=known):
                        if k not in known:
                            known[k] = eng.snap(i * 2 + (p + k))
                        return known[k]
                    step(count(0), p, count)
            step(B - 2, 0, lambda k: B - 2 + k)
            step(B - 1, 1, lambda k: B - 1 + k)

        def dma_count(n, p, k):
            v = n(k)
            if isinstance(v, int):
                return 16 * (v // 2 + 1)
            return (v - p) * 8 + 16

        def static(b, value):
            return isinstance(b, int) and b == value

        def halves(t, start):
            return t[:, start:start + 2 * PH].rearrange("p (i s) -> p s i", s=2)

        def sums_differences(TT, eng, n, k):
            after(eng, s_h1, n(k + 1)); after(eng, s_sdh, n(k)); after(eng, s_sdl, n(k))
            TT(sd[:, 0], halves(h1, 1), halves(h1, 0), ALU.add)
            TT(sd[:, 1], halves(h1, 1), halves(h1, 0), ALU.subtract).then_inc(s_sd, 1)

        S_ROWS, S_C1, S_MSG, S_T, S_NMP, S_D0 = 0, 1, 2, 3, 4, 5

        def bank(p, k):
            return ring[(9 * p + k) % 2]

        FIRST_MSG = p_z
        GATE = {"r": 0, "z": 1, "n": 2}

        def store_groups(eng, i, q):
            j0, j1 = LOTS[i]
            eng.wait_ge(s_out[q], 16 * (j1 + 1))
            eng.wait_ge(s_yfin, i + 1)
            eng.dma_start(out[2 * j0 + q:2 * j1:2, 0:GN, :].rearrange("j n d -> n j d"),
                          yfin[SLOT * q:SLOT * q + GN, j0:j1, :]).then_inc(s_fin, 16)

        @block.sync
        def _(sp):
            sp.dma_start(xin[0][:], xT[0, :, :]).then_inc(s_x[0], 16)
            sp.dma_start(wc1[:], w_c1[:, :]).then_inc(s_wc1d, 16)
            sp.dma_start(vec[:], vecs[:, :]).then_inc(s_vec, 16)
            sp.dma_start(cst[:], consts[:, :]).then_inc(s_cst, 16)
            sp.dma_start(wrow[:], w_rows[:, :]).then_inc(s_wrowd, 16)
            sp.dma_start(wc2[:, 0::3, :], w_c2[:, 0::3, :]).then_inc(s_w2d[0], 16)
            sp.dma_start(brow[:], b_rows[:, :]).then_inc(s_brow, 16)
            sp.dma_start(wmsg[:], w_msg[:, :]).then_inc(s_wmsgd, 16)
            sp.dma_start(wc2[:, 2::3, :], w_c2[:, 2::3, :]).then_inc(s_w2d[2], 16)
            sp.dma_start(wc2[:, 1::3, :], w_c2[:, 1::3, :]).then_inc(s_w2d[1], 16)
            sp.dma_start(bmsg[:], b_msg[:, :].to_broadcast([128, D])).then_inc(s_bmsg, 16)
            sp.dma_start(adj[0][:], adjT[0, :, :].rearrange("(c p) n -> p c n", p=128)).then_inc(s_adj[0], 16)
            sp.dma_start(wg[:, 0:2, :], w_ih[:, :, :]).then_inc(s_wgd, 16)
            sp.dma_start(wg[:, 2, :], w_hh[:, :]).then_inc(s_wgd, 16)
            sp.dma_start(xin[1][:], xT[1, :, :]).then_inc(s_x[1], 16)
            sp.wait_ge(s_zero, 4)
            for q in range(2):
                sp.dma_start(bd[SLOT * q:SLOT * q + GN, :, SLOT * q:SLOT * q + GN],
                             adjT[q::2, 0:GN, 0:GN].rearrange("j m n -> m j n")).then_inc(s_bdd, 16)
            sp.dma_start(fw[:], g_fw[:, :].to_broadcast([CC, NG])).then_inc(s_gd, 16)
            sp.dma_start(gb1[:], g_b1[:, :, :]).then_inc(s_gd, 16)
            sp.dma_start(gw1[:], g_w1.rearrange("g p h -> p g h")).then_inc(s_gd, 16)
            sp.dma_start(gw2[:], g_w2.rearrange("g (h p) o -> p g h o", p=128)).then_inc(s_gd, 16)

            sp.dma_start(adj[1][:], adjT[1, :, :].rearrange("(c p) n -> p c n", p=128)).then_inc(s_adj[1], 16)

            def step(b, p, n):
                if not (static(b, B - 2) or static(b, B - 1)):
                    after(sp, s_xl, n(1)); after(sp, s_xh, n(1)); after(sp, s_xk, n(1)); after(sp, s_msg, n(1))
                    sp.dma_start(xin[p][:], xT[b + 2, :, :]).then_inc(s_x[p], 16)
                    if static(b, 0):
                        sp.wait_ge(s_am[0], 1); sp.wait_ge(s_am[1], 1); sp.wait_ge(s_am[2], 1)
                    after(sp, s_am[CH - 1], n(1))
                    sp.dma_start(adj[p][:], adjT[b + 2, :, :].rearrange("(c p) n -> p c n", p=128)).then_inc(s_adj[p], 16)
                if not static(b, 0):
                    store(b - 1, 1 - p, n(0))

            def store(b, p, count):
                after(sp, s_yo, count)
                sp.dma_start(out[b, :, :].rearrange("(c p) d -> p c d", p=128), yo[p][:]).then_inc(s_out[p], 16)

            batches(sp, step)
            sp.wait_ge(s_combined, 2); sp.wait_ge(s_aml, B)
            sp.dma_start(ac[CC:CC + NG, :, :], consts[0:NG, C_G5T:C_G5T + CC].unsqueeze(1).broadcast_to([NG, PAIRS, CC])).then_inc(s_bias, 16)
            sp.dma_start(ss[CC:CC + NG, :, :], g_b2.unsqueeze(1).broadcast_to([NG, PAIRS, D])).then_inc(s_bias, 16)
            store(B - 1, 1, B)
            for i in range(3):
                for q in range(2):
                    if (i, q) != (2, 1):
                        store_groups(sp, i, q)
            sp.wait_ge(s_fin, 96)

        @block.tensor
        def _(pe):
            def mm(out_, w, x, start=True, stop=True):
                return nc.tensor.matmul(out_, w, x, start=start, stop=stop, skip_group_check=True)

            def mm3(out_, w_h, w_l, v_h, v_l, start=True, stop=True):
                mm(out_, w_h, v_h, start, False)
                mm(out_, w_h, v_l, False, False)
                return mm(out_, w_l, v_h, False, stop)

            def rows(p, n, k):
                after(pe, s_xh, n(k + 1)); after(pe, s_xl, n(k + 1))
                to = bank(1 - p, S_ROWS)
                mm(to[:], wrow_hl[:], x_h[p][:])
                mm(to[0:64, :], wrow_hl[:, 0:64], x_l[p][:], False, True).then_inc(s_rows, 1)

            def conv1(p, n, k):
                mm3(bank(1 - p, S_C1)[:], wc1_h[:], wc1_l[:], x_h[p][:], x_l[p][:]).then_inc(s_c1, 1)

            def msg(p, to):
                for c in range(CH):
                    last = mm(to[:, D * c:D * c + D], xin[p][:, D * c:D * c + D], wmsg[:])
                last.then_inc(s_msg, 1)

            def dist(p, c):
                mm(bank(1 - p, S_D0 + c)[:], left[:, D * c:D * c + D], right[:]).then_inc(s_d[c], 1)

            pe.wait_ge(s_xh, 1); pe.wait_ge(s_xl, 1); pe.wait_ge(s_w1s, 2)
            conv1(0, None, 0)
            pe.wait_ge(s_w1s, 4)
            mm3(bank(1, S_ROWS)[0:64, :], wrow_hl[:, 0:64], wrow_hl[:, 64:128], x_h[0][:], x_l[0][:]).then_inc(s_rows, 1)
            pe.wait_ge(s_wmsgd, 16)
            msg(0, FIRST_MSG)

            def conv_part(out_, w_h, w_l, v_h, v_l, first):
                count = w_h.shape[1]
                for g in range(count):
                    par, i = (3 * g + first) % 2, (3 * g + first) // 2
                    last = mm3(out_, w_h[:, g, :], w_l[:, g, :], v_h[:, par, i:i + HALF], v_l[:, par, i:i + HALF],
                               g == 0, g == count - 1)
                return last

            def gate(out_, name, source, v_h, v_l, start, stop):
                cols = slice(D * GATE[name], D * GATE[name] + D)
                return mm3(out_[:], wg_h[:, source, cols], wg_l[:, source, cols], v_h[:], v_l[:], start, stop)

            def transposes(p, q):
                for c in range(CH):
                    last = nc.tensor.transpose(bank(p, S_T)[:, D * c:D * c + D], y2[:, D * c:D * c + D], cst[:, C_ID:C_ID + D])
                last.then_inc(s_t, 1)

            def adjacency(stage):
                sel = cst[0:64, C_SEL:C_SEL + CC]
                if stage == 0:
                    pe.wait_ge(s_bdi, 1)
                    for h in range(2):
                        for j in range(HP):
                            last = mm((p_r, p_z)[h][0:64, CC * j:CC * j + CC], bd[:, HP * h + j, :], sel)
                        last.then_inc(s_sel1m, 1)
                elif stage == 1:
                    for h in range(2):
                        pe.wait_ge(s_sel1, h + 1)
                        for j in range(HP):
                            last = mm((p_gi, p_gh)[h][0:CC, CC * j:CC * j + CC], sel1[:, HP * h + j, :], sel)
                        last.then_inc(s_acm, 1)
                else:
                    pe.wait_ge(s_ac, 2)
                    for j in range(PAIRS):
                        last = mm(p_middle[0:CC, j:j + 1], ac[0:CC, j, :], cst[0:CC, C_ONE:C_ONE + 1])
                    last.then_inc(s_deg, 1)

            def step(b, p, n):
                q = 1 - p
                more = not static(b, B - 1)

                def differences_part():
                    after(pe, s_sdh, n(1)); after(pe, s_sdl, n(1))
                    after(pe, s_mid, n(0))
                    if static(b, 0):
                        pe.wait_ge(s_whi, 3); pe.wait_ge(s_wlo, 2)
                    if static(b, 1):
                        pe.wait_ge(s_dg, 1)
                    conv_part(p_middle[:, HALF:N], w3_h, w3_l, sd_h[:, 1], sd_l[:, 1], 1)

                def sums_part():
                    if static(b, 0):
                        pe.wait_ge(s_whi, 4); pe.wait_ge(s_wlo, 3)
                    conv_part(p_middle[:, 0:HALF], w2_h, w2_l, sd_h[:, 0], sd_l[:, 0], 1).then_inc(s_middle, 1)

                after(pe, s_ddh, n(1)); after(pe, s_ddl, n(1))
                after(pe, s_cu, n(0))
                if static(b, 0):
                    pe.wait_ge(s_whi, 1); pe.wait_ge(s_wlo, 1)
                conv_part(p_outer[:, 0:HALF], w1_h, w1_l, dd_h, dd_l, 0)

                def last_taps():
                    if static(b, 0):
                        pe.wait_ge(s_whi, 2); pe.wait_ge(s_w4l, 1)
                    conv_part(p_outer[:, HALF:N], w4_h, w4_l, dd_h, dd_l, 1).then_inc(s_outer, 1)

                if static(b, 0):
                    last_taps()
                    pe.wait_ge(s_left, 1); pe.wait_ge(s_right, 1); pe.wait_ge(s_h1, 1)
                    dist(0, 0)
                    pe.wait_ge(s_u, 1)
                    dist(0, 1)
                    pe.wait_ge(s_e[0], 1)
                    dist(0, 2)
                    pe.wait_ge(s_e[1], 1)
                    dist(0, 3)
                    pe.wait_ge(s_mt, 1)
                if static(b, B - 1):
                    pe.wait_ge(s_rt, B - 1); pe.wait_ge(s_zt, B - 1)
                    g_pe.spread(pe, mm)
                if more and not static(b, 0):
                    after(pe, s_e[2], n(1))
                    rows(q, n, 1)
                if not static(b, 0):
                    last_taps()
                if static(b, 0):
                    differences_part()
                    sums_part()
                    pe.wait_ge(s_e[2], 1)
                    rows(q, n, 1)
                    adjacency(0)
                if more:
                    after(pe, s_e[3], n(1))
                    conv1(q, n, 1)
                    after(pe, s_u0, n(1))
                    msg(q, bank(p, S_MSG))
                if not static(b, 0):
                    differences_part()
                if static(b, B - 1):
                    pe.wait_ge(s_gg, B - 1); pe.wait_ge(s_tt, B - 1)
                    g_pe.combine(pe, mm)
                if not static(b, 0):
                    after(pe, s_y2, n(0))
                    if more:
                        after(pe, s_h1, n(2))
                    else:
                        after(pe, s_e[3], n(1))
                    transposes(p, q)
                if static(b, 0):
                    adjacency(1)
                else:
                    sums_part()
                if static(b, B - 1):
                    pe.wait_ge(s_msel, 2)
                    pe.wait_ge(s_grow, B - 2)
                    for i in EARLY:
                        g_pe.aggregate(pe, mm, i)
                after(pe, s_amh, n(1)); after(pe, s_aml, n(1)); after(pe, s_mh, n(1)); after(pe, s_ml, n(1))
                if more:
                    after(pe, s_mt, n(2))
                else:
                    after(pe, s_e[2], n(1))
                for c in range(CH):
                    cols = slice(D * c, D * c + D)
                    last = mm3(bank(p, S_NMP)[:], m_h[p][:, cols], m_l[p][:, cols], am_h[:, c, :], am_l[:, c, :],
                               c == 0, c == CH - 1)
                last.then_inc(s_nmp, 1)
                if more:
                    after(pe, s_left, n(2)); after(pe, s_right, n(2))
                    if static(b, 0):
                        pe.wait_ge(s_h1, 2)
                    after(pe, s_yn, n(0))
                    dist(q, 0)
                if static(b, 0):
                    pe.wait_ge(s_wgs, 2)
                if static(b, B - 1):
                    pe.wait_ge(s_agT, 2)
                after(pe, s_rt, n(0)); gate(p_r, "r", 2, x_h[p], x_l[p], True, False)
                after(pe, s_zt, n(0)); gate(p_z, "z", 2, x_h[p], x_l[p], True, False)
                if static(b, 0):
                    pe.wait_ge(s_ac, 2)
                after(pe, s_gg, n(0)); gate(p_gh, "n", 2, x_h[p], x_l[p], True, True).then_inc(s_gx, 1)
                after(pe, s_nh, n(1)); after(pe, s_nl, n(1))
                if more:
                    dist(q, 1)
                gate(p_r, "r", 1, n_h, n_l, False, False)
                if static(b, 0):
                    pe.wait_ge(s_mid, 1)
                    adjacency(2)
                if more:
                    after(pe, s_e[0], n(2))
                    dist(q, 2)
                gate(p_z, "z", 1, n_h, n_l, False, False)
                after(pe, s_tt, n(0)); gate(p_gi, "n", 1, n_h, n_l, True, False).then_inc(s_gn, 1)
                if more:
                    after(pe, s_e[1], n(2))
                    dist(q, 3)
                after(pe, s_ch, n(1)); after(pe, s_cl, n(1))
                gate(p_r, "r", 0, c_h, c_l, False, True).then_inc(s_gr, 1)
                gate(p_gi, "n", 0, c_h, c_l, False, True).then_inc(s_gi, 1)
                gate(p_z, "z", 0, c_h, c_l, False, True).then_inc(s_gz, 1)

            batches(pe, step)
            pe.wait_ge(s_cu, B); pe.wait_ge(s_mid, B); pe.wait_ge(s_nl, B)
            pe.wait_ge(s_agT, 2)
            g_pe.first_early(pe, mm, range(3))
            pe.wait_ge(s_tt, B)
            g_pe.second_early(pe, mm, range(1))
            pe.wait_ge(s_y2, B)
            transposes(1, 0)
            g_pe.first_early(pe, mm, range(3, NG))
            g_pe.second_early(pe, mm, range(1, NG))
            pe.wait_ge(s_sT, NG)
            for i in EARLY:
                g_pe.back(pe, mm, i)
            g_pe.aggregate2(pe, mm, 0)
            pe.wait_ge(s_grow, B)
            g_pe.aggregate(pe, mm, 2)
            g_pe.aggregate2(pe, mm, 1)
            pe.wait_ge(s_yn, B)
            g_pe.first_late(pe, mm)
            g_pe.scatter(pe, mm, 0)
            g_pe.scatter(pe, mm, 1)
            g_pe.second_late(pe, mm)
            g_pe.residual(pe, mm, 2)
            g_pe.aggregate2(pe, mm, 2)
            g_pe.scatter(pe, mm, 2)

        @block.scalar
        def _(act):
            A = nc.scalar.activation

            def rows_parts(p, n, k):
                after(act, s_rows, n(k + 1)); after(act, s_val, n(k))
                A(ab, bank(1 - p, S_ROWS)[64:128, :], ACT.Copy)
                A(u, bank(1 - p, S_ROWS)[0:64, :], ACT.Identity, bias=brow[:, 0:1]).then_inc(s_u0, 1)

            def rows_factor(n, k):
                after(act, s_u, n(k + 1))
                A(ab, u, ACT.Identity, bias=cst[0:64, C_ROW + 1:C_ROW + 2], scale=cst[0:64, C_ROW:C_ROW + 1]).then_inc(s_ab, 1)

            def first_conv(p, n, k):
                after(act, s_c1, n(k + 1)); after(act, s_dd, n(k)); after(act, s_sd, n(k))
                A(h1[:, PAD:PAD + N], bank(1 - p, S_C1)[:], ACT.Relu, bias=prm[:, P_A1:P_A1 + 1],
                  scale=prm[:, P_S1:P_S1 + 1]).then_inc(s_h1, 1)

            def sums_high(n, k):
                after(act, s_sd, n(k + 1)); after(act, s_middle, n(k)); after(act, s_sdl, n(k))
                A(sd_h[:], sd[:], ACT.Copy).then_inc(s_sdh, 1)

            def keep_x(p, n, k):
                after(act, s_ya, n(k - 1)); after(act, s_cu, n(k - 1))
                A(xkeep[p][:], xin[p][:], ACT.Copy).then_inc(s_xk, 1)

            def msg_high(p, n, k):
                after(act, s_mt, n(k + 1)); after(act, s_nmp, n(k - 1))
                A(m_h[p][:], mt[:], ACT.Relu).then_inc(s_mh, 1)

            def exps(p, n, k, c):
                after(act, s_d[c], n(k + 1)); after(act, s_amh, n(k)); after(act, s_aml, n(k))
                A(am[:, c, :], bank(1 - p, S_D0 + c)[:], ACT.Exp).then_inc(s_e[c], 1)

            act.wait_ge(s_w2d[0], 16)
            A(w1_h[:], wc2[:, 0::3, :], ACT.Copy).then_inc(s_whi, 1)
            z = lambda k: k
            act.wait_ge(s_zero, 4); act.wait_ge(s_prm, 7)
            first_conv(0, z, 0)
            act.wait_ge(s_w2d[2], 16)
            A(w4_h[:], wc2[:, 2::3, :], ACT.Copy).then_inc(s_whi, 1)
            act.wait_ge(s_brow, 16); act.wait_ge(s_cst, 16)
            act.wait_ge(s_rows, 1)
            A(u, bank(1, S_ROWS)[0:64, :], ACT.Identity, bias=brow[:, 0:1]).then_inc(s_u, 1)
            rows_factor(z, 0)
            sums_high(z, 0)
            msg_high(0, z, 0)
            act.wait_ge(s_wsum, 2)
            A(w3_h[:], wsum[:, 1], ACT.Copy).then_inc(s_whi, 1)
            exps(0, z, 0, 0)
            exps(0, z, 0, 1)
            act.wait_ge(s_wsum, 3)
            A(w2_h[:], wsum[:, 0], ACT.Copy).then_inc(s_whi, 1)
            exps(0, z, 0, 2)
            exps(0, z, 0, 3)
            act.wait_ge(s_prm, 9)
            act.wait_ge(s_x[0], 16)
            keep_x(0, z, 0)

            def node_rows(p, n, k):
                after(act, s_t, n(k + 1)); after(act, s_yo, n(k))
                A(yn[:].rearrange("p c d -> p (c d)"), bank(p, S_T)[:], ACT.Copy).then_inc(s_yn, 1)

            def candidate(n, k):
                after(act, s_tt, n(k + 1)); after(act, s_yb, n(k))
                A(nn[:], tt[:], ACT.Tanh, bias=vec[:, V_IN:V_IN + 1]).then_inc(s_nn, 1)

            def step(b, p, n):
                q = 1 - p
                more = not static(b, B - 1)
                if not static(b, 0):
                    candidate(n, -1)
                if more and not static(b, 0):
                    rows_parts(q, n, 1)
                for c in range(CH):
                    after(act, s_am[c], n(1))
                after(act, s_nmp, n(0))
                A(am_h[:], am[:], ACT.Copy).then_inc(s_amh, 1)
                if static(b, 0):
                    rows_parts(q, n, 1)
                    act.wait_ge(s_wgd, 32)
                    A(wg_h[:], wg[:], ACT.Copy).then_inc(s_wgs, 1)
                    act.wait_ge(s_wlo, 3); act.wait_ge(s_w4l, 1)
                    for h in range(2):
                        act.wait_ge(s_sel1m, h + 1)
                        A(sel1[:, pairs(h), :], banked((p_r, p_z)[h], 64, CC), ACT.Copy).then_inc(s_sel1, 1)
                if more:
                    rows_factor(n, 1)
                    first_conv(q, n, 1)
                    after(act, s_x[q], dma_count(n, q, 1))
                    keep_x(q, n, 1)
                if static(b, B - 1):
                    g_act.combined(act)
                if not static(b, 0):
                    node_rows(p, n, -1)
                if more:
                    msg_high(q, n, 1)
                after(act, s_middle, n(1)); after(act, s_mids, n(0))
                A(mid[:, 0, :], p_middle[:, 0:HALF], ACT.Identity, bias=prm[:, P_A2:P_A2 + 1], scale=prm[:, P_H2:P_H2 + 1])
                A(mid[:, 1, :], p_middle[:, HALF:N], ACT.Identity, scale=prm[:, P_H2:P_H2 + 1]).then_inc(s_mid, 1)
                if more and not static(b, 0):
                    sums_high(n, 1)
                if static(b, B - 1):
                    for i in EARLY:
                        g_act.channels(act, i)
                after(act, s_nmp, n(1)); after(act, s_gn, n(0))
                A(n_h[:], bank(p, S_NMP)[:], ACT.Copy).then_inc(s_nh, 1)
                if static(b, 0):
                    sums_high(n, 1)
                if more:
                    exps(q, n, 1, 0)
                after(act, s_cv, n(1)); after(act, s_gz, n(0))
                A(c_h[:], cv[:], ACT.Relu).then_inc(s_ch, 1)
                if more:
                    for c in range(1, CH):
                        exps(q, n, 1, c)
                if static(b, 0):
                    act.wait_ge(s_fw, 2)
                    A(fe[:], fw[:], ACT.Exp, bias=fs[:, 1:2], accum_out=fs[:, 2:3]).then_inc(s_fe, 1)
                after(act, s_gr, n(1)); after(act, s_gg, n(0))
                A(rt[:], p_r[:], ACT.Tanh, bias=prm[:, P_RH:P_RH + 1], scale=0.5).then_inc(s_rt, 1)
                after(act, s_gz, n(1)); after(act, s_yb, n(0)); after(act, s_ya, n(0))
                A(zt[:], p_z[:], ACT.Tanh, bias=prm[:, P_ZH:P_ZH + 1], scale=0.5).then_inc(s_zt, 1)

            batches(act, step)
            g_act.hidden(act, 0)
            candidate(lambda k: B + k, -1)
            g_act.hidden(act, 1)
            g_act.hidden(act, 2)
            node_rows(1, lambda k: B + k, -1)
            g_act.hidden(act, 3)
            g_act.hidden(act, 4)
            for g in range(NG):
                g_act.support(act, g)
            for i in EARLY:
                g_act.rows_early(act, i)
            g_act.channels(act, 2)
            g_act.weigh(act, 0)
            g_act.weigh(act, 1)
            g_act.hidden_late(act)
            g_act.rows_late(act)
            g_act.weigh(act, 2)
            store_groups(act, 2, 1)

        @block.gpsimd
        def _(pool):
            TT, TS = nc.gpsimd.tensor_tensor, nc.gpsimd.tensor_scalar
            for q in range(2):
                nc.gpsimd.memset(yo[q][:, 0, 0:1], 0.0).then_inc(s_out[q], 16)
            nc.gpsimd.memset(bd[:], 0.0).then_inc(s_zero, 1)
            nc.gpsimd.memset(x1[:], 0.0).then_inc(s_zero, 1)
            nc.gpsimd.memset(h1[:, 0:PAD], 0.0).then_inc(s_zero, 1)
            nc.gpsimd.memset(h1[:, PAD + N:], 0.0).then_inc(s_zero, 1)
            pool.wait_ge(s_prm, 2)
            pool.wait_ge(s_cst, 16)
            TT(prm[:, P_RS:P_RS + 2], prm[:, P_VE:P_VE + 2], cst[:, C_MH:C_MH + 2], ALU.pow).then_inc(s_pow, 1)

            def rows_sum(n, k):
                after(pool, s_u0, n(k))
                TT(u, u, ab, ALU.add).then_inc(s_u, 1)

            def rows_val(n, k):
                after(pool, s_u, n(k + 1)); after(pool, s_ab, n(k + 1)); after(pool, s_valh, n(k))
                after(pool, s_left, n(k)); after(pool, s_right, n(k))
                TT(val[:], u, ab, ALU.mult).then_inc(s_val, 1)

            def sums_low(n, k):
                after(pool, s_sd, n(k + 1)); after(pool, s_sdh, n(k + 1)); after(pool, s_middle, n(k))
                TT(sd_l[:], sd[:], full(sd_h[:]), ALU.subtract).then_inc(s_sdl, 1)

            def mask(p, n, k, c):
                if c == 0:
                    after(pool, s_adj[p], dma_count(n, p, k))
                after(pool, s_e[c], n(k + 1))
                TT(am[:, c, :], am[:, c, :], adj[p][:, c, :], ALU.mult).then_inc(s_am[c], 1)

            def powers(n, k):
                after(pool, s_base, n(k + 1))
                after(pool, s_yo, n(k))
                TT(rs[:], base[:], cst[:, C_MH:C_MH + CH + 1], ALU.pow).then_inc(s_rs, 1)

            pool.wait_ge(s_w2d[0], 16)
            nc.gpsimd.tensor_copy(wsum[:, 0, G3 - 1:G3, :], wc2[:, TAPS - 2:TAPS - 1, :])
            pool.wait_ge(s_w2d[2], 16)
            TT(wsum[:, 0, 0:G3 - 1, :], wc2[:, 0:TAPS - 2:3, :], wc2[:, 2::3, :], ALU.add).then_inc(s_wsum, 1)
            pool.wait_ge(s_whi, 2)
            TT(w4_l[:], wc2[:, 2::3, :], full(w4_h[:]), ALU.subtract).then_inc(s_w4l, 1)
            rows_val(lambda k: k, 0)
            pool.wait_ge(s_w2d[1], 16); pool.wait_ge(s_wsum, 1)
            TT(wsum[:, 1], wsum[:, 0], wc2[:, 1::3, :], ALU.subtract).then_inc(s_wsum, 1)
            sums_low(lambda k: k, 0)
            pool.wait_ge(s_adj[0], 16)
            for c in range(CH // 2, CH):
                mask(0, lambda k: k, 0, c)

            def step(b, p, n):
                q = 1 - p
                more = not static(b, B - 1)
                if more:
                    rows_sum(n, 1)
                    rows_val(n, 1)
                if more:
                    sums_differences(TT, pool, n, 1)
                after(pool, s_mid, n(1)); after(pool, s_ch, n(0)); after(pool, s_cl, n(0))
                TT(cv[:, 0::2], mid[:, 0, :], mid[:, 1, :], ALU.add)
                TT(cv[:, 1::2], mid[:, 0, :], mid[:, 1, :], ALU.subtract).then_inc(s_mids, 1)
                if more:
                    sums_low(n, 1)
                if static(b, B - 2):
                    TS(dg[:, 0, :], dg[:, 1, :], -1.0, 1.0, ALU.mult, ALU.add).then_inc(s_dinv, 1)
                    pool.wait_ge(s_dinv, 1); pool.wait_ge(s_dpow, 1)
                    TT(dinv[:], dg[:, 3, :], dg[:, 0, :], ALU.mult).then_inc(s_dinv, 1)
                    pool.wait_ge(s_dinv, 2)
                    TT(diag[:], cst[0:CC, C_ID:C_ID + CC].unsqueeze(1).broadcast_to([CC, PAIRS, CC]),
                       dinv[:].unsqueeze(2).broadcast_to([CC, PAIRS, CC]), ALU.mult).then_inc(s_diag, 1)
                    TT(ac[0:CC, :, :], ac[0:CC, :, :], dinv[:].unsqueeze(2).broadcast_to([CC, PAIRS, CC]), ALU.mult).then_inc(s_diag, 1)
                if static(b, B - 1):
                    nc.gpsimd.memset(hz[:], 0.0).then_inc(s_hz, 1)
                if not static(b, 0):
                    powers(n, -1)
                if static(b, 1):
                    pool.wait_ge(s_dg, 3)
                    TT(dg[:, 3, :], dg[:, 2, :], cst[0:CC, C_MH:C_MH + PAIRS], ALU.pow).then_inc(s_dpow, 1)
                if more:
                    for c in range(CH):
                        mask(q, n, 1, c)

            batches(pool, step)
            powers(lambda k: B + k, -1)
            for i in range(3):
                groups_power(pool, i)

        @block.vector
        def _(dve):
            TT, TS, STT, CP = nc.vector.tensor_tensor, nc.vector.tensor_scalar, nc.vector.scalar_tensor_tensor, nc.vector.tensor_copy

            dve.wait_ge(s_vec, 16)
            TS(prm[:, P_VE:P_VE + 1], vec[:, V_V1:V_V1 + 1], EPS, None, ALU.add).then_inc(s_prm, 1)
            TS(prm[:, P_VE + 1:P_VE + 2], vec[:, V_V2:V_V2 + 1], EPS, None, ALU.add).then_inc(s_prm, 1)

            def split_x(p, n, k):
                after(dve, s_x[p], dma_count(n, p, k)); after(dve, s_gx, n(k - 1))
                CP(x_h[p][:], xin[p][:]).then_inc(s_xh, 1)
                after(dve, s_xh, n(k + 1))
                TT(x_l[p][:], xin[p][:], full(x_h[p][:]), ALU.subtract).then_inc(s_xl, 1)

            split_x(0, lambda k: k, 0)
            dve.wait_ge(s_wc1d, 16)
            CP(wc1_h[:], wc1[:]).then_inc(s_w1s, 1)
            dve.wait_ge(s_w1s, 1)
            TT(wc1_l[:], wc1[:], full(wc1_h[:]), ALU.subtract).then_inc(s_w1s, 1)
            dve.wait_ge(s_wrowd, 16)
            CP(wrow_hl[:, 0:64], wrow[:]).then_inc(s_w1s, 1)
            dve.wait_ge(s_w1s, 3)
            TT(wrow_hl[:, 64:128], wrow[:], full(wrow_hl[:, 0:64]), ALU.subtract).then_inc(s_w1s, 1)
            dve.wait_ge(s_pow, 1)
            TT(prm[:, P_S1:P_S1 + 1], vec[:, V_G1:V_G1 + 1], prm[:, P_RS:P_RS + 1], ALU.mult).then_inc(s_prm, 1)
            TT(prm[:, P_S2:P_S2 + 1], vec[:, V_G2:V_G2 + 1], prm[:, P_RS + 1:P_RS + 2], ALU.mult).then_inc(s_prm, 1)
            dve.wait_ge(s_prm, 3)
            TT(prm[:, P_T1:P_T1 + 1], vec[:, V_M1:V_M1 + 1], prm[:, P_S1:P_S1 + 1], ALU.mult).then_inc(s_prm, 1)
            dve.wait_ge(s_prm, 4)
            TT(prm[:, P_T2:P_T2 + 1], vec[:, V_M2:V_M2 + 1], prm[:, P_S2:P_S2 + 1], ALU.mult).then_inc(s_prm, 1)
            dve.wait_ge(s_prm, 5)
            TT(prm[:, P_A1:P_A1 + 1], vec[:, V_B1:V_B1 + 1], prm[:, P_T1:P_T1 + 1], ALU.subtract).then_inc(s_prm, 1)
            dve.wait_ge(s_prm, 6)
            TT(prm[:, P_A2:P_A2 + 1], vec[:, V_B2:V_B2 + 1], prm[:, P_T2:P_T2 + 1], ALU.subtract)
            TS(prm[:, P_H2:P_H2 + 1], prm[:, P_S2:P_S2 + 1], 0.5, None, ALU.mult)
            TS(prm[:, P_N2:P_N2 + 1], prm[:, P_S2:P_S2 + 1], -1.0, None, ALU.mult)
            TT(prm[:, P_R:P_R + 2], vec[:, V_IR:V_IR + 2], vec[:, V_HR:V_HR + 2], ALU.add).then_inc(s_prm, 1)
            dve.wait_ge(s_prm, 8)
            TS(prm[:, P_RH:P_RH + 2], prm[:, P_R:P_R + 2], 0.5, None, ALU.mult).then_inc(s_prm, 1)

            def left_right(n, k):
                after(dve, s_val, n(k + 1))
                CP(val_h[:], val[:]).then_inc(s_valh, 1)
                after(dve, s_valh, n(k + 1)); after(dve, s_d[CH - 1], n(k))
                STT(left[:], full(val_h[0:KD, :]), cst[0:KD, C_ROW + 2:C_ROW + 3], val[0:KD, :], ALU.mult, ALU.add).then_inc(s_left, 1)
                STT(right[:], full(val_h[32:32 + KD, :]), cst[32:32 + KD, C_ROW + 2:C_ROW + 3], val[32:32 + KD, :],
                    ALU.mult, ALU.add).then_inc(s_right, 1)

            def differences(n, k):
                after(dve, s_h1, n(k + 1)); after(dve, s_ddl, n(k)); after(dve, s_ddh, n(k))
                TT(dd[:], halves(h1, 0), halves(h1, 2), ALU.subtract).then_inc(s_dd, 1)
                after(dve, s_dd, n(k + 1)); after(dve, s_outer, n(k))
                CP(dd_h[:], dd[:]).then_inc(s_ddh, 1)
                after(dve, s_ddh, n(k + 1))
                TT(dd_l[:], dd[:], full(dd_h[:]), ALU.subtract).then_inc(s_ddl, 1)

            def msg_sum(n, k, source):
                after(dve, s_msg, n(k + 1)); after(dve, s_mh, n(k)); after(dve, s_ml, n(k))
                TT(mt[:].rearrange("p (c d) -> p c d", c=CH), source[:].rearrange("p (c d) -> p c d", c=CH),
                   bmsg[:].unsqueeze(1).broadcast_to([128, CH, D]), ALU.add).then_inc(s_mt, 1)

            def msg_low(p, n, k):
                after(dve, s_mh, n(k + 1)); after(dve, s_mt, n(k + 1))
                STT(m_l[p][:], mt[:], 0.0, full(m_h[p][:]), ALU.max, ALU.subtract).then_inc(s_ml, 1)

            zero = lambda k: k
            dve.wait_ge(s_whi, 1)
            TT(w1_l[:], wc2[:, 0::3, :], full(w1_h[:]), ALU.subtract).then_inc(s_wlo, 1)
            dve.wait_ge(s_zero, 4)
            differences(zero, 0)
            sums_differences(TT, dve, zero, 0)
            dve.wait_ge(s_bmsg, 16)
            msg_sum(zero, 0, FIRST_MSG)
            left_right(zero, 0)
            dve.wait_ge(s_w2d[1], 16); dve.wait_ge(s_wsum, 2)
            TT(wsum[:, 0], wsum[:, 0], wc2[:, 1::3, :], ALU.add).then_inc(s_wsum, 1)
            dve.wait_ge(s_whi, 3)
            TT(w3_l[:], wsum[:, 1], full(w3_h[:]), ALU.subtract).then_inc(s_wlo, 1)
            dve.wait_ge(s_whi, 4)
            TT(w2_l[:], wsum[:, 0], full(w2_h[:]), ALU.subtract).then_inc(s_wlo, 1)
            dve.wait_ge(s_adj[0], 16)
            for c in range(CH // 2):
                dve.wait_ge(s_e[c], 1)
                TT(am[:, c, :], am[:, c, :], adj[0][:, c, :], ALU.mult).then_inc(s_am[c], 1)

            def adjacency(stage):
                if stage == 0:
                    for h in range(2):
                        dve.wait_ge(s_acm, h + 1)
                        TT(ac[0:CC, pairs(h), :], banked((p_gi, p_gh)[h], CC, CC),
                           cst[0:CC, C_SAME:C_SAME + CC].unsqueeze(1).broadcast_to([CC, HP, CC]), ALU.mult).then_inc(s_ac, 1)
                else:
                    dve.wait_ge(s_deg, 1)
                    CP(dg[:, 0, :], p_middle[0:CC, 0:PAIRS]).then_inc(s_dg, 1)
                    dve.wait_ge(s_dg, 1)
                    TS(dg[:, 1, :], dg[:, 0, :], 0.0, None, ALU.is_equal).then_inc(s_dg, 1)
                    dve.wait_ge(s_dg, 2)
                    TT(dg[:, 2, :], dg[:, 0, :], dg[:, 1, :], ALU.add).then_inc(s_dg, 1)

            def gate_mid(n, k):
                after(dve, s_rt, n(k + 1)); after(dve, s_gg, n(k))
                TS(r1[:], rt[:], 0.5, 0.5, ALU.mult, ALU.add).then_inc(s_r1, 1)
                after(dve, s_r1, n(k + 1)); after(dve, s_gx, n(k + 1)); after(dve, s_tt, n(k))
                STT(gg[:], p_gh[:], vec[:, V_HN:V_HN + 1], r1[:], ALU.add, ALU.mult).then_inc(s_gg, 1)
                after(dve, s_gg, n(k + 1)); after(dve, s_gi, n(k + 1)); after(dve, s_nn, n(k))
                TT(tt[:], p_gi[:], gg[:], ALU.add).then_inc(s_tt, 1)

            def result(p, n, k, between=lambda: None):
                after(dve, s_zt, n(k + 1)); after(dve, s_xk, n(k + 1)); after(dve, s_y2, n(k))
                STT(ya, zt[:], 3.0, xkeep[p][:], ALU.add, ALU.mult).then_inc(s_ya, 1)
                between()
                after(dve, s_nn, n(k + 1))
                STT(yb, zt[:], -1.0, nn[:], ALU.add, ALU.mult).then_inc(s_yb, 1)
                after(dve, s_ya, n(k + 1)); after(dve, s_yb, n(k + 1)); after(dve, s_t, n(k))
                TT(y2, ya, yb, ALU.subtract).then_inc(s_y2, 1)

            def stats(n, k):
                after(dve, s_yn, n(k + 1)); after(dve, s_mv, n(k))
                for c in range(CH):
                    last = nc.vector.bn_stats(st[:, c, :], yn[:, c, :])
                last.then_inc(s_st, 1)
                after(dve, s_st, n(k + 1)); after(dve, s_base, n(k)); after(dve, s_yo, n(k))

            def moments(n, k):
                for c in range(CH):
                    last = nc.vector.bn_aggr(mv[:, c, :], st[:, c, :])
                last.then_inc(s_mv, 1)
                after(dve, s_mv, n(k + 1)); after(dve, s_rs, n(k))
                TS(base[:, 0:CH], mv[:, :, 1], 1.0 + EPS, 4 * EPS * EPS, ALU.mult, ALU.add)
                TS(base[:, CH:CH + 1], mv[:, 0, 1:2], 1.0, 4 * EPS, ALU.mult, ALU.add).then_inc(s_base, 1)

            def normalise(q, n, k, pair):
                after(dve, s_mv, n(k + 1)); after(dve, s_rs, n(k + 1))
                TS(x1[SLOT * q:SLOT * q + GN, pair, :], yn[0:GN, 0, :], mv[0:GN, 0, 0:1], rs[0:GN, CH:CH + 1],
                   ALU.subtract, ALU.mult).then_inc(s_grow, 1)
                dve.wait_ge(s_out[q], dma_count(n, q, k))
                for c in range(CH):
                    last = TS(yo[q][:, c, :], yn[:, c, :], mv[:, c, 0:1], rs[:, c:c + 1], ALU.subtract, ALU.mult)
                last.then_inc(s_yo, 1)
            def conv_sum(n):
                after(dve, s_mids, n(1)); after(dve, s_cu, n(1))
                TT(cv[:], cu[:], cv[:], ALU.add).then_inc(s_cv, 1)

            def step(b, p, n):
                q = 1 - p
                more = not static(b, B - 1)
                if more:
                    split_x(q, n, 1)
                if not static(b, 0):
                    gate_mid(n, -1)
                    result(q, n, -1)
                if static(b, B - 1):
                    g_dve.columns(dve)
                if static(b, 0):
                    msg_low(0, n, 0)
                    dve.wait_ge(s_bdd, 32); dve.wait_ge(s_cst, 16)
                    TT(bd[:], bd[:], cst[0:64, C_ID:C_ID + 64].unsqueeze(1).broadcast_to([64, PAIRS, 64]), ALU.add).then_inc(s_bdi, 1)
                after(dve, s_outer, n(1)); after(dve, s_cv, n(0)); after(dve, s_xk, n(1))
                STT(cu[:, 0::2], p_outer[:, 0:HALF], prm[:, P_S2:P_S2 + 1], xkeep[p][:, 0::2], ALU.mult, ALU.add)
                STT(cu[:, 1::2], p_outer[:, HALF:N], prm[:, P_N2:P_N2 + 1], xkeep[p][:, 1::2], ALU.mult, ALU.add).then_inc(s_cu, 1)
                after(dve, s_amh, n(1)); after(dve, s_nmp, n(0))
                TT(am_l[:], am[:], full(am_h[:]), ALU.subtract).then_inc(s_aml, 1)
                if static(b, B - 1):
                    g_dve.prepare(dve)
                if more:
                    msg_sum(n, 1, bank(p, S_MSG))
                if static(b, 0):
                    dve.wait_ge(s_wgs, 1)
                    TT(wg_l[:], wg[:], full(wg_h[:]), ALU.subtract).then_inc(s_wgs, 1)
                    adjacency(0)
                if more:
                    left_right(n, 1)
                if not static(b, 0):
                    stats(n, -1)
                if more:
                    differences(n, 1)
                if static(b, B - 1):
                    conv_sum(n)
                after(dve, s_nh, n(1)); after(dve, s_gn, n(0))
                TT(n_l[:], bank(p, S_NMP)[:], full(n_h[:]), ALU.subtract).then_inc(s_nl, 1)
                if not static(b, 0) and not static(b, B - 1):
                    moments(n, -1)
                if not static(b, B - 1):
                    conv_sum(n)
                after(dve, s_ch, n(1)); after(dve, s_cv, n(1)); after(dve, s_gz, n(0))
                STT(c_l[:], cv[:], 0.0, full(c_h[:]), ALU.max, ALU.subtract).then_inc(s_cl, 1)
                if static(b, B - 1):
                    moments(n, -1)
                if static(b, 0):
                    adjacency(1)
                    dve.wait_ge(s_gd, 64)
                    nc.vector.reduce_max(fs[:, 0:1], fw[:], AX.X).then_inc(s_fw, 1)
                    dve.wait_ge(s_fw, 1)
                    TS(fs[:, 1:2], fs[:, 0:1], -1.0, None, ALU.mult).then_inc(s_fw, 1)
                if more:
                    msg_low(q, n, 1)
                if not static(b, 0):
                    normalise(q, n, -1, pair_of(b, p, n))

            def pair_of(b, p, n):
                if isinstance(b, int):
                    return (b - 1) // 2
                return loop_pair[0] - (1 - p)

            loop_pair = [None]
            step(0, 0, lambda k: k)
            step(1, 1, lambda k: 1 + k)
            with dve.Fori(1, PAIRS - 1) as i:
                loop_pair[0] = i
                for p in range(2):
                    known = {}

                    def count(k, p=p, known=known):
                        if k not in known:
                            known[k] = dve.snap(i * 2 + (p + k))
                        return known[k]
                    step(count(0), p, count)
            step(B - 2, 0, lambda k: B - 2 + k)
            step(B - 1, 1, lambda k: B - 1 + k)
            last = lambda k: B + k
            gate_mid(last, -1)
            result(1, last, -1, lambda: g_dve.hidden(dve, 0))
            for g in range(1, NG):
                g_dve.hidden(dve, g)
            stats(last, -1)
            moments(last, -1)
            normalise(1, last, -1, PAIRS - 1)
            g_dve.hidden_late(dve)
            g_dve.sums(dve, 0)
            g_dve.moments(dve, 0)
            g_dve.sums(dve, 1)
            g_dve.moments(dve, 1)
            g_dve.normalise(dve, 0)
            g_dve.sums(dve, 2)
            g_dve.moments(dve, 2)
            g_dve.normalise(dve, 1)
            g_dve.normalise(dve, 2)


def kernel(x, adj, L0_gnn_w_se, L0_gnn_b_se, L0_gnn_conv1_w, L0_gnn_bn1_g, L0_gnn_bn1_b, L0_gnn_bn1_m, L0_gnn_bn1_v,
           L0_gnn_conv2_w, L0_gnn_bn2_g, L0_gnn_bn2_b, L0_gnn_bn2_m, L0_gnn_bn2_v, L0_gnn_w_msg, L0_gnn_b_msg,
           L0_gnn_w_ih, L0_gnn_b_ih, L0_gnn_w_hh, L0_gnn_b_hh, L1_gnn_W1, L1_gnn_b1, L1_gnn_W2, L1_gnn_b2, L1_gnn_fusion_w):
    import concourse.bacc as bacc
    from concourse.bass_utils import run_bass_kernel_spmd

    a = lambda t: np.asarray(t)
    c = np.ascontiguousarray
    b_ih, b_hh = a(L0_gnn_b_ih).reshape(3, D), a(L0_gnn_b_hh).reshape(3, D)
    vecs = c(np.stack([a(L0_gnn_bn1_g), a(L0_gnn_bn1_b), a(L0_gnn_bn1_m), a(L0_gnn_bn1_v),
                       a(L0_gnn_bn2_g), a(L0_gnn_bn2_b), a(L0_gnn_bn2_m), a(L0_gnn_bn2_v),
                       b_ih[0], b_ih[1], b_ih[2], b_hh[0], b_hh[1], b_hh[2]], axis=1))
    w_se, b_se = a(L0_gnn_w_se), a(L0_gnn_b_se)
    w_rows, b_rows = np.zeros((D, 64), w_se.dtype), np.zeros((64, 1), b_se.dtype)
    for side, rows in enumerate(dist_rows()):
        for r, (k, _, _, _) in enumerate(rows):
            if k is None:
                b_rows[32 * side + r, 0] = 1
            else:
                w_rows[:, 32 * side + r] = w_se[k]
                b_rows[32 * side + r, 0] = b_se[k]
    arrays = {
        "xT": c(a(x).transpose(0, 2, 1)), "adjT": c(a(adj).transpose(0, 2, 1)), "consts": constants(),
        "vecs": vecs, "w_rows": w_rows, "b_rows": b_rows,
        "w_c1": c(a(L0_gnn_conv1_w)[:, :, 0].T), "w_c2": c(a(L0_gnn_conv2_w).transpose(1, 2, 0)),
        "w_ih": c(a(L0_gnn_w_ih).reshape(3 * D, 2, D).transpose(2, 1, 0)), "w_hh": c(a(L0_gnn_w_hh).T),
        "w_msg": c(a(L0_gnn_w_msg).T), "b_msg": a(L0_gnn_b_msg).reshape(1, D),
        "g_w1": a(L1_gnn_W1), "g_b1": c(a(L1_gnn_b1).reshape(NG, 2, D).transpose(2, 0, 1)),
        "g_w2": a(L1_gnn_W2), "g_b2": a(L1_gnn_b2), "g_fw": a(L1_gnn_fusion_w).reshape(1, NG),
    }
    nc = bacc.Bacc("TRN2", target_bir_lowering=False, num_devices=1)
    args = [nc.dram_tensor(name, v.shape, mybir.dt.from_np(v.dtype), kind="ExternalInput").ap() for name, v in arrays.items()]
    args.append(nc.dram_tensor("out", (B, N, D), mybir.dt.float32, kind="ExternalOutput").ap())
    gnn_kernel(nc, *args)
    result = run_bass_kernel_spmd(nc, [arrays], core_ids=[0])
    return result.results[0]["out"]
```
